# Optimizing a Trainium2 kernel written in Bass

```python
import numpy as np
import jax
import jax.numpy as jnp

def _softmax(x, axis=-1):
    return jax.nn.softmax(x, axis=axis)

def _gelu(x):
    return jax.nn.gelu(x, approximate=True)

def _silu(x):
    return jax.nn.silu(x)

def _sigmoid(x):
    return jax.nn.sigmoid(x)

def _layernorm(x, axis=-1, eps=1e-05):
    m = jnp.mean(x, axis=axis, keepdims=True)
    v = jnp.var(x, axis=axis, keepdims=True)
    return (x - m) / jnp.sqrt(v + eps)

def _scatter_add(tgt, idx, src, axis=0):
    return tgt.at[idx].add(src)

def _segment_sum(src, seg, n):
    return jax.ops.segment_sum(src, seg, n)
kernel_name = 'mk_perceiver_d2_seqx_r4_6875f8'

def setup_inputs(seed: int=0):
    np.random.seed(seed)
    _w = jnp.asarray

    def _rec_inputs():
        import jax
        import jax.numpy as jnp
        _rk = jax.random.key(seed)
        x = -0.0002928 + 1 * jax.random.normal(jax.random.fold_in(_rk, 1), (2, 256, 256), jnp.float32)
        _lenS = 256 - jax.random.randint(jax.random.fold_in(_rk, 7), (2,), 0, max(1, 256 // 4) + 1, jnp.int32)
        _lenS2 = 4096 - jax.random.randint(jax.random.fold_in(_rk, 8), (2,), 0, max(1, 4096 // 4) + 1, jnp.int32)
        _ctx_1024P = jax.random.normal(jax.random.fold_in(_rk, 11), (2, 16, 256), jnp.float32)
        _ctx_1024c = jax.random.dirichlet(jax.random.fold_in(_rk, 511), 0.3 * jnp.ones((16,), jnp.float32), (2, 4096))
        _ctx_1024t = jnp.einsum('bsk,bkd->bsd', _ctx_1024c, _ctx_1024P)
        _ctx_1024t = _ctx_1024t * jax.lax.rsqrt(jnp.mean(jnp.square(_ctx_1024t)) + 1e-12) * 0.953939
        ctx_1024 = -1.39393e-06 + 0.999914 * (_ctx_1024t + 0.3 * jax.random.normal(jax.random.fold_in(_rk, 611), (2, 4096, 256), jnp.float32))
        return (x, ctx_1024)
    x, ctx_1024 = _rec_inputs()

    def _L0_xattn_setup():
        import jax, jax.numpy as jnp
        import numpy as np
        HEADS = 8
        DIM_HEAD = 64
        DIM = 256
        CTX_DIM = 256
        HIDDEN = HEADS * DIM_HEAD
        key = jax.random.key(seed)
        ks = jax.random.split(key, 7)
        b, n, m = (2, 512, 512)
        x = jax.random.normal(ks[0], (b, n, DIM), dtype=jnp.float32)
        context = jax.random.normal(ks[1], (b, m, CTX_DIM), dtype=jnp.float32)
        Wq = jax.random.normal(ks[2], (DIM, HIDDEN), dtype=jnp.float32) * (1.0 / np.sqrt(DIM))
        Wk = jax.random.normal(ks[3], (CTX_DIM, HIDDEN), dtype=jnp.float32) * (1.0 / np.sqrt(CTX_DIM))
        Wv = jax.random.normal(ks[4], (CTX_DIM, HIDDEN), dtype=jnp.float32) * (1.0 / np.sqrt(CTX_DIM))
        Wo = jax.random.normal(ks[5], (HIDDEN, DIM), dtype=jnp.float32) * (1.0 / np.sqrt(HIDDEN))
        bo = jax.random.normal(ks[6], (DIM,), dtype=jnp.float32) * 0.01
        return {'x': x, 'context': context, 'Wq': Wq, 'Wk': Wk, 'Wv': Wv, 'Wo': Wo, 'bo': bo}
    _L0_xattn_all = _L0_xattn_setup()
    _L0_xattn_in = {k: v for k, v in _L0_xattn_all.items() if k in ('Wq', 'Wk', 'Wv', 'Wo', 'bo')}
    del _L0_xattn_all

    def _L0_attn_setup():
        import jax, jax.numpy as jnp
        import numpy as np
        D_MODEL = 256
        N_HEADS = 16
        LATENT_HEADS = 8
        LATENT_DIM = 128
        N_LATENTS = 64
        WINDOW = 64
        HEAD_DIM = D_MODEL // N_HEADS
        LAT_HD = LATENT_DIM // LATENT_HEADS
        B, S = (2, 1024)

        def _pool_to_latents(x):
            Bx, Sx, C = x.shape
            chunk = max(1, Sx // N_LATENTS)
            return x.reshape(Bx, N_LATENTS, chunk, C).mean(axis=2)

        def _local_window_attn(Q, K, V):
            Bx, H, Sx, D = Q.shape
            W = WINDOW
            nb = Sx // W
            Qb = Q.reshape(Bx, H, nb, W, D)
            Kp = jnp.pad(K, ((0, 0), (0, 0), (W, 0), (0, 0))).reshape(Bx, H, nb + 1, W, D)
            Vp = jnp.pad(V, ((0, 0), (0, 0), (W, 0), (0, 0))).reshape(Bx, H, nb + 1, W, D)
            Kw = jnp.concatenate([Kp[:, :, :-1], Kp[:, :, 1:]], axis=3)
            Vw = jnp.concatenate([Vp[:, :, :-1], Vp[:, :, 1:]], axis=3)
            i = jnp.arange(W)[:, None]
            j = jnp.arange(2 * W)[None, :]
            base = (j > i) & (j <= i + W)
            blk0 = (jnp.arange(nb) > 0)[:, None, None] | (j >= W)[None, :, :]
            mask = base[None, :, :] & blk0
            sc = jnp.einsum('bhnid,bhnjd->bhnij', Qb, Kw) / np.sqrt(D).astype(np.float32)
            sc = jnp.where(mask[None, None], sc, -jnp.inf)
            p = jax.nn.softmax(sc, axis=-1)
            out = jnp.einsum('bhnij,bhnjd->bhnid', p, Vw)
            return out.reshape(Bx, H, Sx, D)
        key = jax.random.key(seed)
        ks = jax.random.split(key, 11)
        std = 0.02
        w = lambda k, shp: jax.random.normal(k, shp, jnp.float32) * std
        return {'x': jax.random.normal(ks[0], (B, S, D_MODEL), jnp.float32), 'wq': w(ks[1], (D_MODEL, D_MODEL)), 'wk': w(ks[2], (D_MODEL, D_MODEL)), 'wv': w(ks[3], (D_MODEL, D_MODEL)), 'wgq': w(ks[4], (D_MODEL, LATENT_DIM)), 'wgk': w(ks[5], (D_MODEL, LATENT_DIM)), 'wgv': w(ks[6], (D_MODEL, LATENT_DIM)), 'r_out_w': w(ks[7], (LATENT_DIM, D_MODEL)), 'gate_local_w': w(ks[8], (N_HEADS, HEAD_DIM)), 'gate_remote_w': w(ks[9], (N_HEADS, HEAD_DIM)), 'w_out': w(ks[10], (D_MODEL, D_MODEL))}
    _L0_attn_all = _L0_attn_setup()
    _L0_attn_in = {k: v for k, v in _L0_attn_all.items() if k in ('wq', 'wk', 'wv', 'wgq', 'wgk', 'wgv', 'r_out_w', 'gate_local_w', 'gate_remote_w', 'w_out')}
    del _L0_attn_all

    def _L0_ffn_setup():
        import jax, jax.numpy as jnp
        import numpy as np
        B, S, D, E, F, TOP_K = (4, 512, 256, 8, 1024, 2)
        key = jax.random.key(seed)
        k0, k1, k2, k3 = jax.random.split(key, 4)
        init = lambda k, shape, fan: (jax.random.normal(k, shape, jnp.float32) / np.sqrt(fan)).astype(jnp.float32)
        return {'x': jax.random.normal(k0, (B, S, D), jnp.float32), 'gate_w': init(k1, (D, E), D), 'w1': init(k2, (E, D, F), D), 'b1': jnp.zeros((E, F), jnp.float32), 'w2': init(k3, (E, F, D), F), 'b2': jnp.zeros((E, D), jnp.float32)}
    _L0_ffn_all = _L0_ffn_setup()
    _L0_ffn_in = {k: v for k, v in _L0_ffn_all.items() if k in ('gate_w', 'w1', 'b1', 'w2', 'b2')}
    del _L0_ffn_all

    def _L1_xattn_setup():
        import jax, jax.numpy as jnp
        import numpy as np
        DIM = 256
        NUM_HEAD = 16
        DIM_HEAD = DIM // NUM_HEAD
        key = jax.random.key(seed)
        ks = jax.random.split(key, 11)
        B, S = (2, 512)
        s = 1.0 / np.sqrt(DIM)
        return {'query': jax.random.normal(ks[0], (B, S, DIM), jnp.float32), 'key': jax.random.normal(ks[1], (B, S, DIM), jnp.float32), 'value': jax.random.normal(ks[2], (B, S, DIM), jnp.float32), 'wq': jax.random.normal(ks[3], (DIM, DIM), jnp.float32) * s, 'bq': jax.random.normal(ks[4], (DIM,), jnp.float32) * s, 'wk': jax.random.normal(ks[5], (DIM, DIM), jnp.float32) * s, 'bk': jax.random.normal(ks[6], (DIM,), jnp.float32) * s, 'wv': jax.random.normal(ks[7], (DIM, DIM), jnp.float32) * s, 'bv': jax.random.normal(ks[8], (DIM,), jnp.float32) * s, 'wo': jax.random.normal(ks[9], (DIM, DIM), jnp.float32) * s, 'bo': jax.random.normal(ks[10], (DIM,), jnp.float32) * s}
    _L1_xattn_all = _L1_xattn_setup()
    _L1_xattn_in = {k: v for k, v in _L1_xattn_all.items() if k in ('wq', 'bq', 'wk', 'bk', 'wv', 'bv', 'wo', 'bo')}
    del _L1_xattn_all

    def _L1_attn_setup():
        import jax, jax.numpy as jnp
        import numpy as np
        B, T, C = (8, 512, 256)
        NEG = -1e+30

        def wkv(w, u, k, v):
            w_exp = -jnp.exp(w)
            p0 = jnp.zeros(k.shape[::2], k.dtype)
            q0 = jnp.zeros(k.shape[::2], k.dtype)
            o0 = jnp.full(k.shape[::2], NEG, k.dtype)

            def step(carry, kv_t):
                p, q, o = carry
                k_t, v_t = kv_t
                uk = u + k_t
                no = jnp.maximum(o, uk)
                A = jnp.exp(o - no)
                Bc = jnp.exp(uk - no)
                out = (A * p + Bc * v_t) / (A * q + Bc)
                wo = w_exp + o
                no2 = jnp.maximum(wo, k_t)
                A2 = jnp.exp(wo - no2)
                B2 = jnp.exp(k_t - no2)
                return ((A2 * p + B2 * v_t, A2 * q + B2, no2), out)
            kT = jnp.swapaxes(k, 0, 1)
            vT = jnp.swapaxes(v, 0, 1)
            _, outs = jax.lax.scan(step, (p0, q0, o0), (kT, vT))
            return jnp.swapaxes(outs, 0, 1)
        key = jax.random.key(seed)
        ks = jax.random.split(key, 5)
        x = jax.random.normal(ks[0], (B, T, C), dtype=jnp.float32)
        scales = jnp.arange(C, dtype=jnp.float32) / C
        Wk = jax.random.normal(ks[1], (C, C), dtype=jnp.float32) * 0.02
        Wv = jax.random.normal(ks[2], (C, C), dtype=jnp.float32) * 0.02
        Wr = jax.random.normal(ks[3], (C, C), dtype=jnp.float32) * 0.02
        Wo = jax.random.normal(ks[4], (C, C), dtype=jnp.float32) * 0.02
        return {'x': x, 'w': scales, 'u': scales, 'mix_k': scales, 'mix_v': scales, 'mix_r': scales, 'Wk': Wk, 'Wv': Wv, 'Wr': Wr, 'Wo': Wo}
    _L1_attn_all = _L1_attn_setup()
    _L1_attn_in = {k: v for k, v in _L1_attn_all.items() if k in ('w', 'u', 'mix_k', 'mix_v', 'mix_r', 'Wk', 'Wv', 'Wr', 'Wo')}
    del _L1_attn_all

    def _L1_ffn_setup():
        import jax, jax.numpy as jnp
        import numpy as np
        B, T, D, FF, E, TOP_K = (8, 512, 256, 1024, 8, 2)
        key = jax.random.key(seed)
        kx, kr, k1, k2 = jax.random.split(key, 4)
        x = jax.random.normal(kx, (B, T, D), dtype=jnp.float32)
        Wr = jax.random.normal(kr, (E, D), dtype=jnp.float32) * 0.02
        W1 = jax.random.normal(k1, (E, D, FF), dtype=jnp.float32) * 0.02
        W2 = jax.random.normal(k2, (E, FF, D), dtype=jnp.float32) * 0.02
        return {'x': x, 'Wr': Wr, 'W1': W1, 'W2': W2}
    _L1_ffn_all = _L1_ffn_setup()
    _L1_ffn_in = {k: v for k, v in _L1_ffn_all.items() if k in ('Wr', 'W1', 'W2')}
    del _L1_ffn_all
    return {'x': x, 'ctx_1024': ctx_1024, 'L0_xattn_Wq': _L0_xattn_in['Wq'], 'L0_xattn_Wk': _L0_xattn_in['Wk'], 'L0_xattn_Wv': _L0_xattn_in['Wv'], 'L0_xattn_Wo': _L0_xattn_in['Wo'], 'L0_xattn_bo': _L0_xattn_in['bo'], 'L0_attn_wq': _L0_attn_in['wq'], 'L0_attn_wk': _L0_attn_in['wk'], 'L0_attn_wv': _L0_attn_in['wv'], 'L0_attn_wgq': _L0_attn_in['wgq'], 'L0_attn_wgk': _L0_attn_in['wgk'], 'L0_attn_wgv': _L0_attn_in['wgv'], 'L0_attn_r_out_w': _L0_attn_in['r_out_w'], 'L0_attn_gate_local_w': _L0_attn_in['gate_local_w'], 'L0_attn_gate_remote_w': _L0_attn_in['gate_remote_w'], 'L0_attn_w_out': _L0_attn_in['w_out'], 'L0_ffn_gate_w': _L0_ffn_in['gate_w'], 'L0_ffn_w1': _L0_ffn_in['w1'], 'L0_ffn_b1': _L0_ffn_in['b1'], 'L0_ffn_w2': _L0_ffn_in['w2'], 'L0_ffn_b2': _L0_ffn_in['b2'], 'L1_xattn_wq': _L1_xattn_in['wq'], 'L1_xattn_bq': _L1_xattn_in['bq'], 'L1_xattn_wk': _L1_xattn_in['wk'], 'L1_xattn_bk': _L1_xattn_in['bk'], 'L1_xattn_wv': _L1_xattn_in['wv'], 'L1_xattn_bv': _L1_xattn_in['bv'], 'L1_xattn_wo': _L1_xattn_in['wo'], 'L1_xattn_bo': _L1_xattn_in['bo'], 'L1_attn_w': _L1_attn_in['w'], 'L1_attn_u': _L1_attn_in['u'], 'L1_attn_mix_k': _L1_attn_in['mix_k'], 'L1_attn_mix_v': _L1_attn_in['mix_v'], 'L1_attn_mix_r': _L1_attn_in['mix_r'], 'L1_attn_Wk': _L1_attn_in['Wk'], 'L1_attn_Wv': _L1_attn_in['Wv'], 'L1_attn_Wr': _L1_attn_in['Wr'], 'L1_attn_Wo': _L1_attn_in['Wo'], 'L1_ffn_Wr': _L1_ffn_in['Wr'], 'L1_ffn_W1': _L1_ffn_in['W1'], 'L1_ffn_W2': _L1_ffn_in['W2']}

def reference(x, ctx_1024, L0_xattn_Wq, L0_xattn_Wk, L0_xattn_Wv, L0_xattn_Wo, L0_xattn_bo, L0_attn_wq, L0_attn_wk, L0_attn_wv, L0_attn_wgq, L0_attn_wgk, L0_attn_wgv, L0_attn_r_out_w, L0_attn_gate_local_w, L0_attn_gate_remote_w, L0_attn_w_out, L0_ffn_gate_w, L0_ffn_w1, L0_ffn_b1, L0_ffn_w2, L0_ffn_b2, L1_xattn_wq, L1_xattn_bq, L1_xattn_wk, L1_xattn_bk, L1_xattn_wv, L1_xattn_bv, L1_xattn_wo, L1_xattn_bo, L1_attn_w, L1_attn_u, L1_attn_mix_k, L1_attn_mix_v, L1_attn_mix_r, L1_attn_Wk, L1_attn_Wv, L1_attn_Wr, L1_attn_Wo, L1_ffn_Wr, L1_ffn_W1, L1_ffn_W2):
    import jax
    import jax.numpy as jnp

    def _L0_xattn_ref(x, context, Wq, Wk, Wv, Wo, bo):
        import jax, jax.numpy as jnp
        import numpy as np
        HEADS = 8
        DIM_HEAD = 64
        DIM = 256
        CTX_DIM = 256
        HIDDEN = HEADS * DIM_HEAD
        b, n, _ = x.shape
        m = context.shape[1]
        scale = DIM_HEAD ** (-0.5)
        q = (x @ Wq).reshape(b, n, HEADS, DIM_HEAD).transpose(0, 2, 1, 3)
        k = (context @ Wk).reshape(b, m, HEADS, DIM_HEAD).transpose(0, 2, 1, 3)
        v = (context @ Wv).reshape(b, m, HEADS, DIM_HEAD).transpose(0, 2, 1, 3)
        scores = jnp.einsum('bhnd,bhmd->bhnm', q, k) * scale
        attn = jax.nn.softmax(scores, axis=-1)
        out = jnp.einsum('bhnm,bhmd->bhnd', attn, v)
        out = out.transpose(0, 2, 1, 3).reshape(b, n, HIDDEN)
        return out @ Wo + bo

    def _L0_attn_ref(x, wq, wk, wv, wgq, wgk, wgv, r_out_w, gate_local_w, gate_remote_w, w_out):
        import jax, jax.numpy as jnp
        import numpy as np
        D_MODEL = 256
        N_HEADS = 16
        LATENT_HEADS = 8
        LATENT_DIM = 128
        N_LATENTS = 64
        WINDOW = 64
        HEAD_DIM = D_MODEL // N_HEADS
        LAT_HD = LATENT_DIM // LATENT_HEADS
        B, S = (2, 1024)

        def _pool_to_latents(x):
            Bx, Sx, C = x.shape
            chunk = max(1, Sx // N_LATENTS)
            return x.reshape(Bx, N_LATENTS, chunk, C).mean(axis=2)

        def _local_window_attn(Q, K, V):
            Bx, H, Sx, D = Q.shape
            W = WINDOW
            nb = Sx // W
            Qb = Q.reshape(Bx, H, nb, W, D)
            Kp = jnp.pad(K, ((0, 0), (0, 0), (W, 0), (0, 0))).reshape(Bx, H, nb + 1, W, D)
            Vp = jnp.pad(V, ((0, 0), (0, 0), (W, 0), (0, 0))).reshape(Bx, H, nb + 1, W, D)
            Kw = jnp.concatenate([Kp[:, :, :-1], Kp[:, :, 1:]], axis=3)
            Vw = jnp.concatenate([Vp[:, :, :-1], Vp[:, :, 1:]], axis=3)
            i = jnp.arange(W)[:, None]
            j = jnp.arange(2 * W)[None, :]
            base = (j > i) & (j <= i + W)
            blk0 = (jnp.arange(nb) > 0)[:, None, None] | (j >= W)[None, :, :]
            mask = base[None, :, :] & blk0
            sc = jnp.einsum('bhnid,bhnjd->bhnij', Qb, Kw) / np.sqrt(D).astype(np.float32)
            sc = jnp.where(mask[None, None], sc, -jnp.inf)
            p = jax.nn.softmax(sc, axis=-1)
            out = jnp.einsum('bhnij,bhnjd->bhnid', p, Vw)
            return out.reshape(Bx, H, Sx, D)
        Bx, Sx, _ = x.shape
        chunk = max(1, Sx // N_LATENTS)
        Q = (x @ wq).reshape(Bx, Sx, N_HEADS, HEAD_DIM).transpose(0, 2, 1, 3)
        K = (x @ wk).reshape(Bx, Sx, N_HEADS, HEAD_DIM).transpose(0, 2, 1, 3)
        V = (x @ wv).reshape(Bx, Sx, N_HEADS, HEAD_DIM).transpose(0, 2, 1, 3)
        local = _local_window_attn(Q, K, V)
        GQ = (x @ wgq).reshape(Bx, Sx, LATENT_HEADS, LAT_HD).transpose(0, 2, 1, 3)
        GK = _pool_to_latents(x @ wgk).reshape(Bx, N_LATENTS, LATENT_HEADS, LAT_HD).transpose(0, 2, 1, 3)
        GV = _pool_to_latents(x @ wgv).reshape(Bx, N_LATENTS, LATENT_HEADS, LAT_HD).transpose(0, 2, 1, 3)
        lsc = jnp.einsum('bhsd,bhnd->bhsn', GQ, GK) / np.sqrt(LAT_HD).astype(np.float32)
        lmask = jnp.arange(N_LATENTS)[None, :] <= (jnp.arange(Sx) // chunk)[:, None]
        lsc = jnp.where(lmask[None, None], lsc, -jnp.inf)
        lp = jax.nn.softmax(lsc, axis=-1)
        rem = jnp.einsum('bhsn,bhnd->bhsd', lp, GV)
        rem = rem.transpose(0, 2, 1, 3).reshape(Bx, Sx, LATENT_DIM) @ r_out_w
        rem = rem.reshape(Bx, Sx, N_HEADS, HEAD_DIM).transpose(0, 2, 1, 3)
        gl = jax.nn.sigmoid(jnp.einsum('bhsd,hd->bhs', Q, gate_local_w))[..., None]
        gr = jax.nn.sigmoid(jnp.einsum('bhsd,hd->bhs', Q, gate_remote_w))[..., None]
        out = gl * local + gr * rem
        out = out.transpose(0, 2, 1, 3).reshape(Bx, Sx, D_MODEL)
        return out @ w_out

    def _L0_ffn_ref(x, gate_w, w1, b1, w2, b2):
        import jax, jax.numpy as jnp
        import numpy as np
        B, S, D, E, F, TOP_K = (4, 512, 256, 8, 1024, 2)
        b, s, d = x.shape
        e = gate_w.shape[1]
        xf = x.reshape(-1, d)
        t = xf.shape[0]
        logits = xf @ gate_w
        top_w, top_idx = jax.lax.top_k(logits, TOP_K)
        top_w = jax.nn.softmax(top_w.astype(jnp.float32), axis=-1).astype(x.dtype)
        combine = jnp.zeros((t, e), x.dtype).at[jnp.arange(t)[:, None], top_idx].add(top_w)
        h = jax.nn.gelu(jnp.einsum('td,edf->tef', xf, w1) + b1, approximate=False)
        y = jnp.einsum('tef,efd->ted', h, w2) + b2
        out = jnp.einsum('ted,te->td', y, combine)
        return out.reshape(b, s, d)

    def _L1_xattn_ref(query, key, value, wq, bq, wk, bk, wv, bv, wo, bo):
        import jax, jax.numpy as jnp
        import numpy as np
        DIM = 256
        NUM_HEAD = 16
        DIM_HEAD = DIM // NUM_HEAD
        B, S, _ = query.shape

        def proj(x, w, b):
            y = x @ w.T + b
            return y.reshape(B, -1, NUM_HEAD, DIM_HEAD).transpose(0, 2, 1, 3)
        Q = proj(query, wq, bq).astype(jnp.float32)
        K = proj(key, wk, bk).astype(jnp.float32)
        V = proj(value, wv, bv).astype(jnp.float32)
        energy = jnp.einsum('bhqd,bhkd->bhqk', Q, K) / np.sqrt(DIM_HEAD).astype(np.float32)
        attn = jax.nn.softmax(energy, axis=-1)
        out = jnp.einsum('bhqk,bhkd->bhqd', attn, V)
        out = out.transpose(0, 2, 1, 3).reshape(B, S, DIM)
        return out @ wo.T + bo

    def _L1_attn_ref(x, w, u, mix_k, mix_v, mix_r, Wk, Wv, Wr, Wo):
        import jax, jax.numpy as jnp
        import numpy as np
        B, T, C = (8, 512, 256)
        NEG = -1e+30

        def wkv(w, u, k, v):
            w_exp = -jnp.exp(w)
            p0 = jnp.zeros(k.shape[::2], k.dtype)
            q0 = jnp.zeros(k.shape[::2], k.dtype)
            o0 = jnp.full(k.shape[::2], NEG, k.dtype)

            def step(carry, kv_t):
                p, q, o = carry
                k_t, v_t = kv_t
                uk = u + k_t
                no = jnp.maximum(o, uk)
                A = jnp.exp(o - no)
                Bc = jnp.exp(uk - no)
                out = (A * p + Bc * v_t) / (A * q + Bc)
                wo = w_exp + o
                no2 = jnp.maximum(wo, k_t)
                A2 = jnp.exp(wo - no2)
                B2 = jnp.exp(k_t - no2)
                return ((A2 * p + B2 * v_t, A2 * q + B2, no2), out)
            kT = jnp.swapaxes(k, 0, 1)
            vT = jnp.swapaxes(v, 0, 1)
            _, outs = jax.lax.scan(step, (p0, q0, o0), (kT, vT))
            return jnp.swapaxes(outs, 0, 1)
        x_prev = jnp.pad(x, ((0, 0), (1, 0), (0, 0)))[:, :-1]
        xk = x_prev + mix_k * (x - x_prev)
        xv = x_prev + mix_v * (x - x_prev)
        xr = x_prev + mix_r * (x - x_prev)
        k = jnp.einsum('btc,dc->btd', xk, Wk)
        v = jnp.einsum('btc,dc->btd', xv, Wv)
        sr = jax.nn.sigmoid(jnp.einsum('btc,dc->btd', xr, Wr))
        rwkv = sr * wkv(w, u, k, v)
        return jnp.einsum('btc,dc->btd', rwkv, Wo)

    def _L1_ffn_ref(x, Wr, W1, W2):
        import jax, jax.numpy as jnp
        import numpy as np
        B, T, D, FF, E, TOP_K = (8, 512, 256, 1024, 8, 2)
        Bs, Ts, Ds = x.shape
        Ne = Wr.shape[0]
        xf = x.reshape(-1, Ds)
        N = xf.shape[0]
        logits = xf @ Wr.T
        topk_vals, topk_idx = jax.lax.top_k(logits, TOP_K)
        w = jax.nn.softmax(topk_vals.astype(jnp.float32), axis=-1).astype(x.dtype)
        idx_flat = topk_idx.reshape(-1)
        w_flat = w.reshape(-1)
        sort_idx = jnp.argsort(idx_flat)
        rev = sort_idx // TOP_K
        sw = w_flat[sort_idx]
        perm = xf[rev]
        S = perm.shape[0]
        chunks = perm.reshape(Ne, S // Ne, Ds)
        h = jax.nn.gelu(jnp.einsum('ecd,edf->ecf', chunks, W1), approximate=False)
        eo = jnp.einsum('ecf,efd->ecd', h, W2).reshape(S, Ds)
        out = jnp.zeros((N, Ds), dtype=x.dtype).at[rev].add(eo * sw[:, None])
        return out.reshape(Bs, Ts, Ds)
    x = x + _L0_xattn_ref(_layernorm(x, axis=-1), ctx_1024, L0_xattn_Wq, L0_xattn_Wk, L0_xattn_Wv, L0_xattn_Wo, L0_xattn_bo)
    x = x + _L0_attn_ref(_layernorm(x, axis=-1), L0_attn_wq, L0_attn_wk, L0_attn_wv, L0_attn_wgq, L0_attn_wgk, L0_attn_wgv, L0_attn_r_out_w, L0_attn_gate_local_w, L0_attn_gate_remote_w, L0_attn_w_out)
    x = x + _L0_ffn_ref(_layernorm(x, axis=-1), L0_ffn_gate_w, L0_ffn_w1, L0_ffn_b1, L0_ffn_w2, L0_ffn_b2)
    x = x + _L1_xattn_ref(_layernorm(x, axis=-1), ctx_1024, ctx_1024, L1_xattn_wq, L1_xattn_bq, L1_xattn_wk, L1_xattn_bk, L1_xattn_wv, L1_xattn_bv, L1_xattn_wo, L1_xattn_bo)
    x = x + _L1_attn_ref(_layernorm(x, axis=-1), L1_attn_w, L1_attn_u, L1_attn_mix_k, L1_attn_mix_v, L1_attn_mix_r, L1_attn_Wk, L1_attn_Wv, L1_attn_Wr, L1_attn_Wo)
    x = x + _L1_ffn_ref(_layernorm(x, axis=-1), L1_ffn_Wr, L1_ffn_W1, L1_ffn_W2)
    return x

_drawn_inputs = setup_inputs


def setup_inputs(seed=0):
    import zlib

    import numpy as np

    out = dict(_drawn_inputs(seed))
    spreads = {'L0_ffn_b1': (0.0, 0.1), 'L0_ffn_b2': (0.0, 0.1)}
    factors = {'L0_attn_wq': 5.186,
     'L0_attn_wk': 8.0,
     'L0_attn_wgq': 8.0,
     'L0_attn_wgk': 120.108,
     'L0_attn_gate_local_w': 5.952,
     'L0_attn_gate_remote_w': 121.652,
     'L1_xattn_bq': 4.004,
     'L1_xattn_bk': 200.0,
     'L1_attn_w': 8.0,
     'L1_attn_u': 8.0,
     'L1_attn_mix_k': 8.0,
     'L1_attn_mix_v': 5.458,
     'L1_attn_mix_r': 8.0,
     'L1_attn_Wk': 8.0,
     'L1_attn_Wr': 8.0}
    for name, (base, spread) in spreads.items():
        noise = np.random.default_rng([zlib.crc32(name.encode()), seed]).standard_normal(out[name].shape)
        drawn = base * np.exp(spread * noise) if base else spread * noise
        out[name] = jnp.asarray(drawn.astype(out[name].dtype))
    for name, factor in factors.items():
        out[name] = (out[name] * factor).astype(out[name].dtype)
    return out
```

```python
import numpy as np
import concourse.bass as bass
from concourse import mybir
from contextlib import ExitStack

F32 = mybir.dt.float32
F32R = mybir.dt.float32r
U32 = mybir.dt.uint32
ALU = mybir.AluOpType
ACT = mybir.ActivationFunctionType
AX = mybir.AxisListType

B, S, D = 2, 256, 256
TOK = B * S
TT = TOK // 128
CTX = 4096
CHUNK = 512
NCH = CTX // CHUNK
KT = CHUNK // 128
EPS = 1e-5
NEG = -1e30
BLOCK_ENGINES = 4


class Cross:

    def __init__(self, layer, heads, dim):
        self.layer, self.heads, self.dim = layer, heads, dim
        self.hid = heads * dim
        self.tiles = self.hid // 128
        self.hpt = heads // self.tiles
        self.groups = self.hid // 64
        self.hpg = heads // self.groups
        self.scale = float(dim) ** -0.5
        self.units = self.groups * (1 if self.hpg == 1 else KT)
        self.upg = self.units // self.groups


X0 = Cross(0, 8, 64)
X1 = Cross(1, 16, 16)


def perceiver(nc, ins, out, upto=6):
    ctx = ExitStack()
    with ctx:
        def sb(name, shape, dt=F32):
            return ctx.enter_context(nc.sbuf_tensor(name, shape, dt))

        def sem(name):
            return ctx.enter_context(nc.semaphore(name))

        ident = sb("ident", [128, 128])
        ones = sb("ones", [128, 128])
        mask_half = sb("mask_half", [128, 2])
        mask_16th = sb("mask_16th", [128, 8])
        den_pick = sb("den_pick", [128, 128])
        iota8 = sb("iota8", [128, 8])
        zeros = sb("zeros", [128, 128], mybir.dt.bfloat16)
        x = sb("x", [128, TT, D])
        q_hi = sb("q_hi", [128, 16, S], F32R)
        q_hh = sb("q_hh", [128, 16, S], F32R)
        q_lm = sb("q_lm", [128, 16, S], F32R)
        k_hl = [sb(f"k_hl{i}", [128, CHUNK], F32R) for i in range(2)]
        k_h1 = [sb(f"k_h1{i}", [65, CHUNK], F32R) for i in range(2)]
        c_hi = sb("c_hi", [128, 2, CHUNK], F32R)
        c_lo = sb("c_lo", [128, 2, CHUNK], F32R)
        k_max = [sb(f"k_max{i}", [128, CHUNK], F32R) for i in range(2)]
        w_split = sb("w_split", [128, 4, 1024], F32R)
        wk_hi, wk_lo, wv_hi, wv_lo = (w_split[:, n, :].rearrange("p (f n) -> p f n", f=2) for n in range(4))
        shift = sb("shift", [32, 128], F32R)
        c_in = sb("c_in", [128, KT, D])
        qT = sb("qT", [128, 4, TOK])
        V = sb("V", [128, KT, 512])
        P = sb("P", [128, 4, 1024])
        arena = sb("arena", [128, 20480])
        xn, xnT = P[:, 0, :].rearrange("p (t d) -> p t d", t=TT), P[:, 1, :].rearrange("p (f t) -> p f t", f=2)
        stats = sb("stats", [128, TT, 6])
        mv = sb("mv", [128, TT, 2])
        rstd = sb("rstd", [128, TT])
        mneg = sb("mneg", [128, 32])
        bias = sb("bias", [128, 16])
        row = sb("row", [1, 256])

        bank = [ctx.enter_context(nc.psum_tensor(f"bank{i}", [128, 512], F32)) for i in (0, 1)]
        score = [ctx.enter_context(nc.psum_tensor(f"score{i}", [128, 1024], F32)) for i in range(2)]
        bank += [ctx.enter_context(nc.psum_tensor(f"bank{i}", [128, 512], F32)) for i in (6, 7)]

        stage_done = sem("stage_done")
        const_ready = sem("const_ready")
        pool_chain, dve_chain, act_chain = sem("pool_chain"), sem("dve_chain"), sem("act_chain")
        x_in = sem("x_in")
        out_stored = sem("out_stored")
        def phase(name, keys):
            return {k: sem(f"{name}_{k}") for k in keys.split()}

        CA = {c.layer: phase(f"ca{c.layer}", "w w0 whl qp q wo wop op res bias" + (" wT wTc pad" if c.layer else "")) for c in (X0, X1)}
        class Phase:

            def __init__(self, sems, base):
                self.sems, self.base = sems, base

            def __getitem__(self, key):
                return self.sems[key]

            def n(self, key, count):
                return count + self.base[key]

        ACC_AHEAD = 3 * KT

        def max_counts(c, b):
            return dict(qh=c.heads, qhh=2 * c.groups, ql=c.heads, ctx=16 * NCH, tr=2 * NCH, ch=2 * NCH, cl=2 * NCH,
                        kp=c.tiles * NCH, kev=c.tiles * NCH, s=c.heads * NCH, red=c.heads * NCH,
                        m=1, mt=1, mr=1, md=16)

        def att_counts(c, b):
            own = dict(z=1, acc=8 * KT * NCH, osb=0) if c.layer == 0 else dict(z=1 - b, acc=0, osb=2)
            return dict(ctx=16 * NCH, tr=2 * NCH, ch=2 * NCH, cl=2 * NCH, vp=KT * NCH, v=KT * NCH, khi=c.groups * NCH,
                        kl=c.groups * NCH, s=c.units * NCH,
                        p=c.units * NCH, pfree=4 + c.units * NCH, d=1, rd=1, o=4, **own)

        ahead = {e: [] for e in ("sp", "pe", "act", "dve", "pool")}
        signals = dict(qh="dve", qhh="act", ql="dve", ctx="sp", tr="pe", ch="act", cl="dve", kp="pe", kev="act", s="pe",
                       red="dve", m="dve", mt="pe", mr="act", md="sp", z="pool", vp="pe", v="dve", khi="dve", kl="dve",
                       p="act", pfree="pe", acc="pool", d="pe", rd="dve", o="dve", osb="act")

        def once(name, looped, rest=""):
            sems = {k: sem(f"{name}_{k}") for k in (*looped, *rest.split())}
            for k, e in looped.items():
                ahead[e].append(sems[k])
            return Phase(sems, {k: int(k in looped) for k in sems})

        def signal_ahead(eng, name):
            for s in ahead[name]:
                eng.sem_inc(s, 1)

        def runs(name, counts):
            sems, base, made = {k: sem(f"{name}_{k}") for k in counts(X0, 0)}, {k: 1 for k in counts(X0, 0)}, {}
            for k in sems:
                ahead[signals[k]].append(sems[k])
            for c in (X0, X1):
                for b in range(B):
                    credit = {"s": c.hpt} if name == "max" else {"s": c.upg, "acc": ACC_AHEAD if c.layer == 0 else 0}
                    made[c.layer, b] = Phase(sems, {k: n + credit.get(k, 0) for k, n in base.items()})
                    for k, total in counts(c, b).items():
                        base[k] += total + credit.get(k, 0)
            return made

        ln_counts = dict(var=1, std=1, xn=TT, tr=1, xT=2)
        ln_sems = {k: sem(f"ln_{k}") for k in ln_counts}
        LN = [Phase(ln_sems, {k: n * total for k, total in ln_counts.items()}) for n in range(6)]
        MAXP, ATT = runs("max", max_counts), runs("att", att_counts)

        block = ctx.enter_context(nc.Block())

        def stage_end(eng, n):
            eng.drain().then_inc(stage_done, 1)
            eng.wait_ge(stage_done, BLOCK_ENGINES * n)

        def hidden_of(c, g):
            return g // 2, 64 * (g % 2)

        Kst = {c.layer: arena[:, 0:c.tiles * CTX].rearrange("p (t k) -> p t k", t=c.tiles) for c in (X0, X1)}
        acc_p = arena[:, 16384:18432].rearrange("p (h q) -> p h q", h=8)
        mx = arena[:, 16384:16384 + NCH * 32].rearrange("p (c h) -> p c h", c=NCH)
        oT = arena[:, 18432:20480].rearrange("p (k t) -> p k t", k=4)
        w_raw = arena[:, 0:3072].rearrange("p (w f n) -> p w f n", w=3, f=2)
        w_nat = arena[:, 4096:5632].rearrange("p (w o n) -> p w o n", w=3, o=2)
        wo_nat = c_in[:, 0:2, :]
        wo_pad = V[:, :, :].rearrange("p a n -> p (a n)")[:, 0:1024].rearrange("p (o k) -> p o k", o=2)
        wout = qT[:, 0:2, :].rearrange("p a t -> p (a t)").rearrange("p (k n) -> p k n", k=4)
        Vp = V[:, :, :].rearrange("p a (h d) -> p a h d", h=16)

        def bc(ap, axis, n):
            new = ap.unsqueeze(axis)
            shape = list(new.shape)
            shape[axis] = n
            return new.broadcast_to(shape)


        NHL, NHG, HD, LAT = 16, 8, 16, 64
        GRP = S // LAT
        la = {k: sem("la_" + k) for k in
              "w msk pj pe gt g qp s sb m e tr ptd pta o rq rt rtc rem cb ct ctc out res".split()}
        la_wqkv = arena[:, 0:1536].rearrange("p (w f n) -> p w f n", w=3, f=2)
        la_wg = arena[:, 1536:2304].rearrange("p (w f n) -> p w f n", w=3, f=2)
        la_rout = arena[:, 2304:2560]
        la_wout = arena[:, 2560:3072].rearrange("p (f n) -> p f n", f=2)
        la_KT = arena[:, 3072:4096].rearrange("p (f t) -> p f t", f=2)
        la_QT = arena[:, 4096:5120].rearrange("p (f t) -> p f t", f=2)
        la_GQT, la_GKT = arena[:, 5120:5632], arena[:, 5632:5760]
        la_gate = arena[:, 5760:5888].rearrange("p (t h) -> p t h", t=TT)
        la_V = arena[:, 5888:6976].rearrange("p (t h d) -> p t h d", t=TT, h=NHL)
        la_GV = arena[:, 6976:7248].rearrange("p (b h d) -> p b h d", b=B, h=NHG)
        la_q = arena[:, 7248:9296].rearrange("p (h q) -> p h q", h=NHL)
        la_gq = arena[:, 9296:10320].rearrange("p (h q) -> p h q", h=NHG)
        la_S = arena[:, 10320:14416].rearrange("p (h k) -> p h k", h=NHL)
        la_PT = arena[:, 14416:18512]
        la_mask = arena[:, 18512:18768]
        la_lmask = arena[:, 18768:18896].rearrange("p (u n) -> p u n", u=2)
        la_m = arena[:, 18896:18920]
        la_r = arena[:, 18920:18944]
        la_rs = arena[:, 18944:18960]
        la_cb, la_cT = arena[:, 18992:19248], arena[:, 19248:19504]
        la_rq, la_rqT = arena[:, 19504:19632], arena[:, 19632:19760]
        la_xp = arena[:, 19760:20272].rearrange("p (f b c n) -> p f b c n", f=2, b=B, c=2)
        la_xs = qT[:, 0, 0:256].rearrange("p (f n) -> p f n", f=2)
        la_LS = P[:, 2, 0:512].rearrange("p (h n) -> p h n", h=NHG)
        la_LPT = P[:, 2, 512:1024]
        la_G = P[:, 3, 0:64].rearrange("p (f h) -> p f h", f=2)
        la_gcol = bias[:, 0:4].rearrange("p (f w) -> p f w", f=2)
        la_keys = [1 if t % 2 == 0 else 2 for t in range(TT)]
        la_bufs = [NHL * k * 128 // 1024 for k in la_keys]
        la_quads = [NHL * k // 4 + 1 for k in la_keys]

        def upto_t(counts, t):
            return sum(counts[:t])

        E, F = 8, 1024
        FM = F // 128
        gm = {k: sem("gm_" + k) for k in "w lp t ex cT cTc b2 done bt btc".split()}
        em = once("em", dict(w="sp", w1h="act", w1l="dve", w2h="act", w2l="dve", h="pe", g="act", hh="dve", hl="dve", y="pe", acc="dve"))
        cm = once("cm", dict(w="sp", w2="sp", h="pe", g="act", y="pe", yc="dve"), "lp t ex c pw pm pmc tr trc s res iota wr")
        gate_w = arena[:, 0:16].rearrange("p (f e) -> p f e", f=2)
        lg = arena[:, 16:48].rearrange("p (t e) -> p t e", t=TT)
        top8 = arena[:, 48:80].rearrange("p (t e) -> p t e", t=TT)
        idx8 = arena[:, 80:112].bitcast(U32).rearrange("p (t e) -> p t e", t=TT)
        idxf = arena[:, 112:144].rearrange("p (t e) -> p t e", t=TT)
        tw = arena[:, 144:152].rearrange("p (k t) -> p k t", k=2)
        comb = arena[:, 152:184].rearrange("p (t e) -> p t e", t=TT)
        ohtmp = arena[:, 184:248].rearrange("p (k t e) -> p k t e", k=2, t=TT)
        rank_e = arena[:, 248:280].rearrange("p (t e) -> p t e", t=TT)
        rank = arena[:, 280:288].rearrange("p (k t) -> p k t", k=2)
        tot = arena[:, 288:296]
        incl = arena[:, 296:304]
        combT = arena[0:8, 512:1024]
        b2sb = arena[0:8, 1024:1280]
        b1n = arena[0:64, 1280:1408]
        b1T = arena[:, 1408:1472]
        wr_nat = arena[0:8, 1472:1728]
        w1raw = arena[:, 2048:4096].rearrange("p (f n) -> p f n", f=2)
        w2raw = arena[:, 4096:6144].rearrange("p (k n) -> p k n", k=FM)
        h32 = arena[:, 6144:10240].rearrange("p (m t) -> p m t", m=FM)
        w1_hi, w1_lo = (w_split[:, 2 * n:2 * n + 2, :] for n in range(2))
        w2_hi, w2_lo = (q_lm[:, 8 * n:8 * n + 8, :] for n in range(2))
        h_hi = q_hi[:].rearrange("p h q -> p (h q)").rearrange("p (m t) -> p m t", m=FM)
        h_lo = q_hh[:].rearrange("p h q -> p (h q)").rearrange("p (m t) -> p m t", m=FM)

        rw = {k: sem("rw_" + k) for k in "w v we tr trc mx pj ev sr a a2 o out res".split()}
        rw_nat = arena[:, 0:2048].rearrange("p (w o n) -> p w o n", w=4, o=2)
        rw_W = arena[:, 2048:4096].rearrange("p (w f n) -> p w f n", w=4, f=2)
        rw_xp, rw_d, rw_xk, rw_xv, rw_xr, rw_k, rw_v, rw_sr = (
            arena[:, 4096 + 1024 * n:5120 + 1024 * n].rearrange("p (m b t) -> p m b t", m=2, b=B) for n in range(8))
        rw_o, rw_p, rw_q = (arena[:, 12288 + 1028 * n:13316 + 1028 * n].rearrange("p (m b t) -> p m b t", m=2, b=B) for n in range(3))
        rw_no, rw_A, rw_Bc = (arena[:, 15372 + 1024 * n:16396 + 1024 * n].rearrange("p (m b t) -> p m b t", m=2, b=B) for n in range(3))
        rw_A2, rw_B2 = rw_xp, rw_d
        rw_num, rw_den, rw_out = rw_xk, rw_xv, rw_xr
        rw_vec = bias[:, 0:10].rearrange("p (n f) -> p n f", n=5)
        rw_wexp = bias[:, 10:12]

        SL = 2 * TOK
        cw1 = [arena[:, 4096 * n + 2048:4096 * n + 4096].rearrange("p (f n) -> p f n", f=2) for n in range(1)]
        cw1 = arena[:, 2048:4096].rearrange("p (f n) -> p f n", f=2)
        cw2 = arena[:, 4096:6144].rearrange("p (k n) -> p k n", k=FM)
        PA = arena[:, 6144:10240].rearrange("p (t s) -> p t s", t=TT)
        PW = arena[:, 10240:14336].rearrange("p (t s) -> p t s", t=TT)
        PWT = arena[:, 14336:18432].rearrange("p (e t) -> p e t", e=E)
        Ptmp = arena[:, 18432:20480].rearrange("p (n s) -> p n s", n=2)
        permT = qT[:, :, :].rearrange("p a t -> p (a t)").rearrange("p (f s) -> p f s", f=2)
        hT = c_in[:, :, :].rearrange("p a t -> p (a t)").rearrange("p (m s) -> p m s", m=FM)
        yS = V[:, :, :].rearrange("p a t -> p (a t)").rearrange("p (e d) -> p e d", e=E)
        iota_s = P[:, 2, :]
        before = P[:, 3, 0:128]

        @block.sync
        def _(sp):
            signal_ahead(sp, "sp")
            sp.dma_start(x[:], ins["x"].rearrange("b (u p) d -> p (b u) d", p=128)).then_inc(x_in, 16)

            def cross(c, stage):
                a = CA[c.layer]
                if c.layer == 0:
                    for n, w in enumerate(("Wq", "Wk", "Wv")):
                        sp.dma_start(w_raw[:, n], ins[f"L0_xattn_{w}"].rearrange("(f p) n -> p f n", p=128)).then_inc(a["w"], 16)
                    sp.dma_start(row[0:1, 0:D], ins["L0_xattn_bo"].rearrange("(a n) -> a n", a=1)).then_inc(a["bias"], 16)
                else:
                    sp.wait_ge(stage_done, BLOCK_ENGINES * stage)
                    for n, w in enumerate(("wq", "wk", "wv")):
                        sp.dma_start(w_nat[:, n], ins[f"L1_xattn_{w}"].rearrange("(o p) n -> p o n", p=128)).then_inc(a["w"], 16)
                    sp.dma_start(wo_nat, ins["L1_xattn_wo"].rearrange("(o p) n -> p o n", p=128)).then_inc(a["w"], 16)
                    sp.dma_start(row[0:1, 0:D], ins["L1_xattn_bo"].rearrange("(a n) -> a n", a=1)).then_inc(a["bias"], 16)
                    for n, w in enumerate(("bq", "bk")):
                        for f in range(2):
                            sp.dma_start(bias[:, 2 * n + f:2 * n + f + 1],
                                         ins[f"L1_xattn_{w}"][128 * f:128 * f + 128].rearrange("(p a) -> p a", a=1)).then_inc(a["bias"], 16)
                    sp.wait_ge(a["pad"], 1)
                    for g in range(4):
                        for j in range(4):
                            h = 4 * g + j
                            sp.dma_start(bias[32 * j:32 * j + 16, 4 + g:5 + g],
                                         ins["L1_xattn_bv"][16 * h:16 * h + 16].rearrange("(p a) -> p a", a=1)).then_inc(a["bias"], 16)
                for b in range(B):
                    chunks = ins["ctx_1024"][b].rearrange("(c k p) d -> c p k d", k=KT, p=128)
                    m, t = MAXP[c.layer, b], ATT[c.layer, b]
                    for ph in (m, t):
                        if ph is m and b == 0 and c.layer == 1:
                            sp.wait_ge(a["pad"], 2)
                        if ph is m and b == 1:
                            sp.wait_ge(ATT[c.layer, 0]["tr"], ATT[c.layer, 0].n("tr", 2 * NCH))
                        if ph is t:
                            sp.wait_ge(m["tr"], m.n("tr", 2 * NCH))
                        with sp.Fori(0, NCH) as i:
                            sp.wait_ge(ph["tr"], ph.n("tr", 2 * i))
                            sp.dma_start(c_in[:], chunks[bass.ds(i, 1), :, :, :].rearrange("a p k d -> p (a k) d")).then_inc(ph["ctx"], 16)
                        if ph is m:
                            sp.wait_ge(m["mr"], m.n("mr", 1))
                            sp.dma_start(q_lm[64:65, 0:c.heads, :].rearrange("a h q -> a (h q)").bitcast(F32),
                                         shift[0:2 * c.heads, :].bitcast(F32)).then_inc(m["md"], 16)
                    if b == 1 and c.layer == 0:
                        sp.wait_ge(MAXP[0, 1]["ql"], MAXP[0, 1].n("ql", c.heads))
                        sp.dma_start(wout, ins["L0_xattn_Wo"].rearrange("(k p) n -> p k n", p=128)).then_inc(a["wo"], 16)


            def stage_free(n):
                sp.wait_ge(stage_done, BLOCK_ENGINES * n)

            def local_attention():
                stage_free(1)
                for n, w in enumerate(("wq", "wk", "wv")):
                    sp.dma_start(la_wqkv[:, n], ins[f"L0_attn_{w}"].rearrange("(f p) n -> p f n", p=128)).then_inc(la["w"], 16)
                for n, w in enumerate(("wgq", "wgk", "wgv")):
                    sp.dma_start(la_wg[:, n], ins[f"L0_attn_{w}"].rearrange("(f p) n -> p f n", p=128)).then_inc(la["w"], 16)
                sp.dma_start(la_rout, ins["L0_attn_r_out_w"]).then_inc(la["w"], 16)
                sp.dma_start(la_wout, ins["L0_attn_w_out"].rearrange("(f p) n -> p f n", p=128)).then_inc(la["w"], 16)
                for n, w in enumerate(("gate_local_w", "gate_remote_w")):
                    for f in range(2):
                        sp.dma_start(la_gcol[:, f, n:n + 1],
                                     ins[f"L0_attn_{w}"][8 * f:8 * f + 8, :].rearrange("h (d a) -> (h d) a", a=1)).then_inc(la["w"], 16)

            def dense_mixture():
                stage_free(2)
                sp.dma_start(gate_w, ins["L0_ffn_gate_w"].rearrange("(f p) e -> p f e", p=128)).then_inc(gm["w"], 16)
                sp.dma_start(b2sb, ins["L0_ffn_b2"]).then_inc(gm["w"], 16)
                sp.dma_start(b1n, ins["L0_ffn_b1"].rearrange("e (m p) -> (e m) p", p=128)).then_inc(gm["w"], 16)
                w1d = ins["L0_ffn_w1"].rearrange("e (f p) n -> e p f n", p=128)
                w2d = ins["L0_ffn_w2"].rearrange("e (k p) n -> e p k n", p=128)
                with sp.Fori(0, E) as e:
                    sp.wait_ge(em["w1l"], em.n("w1l", e))
                    sp.dma_start(w1raw, w1d[bass.ds(e, 1)].rearrange("a p f n -> p (a f) n")).then_inc(em["w"], 16)
                    sp.wait_ge(em["w2l"], em.n("w2l", e))
                    sp.dma_start(w2raw, w2d[bass.ds(e, 1)].rearrange("a p k n -> p (a k) n")).then_inc(em["w"], 16)

            def rwkv():
                stage_free(4)
                for n, w in enumerate(("Wk", "Wv", "Wr", "Wo")):
                    sp.dma_start(rw_nat[:, n], ins[f"L1_attn_{w}"].rearrange("(o p) n -> p o n", p=128)).then_inc(rw["w"], 16)
                for n, w in enumerate(("w", "u", "mix_k", "mix_v", "mix_r")):
                    for f in range(2):
                        sp.dma_start(rw_vec[:, n, f:f + 1], ins[f"L1_attn_{w}"][128 * f:128 * f + 128].rearrange("(p a) -> p a", a=1)).then_inc(rw["v"], 16)

            def chunk_mixture():
                stage_free(5)
                sp.dma_start(wr_nat, ins["L1_ffn_Wr"]).then_inc(cm["wr"], 16)
                w1d = ins["L1_ffn_W1"].rearrange("e (f p) n -> e p f n", p=128)
                w2d = ins["L1_ffn_W2"].rearrange("e (k p) n -> e p k n", p=128)
                with sp.Fori(0, E) as e:
                    sp.wait_ge(cm["h"], cm.n("h", FM * e))
                    sp.dma_start(cw1, w1d[bass.ds(e, 1)].rearrange("a p f n -> p (a f) n")).then_inc(cm["w"], 16)
                    sp.wait_ge(cm["y"], cm.n("y", e))
                    sp.dma_start(cw2, w2d[bass.ds(e, 1)].rearrange("a p k n -> p (a k) n")).then_inc(cm["w2"], 16)

            cross(X0, 0)
            if upto >= 2: local_attention()
            if upto >= 3: dense_mixture()
            if upto >= 4: cross(X1, 3)
            if upto >= 5: rwkv()
            if upto >= 6: chunk_mixture()
            sp.wait_ge(stage_done, BLOCK_ENGINES * upto)
            sp.dma_start(out.rearrange("b (u p) d -> p (b u) d", p=128), x[:]).then_inc(out_stored, 16)
            sp.wait_ge(out_stored, 16)

        @block.gpsimd
        def _(pool):
            chain = [0]

            def link(i):
                chain[0] += 1
                i.then_inc(pool_chain, 1)
                pool.wait_ge(pool_chain, chain[0])

            signal_ahead(pool, "pool")
            link(pool.memset(ident[:], 0.0))
            link(pool.affine_select(out=ident[:], in_=ident[:], compare_op=ALU.not_equal, fill=1.0,
                                    base=0, pattern=[[-1, 128]], channel_multiplier=1))
            link(pool.memset(ones[:], 1.0))
            link(pool.memset(zeros[:], 0.0))
            for tile, width in ((mask_half, 64), (mask_16th, 16)):
                n = 128 // width
                link(pool.memset(tile[:], 1.0))
                link(pool.affine_select(out=tile[:], in_=tile[:], compare_op=ALU.is_ge, fill=0.0,
                                        base=0, pattern=[[-width, n]], channel_multiplier=1))
                link(pool.affine_select(out=tile[:], in_=tile[:], compare_op=ALU.is_gt, fill=0.0,
                                        base=width, pattern=[[width, n]], channel_multiplier=-1))
            link(pool.memset(den_pick[:], 0.0))
            link(pool.affine_select(out=den_pick[:].rearrange("p (j d) -> p j d", j=4),
                                    in_=den_pick[:].rearrange("p (j d) -> p j d", j=4),
                                    compare_op=ALU.not_equal, fill=1.0, base=-16,
                                    pattern=[[-32, 4], [0, 32]], channel_multiplier=1))
            link(pool.iota(iota8[:], pattern=[[1, 8]], base=0, channel_multiplier=0,
                           allow_small_or_imprecise_dtypes=True))
            for i in range(2):
                pool.memset(k_h1[i][64:65, :].bitcast(F32), 1.0)
            pool.engine_nop().then_inc(const_ready, 1)

            def cross(c, stage):
                for b in range(B):
                    t = ATT[c.layer, b]
                    if c.layer == 0:
                        if b == 1:
                            pool.wait_ge(ATT[0, 0]["d"], ATT[0, 0].n("d", 1))
                        pool.sem_inc(t["acc"], ACC_AHEAD)
                        pool.wait_ge(MAXP[0, b]["m"], MAXP[0, b].n("m", 1))
                        pool.memset(acc_p, 0.0).then_inc(t["z"], 1)
                    if c.layer == 1 and b == 0:
                        pool.wait_ge(CA[1]["wop"], 1)
                        link(pool.memset(V[:], 0.0))
                        pool.memset(Vp[:, :, :, 16:17], 1.0).then_inc(t["z"], 1)
                    if c.layer == 1:
                        continue
                    with pool.Fori(0, NCH) as i:
                            def sums(u):
                                pool.wait_ge(t["p"], t.n("p", i * 8 + u + 1))
                                for k in range(KT):
                                    n = (i * 8 + u) * KT + k
                                    if k == 0 and u == 0:
                                        pool.wait_ge(t["z"], t.n("z", 1))
                                    pool.wait_ge(t["acc"], t.n("acc", n))
                                    pool.tensor_tensor(acc_p[:, u, :], acc_p[:, u, :],
                                                       P[:, u % 4, k * S:(k + 1) * S], ALU.add).then_inc(t["acc"], 1)
                            for u in range(8):
                                sums(u)


            def local_attention():
                diag, off = la_mask[:, 128:256], la_mask[:, 0:128]
                link(pool.memset(la_mask, 0.0))
                link(pool.affine_select(out=diag, in_=diag, compare_op=ALU.is_ge, fill=NEG, base=0,
                                        pattern=[[-1, 128]], channel_multiplier=1))
                link(pool.affine_select(out=diag, in_=diag, compare_op=ALU.is_gt, fill=NEG, base=64,
                                        pattern=[[1, 128]], channel_multiplier=-1))
                link(pool.affine_select(out=off, in_=off, compare_op=ALU.is_gt, fill=NEG, base=-64,
                                        pattern=[[1, 128]], channel_multiplier=-1))
                link(pool.memset(la_lmask, 0.0))
                link(pool.affine_select(out=la_lmask, in_=la_lmask, compare_op=ALU.is_ge, fill=NEG, base=0,
                                        pattern=[[128, 2], [-GRP, LAT]], channel_multiplier=1))
                pool.memset(la_V[:, :, :, HD:HD + 1], 1.0)
                link(pool.memset(la_GV, 0.0))
                for r in (0, 1):
                    last = pool.memset(la_GV[64 * r:64 * r + 64, :, r::2, HD:HD + 1], 1.0)
                last.then_inc(la["msk"], 1)

            def chunk_mixture():
                link(pool.iota(iota_s, pattern=[[1, SL]], base=0, channel_multiplier=0, allow_small_or_imprecise_dtypes=True))
                link(pool.memset(before, 1.0))
                pool.affine_select(out=before, in_=before, compare_op=ALU.is_gt, fill=0.0, base=0,
                                   pattern=[[1, 128]], channel_multiplier=-1).then_inc(cm["iota"], 1)

            pool.wait_ge(const_ready, 1)
            cross(X0, 0)
            stage_end(pool, 1)
            if upto >= 2:
                local_attention()
                stage_end(pool, 2)
            if upto >= 3: stage_end(pool, 3)
            if upto >= 4:
                cross(X1, 3)
                stage_end(pool, 4)
            if upto >= 5: stage_end(pool, 5)
            if upto >= 6:
                chunk_mixture()
                stage_end(pool, 6)

        @block.scalar
        def _(act):
            chain = [0]

            def link(i):
                chain[0] += 1
                i.then_inc(act_chain, 1)
                act.wait_ge(act_chain, chain[0])

            def layer_norm(n):
                ln = LN[n]
                act.wait_ge(ln["var"], ln.n("var", 1))
                act.activation(rstd[:], mv[:, :, 1], ACT.Sqrt).then_inc(ln["std"], 1)
                act.wait_ge(ln["tr"], ln.n("tr", 1))
                act.activation(xnT[:, 0, :], bank[0][:], ACT.Copy).then_inc(ln["xT"], 1)

            def context_high(c, ph, f, i, dst):
                act.wait_ge(ph["tr"], ph.n("tr", 2 * i + f + 1))
                act.activation(c_hi[:, f, :], dst[:], ACT.Copy).then_inc(ph["ch"], 1)

            def cross(c, stage):
                a = CA[c.layer]
                if c.layer == 0:
                    act.wait_ge(a["w"], 48)
                    srcs = [w_raw[:, 1], w_raw[:, 2]]
                    for n, (src, hi) in enumerate(zip(srcs, (wk_hi, wv_hi))):
                        act.activation(hi, src, ACT.Copy).then_inc(a["w0"], 1)
                else:
                    for n in range(3):
                        act.wait_ge(a["wT"], n + 1)
                        pt = bank[n % 2]
                        if n == 0:
                            act.activation(w_raw[:, 0, 0, :], pt[:], ACT.Copy).then_inc(a["wTc"], 1)
                        else:
                            hi = (wk_hi, wv_hi)[n - 1]
                            act.activation(hi[:, :, 0:256], pt[:].rearrange("p (f n) -> p f n", f=2), ACT.Copy).then_inc(a["w0"], 1)
                for b in range(B):
                    m, t = MAXP[c.layer, b], ATT[c.layer, b]
                    for h0 in range(0, c.heads, c.hpg):
                        g = h0 // c.hpg
                        _, r = hidden_of(c, g)
                        act.wait_ge(m["qh"], m.n("qh", h0 + c.hpg))
                        if b == 1 and g == 0:
                            act.wait_ge(ATT[c.layer, 0]["s"], ATT[c.layer, 0].n("s", NCH * c.units))
                        for half in (0, 64):
                            act.activation(q_hh[half:half + 64, h0:h0 + c.hpg, :],
                                           q_hi[r:r + 64, h0:h0 + c.hpg, :].bitcast(F32), ACT.Copy).then_inc(m["qhh"], 1)
                    if b == 1:
                        act.wait_ge(ATT[c.layer, 0]["vp"], ATT[c.layer, 0].n("vp", KT * NCH))
                    def high(i):
                        act.wait_ge(m["kp"], m.n("kp", c.tiles * i))
                        for f in range(2):
                            context_high(c, m, f, i, bank[f])

                    def keep(i, tiles):
                        for n in tiles:
                            act.wait_ge(m["kp"], m.n("kp", c.tiles * i + n + 1))
                            act.wait_ge(m["s"], m.n("s", (c.tiles * i + n - 1) * c.hpt))
                            src = bank[2 + n % 2][:]
                            dst = Kst[c.layer][:, n, bass.ts(i, CHUNK)]
                            if c.layer == 0:
                                act.activation(dst, src, ACT.Copy)
                                act.activation(k_max[n % 2][:], src, ACT.Copy).then_inc(m["kev"], 1)
                            else:
                                act.activation(dst, src, ACT.Identity, bias=bias[:, 2 + n:3 + n])
                                act.activation(k_max[n % 2][:], src, ACT.Identity, bias=bias[:, 2 + n:3 + n]).then_inc(m["kev"], 1)

                    def chunk(i, last=False):
                        keep(i, range(1, c.tiles))
                        if not last:
                            high(i + 1)
                            keep(i + 1, range(1))

                    high(0)
                    keep(0, range(1))
                    with act.Fori(0, NCH - 1) as i:
                        chunk(i)
                    chunk(NCH - 1, last=True)
                    act.wait_ge(m["mt"], m.n("mt", 1))
                    act.activation(shift[0:2 * c.heads, :], bank[0][0:2 * c.heads, 0:128], ACT.Copy).then_inc(m["mr"], 1)
                    with act.Fori(0, NCH) as i:
                        for u in range(c.units):
                            n = i * c.units + u
                            act.wait_ge(t["s"], t.n("s", n + 1))
                            act.wait_ge(t["pfree"], t.n("pfree", n + 1))
                            if c.layer == 0:
                                act.wait_ge(t["acc"], t.n("acc", (n - 3) * KT))
                            act.activation(P[:, u % 4, :], score[u % 2][:], ACT.Exp).then_inc(t["p"], 1)
                            if u < 2:
                                if u == 0:
                                    act.wait_ge(t["vp"], t.n("vp", KT * i))
                                context_high(c, t, u, i, bank[2])
                    if c.layer == 1:
                        act.wait_ge(t["pfree"], t.n("pfree", NCH * c.units + 4))
                        for k in range(2):
                            act.activation(P[:, 0, 512 * k:512 * k + 512], bank[k][:], ACT.Copy).then_inc(t["osb"], 1)


            def local_attention():
                act.wait_ge(la["gt"], 2)
                act.activation(la_gate, bank[2][:, 0:128].rearrange("p (t h) -> p t h", t=TT), ACT.Sigmoid).then_inc(la["g"], 1)
                for t in range(TT):
                    keys, quads = 128 * la_keys[t], upto_t(la_quads, t)
                    act.wait_ge(la["m"], 2 * t + 2)
                    for h in range(NHL):
                        last = act.activation(la_S[:, h, 0:keys], la_S[:, h, 0:keys], ACT.Exp, bias=la_m[:, h:h + 1])
                    for h in range(NHG):
                        last = act.activation(la_LS[:, h, :], la_LS[:, h, :], ACT.Exp, bias=la_m[:, NHL + h:NHL + h + 1])
                    last.then_inc(la["e"], 1)
                    for n in range(1, la_quads[t], 2):
                        act.wait_ge(la["tr"], quads + n + 1)
                        dst = la_LPT if n == la_quads[t] - 1 else la_PT[:, 512 * n:512 * n + 512]
                        act.activation(dst, bank[2 + n % 2][:], ACT.Copy).then_inc(la["pta"], 1)

            def dense_mixture():
                act.wait_ge(gm["t"], 1)
                act.activation(tw[:, 1, :], tw[:, 0, :], ACT.Exp).then_inc(gm["ex"], 1)
                with act.Fori(0, E) as e:
                    act.wait_ge(em["w"], em.n("w", 32 * e + 32))
                    act.wait_ge(em["h"], em.n("h", FM * e))
                    act.activation(w1_hi, w1raw, ACT.Copy).then_inc(em["w1h"], 1)
                    act.wait_ge(em["y"], em.n("y", TT * e))
                    act.activation(w2_hi, w2raw, ACT.Copy).then_inc(em["w2h"], 1)
                    for m in range(FM):
                        act.wait_ge(em["h"], em.n("h", FM * e + m + 1))
                        act.wait_ge(em["hl"], em.n("hl", FM * e))
                        act.activation(h32[:, m, :], bank[m % 2][:], ACT.Gelu, bias=b1T[:, bass.ds(e * FM + m, 1)]).then_inc(em["g"], 1)

            def rwkv():
                act.wait_ge(rw["v"], 160)
                act.activation(rw_wexp, rw_vec[:, 0, :], ACT.Exp).then_inc(rw["we"], 1)
                act.wait_ge(rw["pj"], 6)
                for m in range(2):
                    act.activation(rw_sr[:, m].rearrange("p b t -> p (b t)"), bank[2 + m][:], ACT.Sigmoid).then_inc(rw["sr"], 1)
                act.wait_ge(rw["a"], 1)
                act.activation(rw_A[:], rw_A[:], ACT.Exp)
                act.activation(rw_Bc[:], rw_Bc[:], ACT.Exp)
                act.activation(rw_A2[:], rw_A2[:], ACT.Exp)
                act.activation(rw_B2[:], rw_B2[:], ACT.Exp).then_inc(rw["a2"], 1)

            def chunk_mixture():
                act.wait_ge(cm["t"], cm.n("t", 1))
                act.activation(tw[:, 1, :], tw[:, 0, :], ACT.Exp).then_inc(cm["ex"], 1)
                with act.Fori(0, E) as e:
                    for m in range(FM):
                        act.wait_ge(cm["h"], cm.n("h", FM * e + m + 1))
                        act.wait_ge(cm["y"], cm.n("y", e))
                        act.activation(hT[:, m, :], bank[m % 2][:, 0:128], ACT.Gelu).then_inc(cm["g"], 1)

            signal_ahead(act, "act")
            act.wait_ge(const_ready, 1)
            layer_norm(0)
            cross(X0, 0)
            stage_end(act, 1)
            if upto >= 2:
                layer_norm(1)
                local_attention()
                stage_end(act, 2)
            if upto >= 3:
                layer_norm(2)
                dense_mixture()
                stage_end(act, 3)
            if upto >= 4:
                layer_norm(3)
                cross(X1, 3)
                stage_end(act, 4)
            if upto >= 5:
                layer_norm(4)
                rwkv()
                stage_end(act, 5)
            if upto >= 6:
                layer_norm(5)
                chunk_mixture()
                stage_end(act, 6)

        @block.tensor
        def _(pe):
            mm = nc.tensor.matmul

            def layer_norm(n):
                ln = LN[n]
                pe.wait_ge(ln["xn"], ln.n("xn", TT))
                for f in range(2):
                    for t in range(TT):
                        last = nc.tensor.transpose(bank[f][:, 128 * t:128 * t + 128], xn[:, t, 128 * f:128 * f + 128], ident[:])
                last.then_inc(ln["tr"], 1)

            def turn_chunk(ph, f, i, dst):
                if f == 0:
                    pe.wait_ge(ph["ctx"], ph.n("ctx", 16 * i + 16))
                for k in range(KT):
                    last = nc.tensor.transpose(dst[:, 128 * k:128 * k + 128], c_in[:, k, 128 * f:128 * f + 128], ident[:])
                last.then_inc(ph["tr"], 1)

            def three(dst, pairs):
                for n, (l, r) in enumerate(pairs):
                    last = mm(dst, l, r, start=(n == 0), stop=(n == len(pairs) - 1))
                return last

            def cross(c, stage):
                a = CA[c.layer]
                if c.layer == 1:
                    pe.wait_ge(a["w"], 64)
                    pe.wait_ge(LN[3]["xT"], LN[3].n("xT", 2))
                    for n in range(3):
                        if n >= 2:
                            pe.wait_ge(a["wTc"], 1)
                        for f in range(2):
                            for o in range(2):
                                last = nc.tensor.transpose(bank[n % 2][:, 256 * f + 128 * o:256 * f + 128 * o + 128],
                                                           w_nat[:, n, o, 128 * f:128 * f + 128], ident[:])
                        last.then_inc(a["wT"], 1)
                else:
                    pe.wait_ge(a["w"], 48)
                    pe.wait_ge(LN[0]["xT"], LN[0].n("xT", 2))
                wq = w_raw[:, 0] if c.layer == 0 else w_raw[:, 0, 0, :].rearrange("p (f n) -> p f n", f=2)
                for n in range(c.tiles):
                    if n >= 2:
                        pe.wait_ge(a["q"], n - 1)
                    for f in range(2):
                        last = mm(bank[2 + n % 2][:], wq[:, f, 128 * n:128 * n + 128], xnT[:, f, :], start=(f == 0), stop=(f == 1))
                    last.then_inc(a["qp"], 1)
                if c.layer == 1:
                    pe.wait_ge(a["pad"], 2)
                    for k in range(4):
                        for o in range(2):
                            last = nc.tensor.transpose(score[0][:, 256 * k + 128 * o:256 * k + 128 * o + 128],
                                                       wo_pad[:, o, 128 * k:128 * k + 128], ident[:])
                    last.then_inc(a["wop"], 1)
                for b in range(B):
                    m, t = MAXP[c.layer, b], ATT[c.layer, b]
                    pe.sem_inc(m["s"], c.hpt)
                    pe.wait_ge(m["qh"], m.n("qh", c.heads))
                    if b == 0:
                        pe.wait_ge(a["whl"], 2)
                        pe.wait_ge(a["q"], c.tiles)
                        if c.layer == 1:
                            pe.wait_ge(a["wop"], 2)
                    if b == 1:
                        pe.wait_ge(ATT[c.layer, 0]["o"], ATT[c.layer, 0].n("o", 4))
                    def turn_both(i):
                        pe.wait_ge(m["cl"], m.n("cl", 2 * i))
                        turn_chunk(m, 0, i, bank[0])
                        turn_chunk(m, 1, i, bank[1])

                    def project(i, n):
                        if n == 0:
                            pe.wait_ge(m["cl"], m.n("cl", 2 * i + 2))
                        if n < 2:
                            pe.wait_ge(m["kev"], m.n("kev", c.tiles * i))
                        else:
                            pe.wait_ge(m["kev"], m.n("kev", c.tiles * i + n - 1))
                        cols = slice(128 * n, 128 * n + 128)
                        pairs = [(w[:, f, cols], v[:, f, :]) for f in range(2)
                                 for w, v in ((wk_hi, c_hi), (wk_hi, c_lo), (wk_lo, c_hi))]
                        three(bank[2 + n % 2][:], pairs).then_inc(m["kp"], 1)

                    def maxima(i, n, heads):
                        pe.wait_ge(m["kev"], m.n("kev", c.tiles * i + n + 1))
                        for j in heads:
                            h = n * c.hpt + j
                            if h >= 2:
                                pe.wait_ge(m["red"], m.n("red", i * c.heads + h - 1))
                            else:
                                pe.wait_ge(m["red"], m.n("red", i * c.heads))
                            for qt in range(2):
                                last = mm(score[h % 2][:, 512 * qt:512 * qt + 512], q_hi[:, h, 128 * qt:128 * qt + 128],
                                          k_max[n % 2][:], start=True, stop=True)
                            last.then_inc(m["s"], 1)

                    def chunk(i, last=False):
                        for n in range(1, c.tiles):
                            project(i, n)
                            maxima(i, n - 1, range(c.hpt))
                        if last:
                            maxima(i, c.tiles - 1, range(c.hpt))
                        else:
                            turn_both(i + 1)
                            maxima(i, c.tiles - 1, range(c.hpt - 1) if c.layer == 0 else range(c.hpt - 2))
                            project(i + 1, 0)
                            maxima(i, c.tiles - 1, range(c.hpt - 1, c.hpt) if c.layer == 0 else range(c.hpt - 2, c.hpt))

                    turn_both(0)
                    project(0, 0)
                    with pe.Fori(0, NCH - 1) as i:
                        chunk(i)
                    chunk(NCH - 1, last=True)
                    pe.wait_ge(m["m"], m.n("m", 1))
                    nc.tensor.transpose(bank[0][0:2 * c.heads, 0:128], mneg[:, 0:2 * c.heads], ident[:]).then_inc(m["mt"], 1)
                    pe.wait_ge(m["mr"], m.n("mr", 1))
                    pe.sem_inc(t["s"], c.upg)
                    pe.sem_inc(t["pfree"], 4)
                    for k in range(2):
                        for n in range(4):
                            mm(bank[k][:, 128 * n:128 * n + 128], zeros[:], zeros[:], start=(n == 0), stop=False, skip_group_check=True)
                    pe.wait_ge(m["md"], m.n("md", 16))
                    pe.wait_ge(m["ql"], m.n("ql", c.heads))
                    pe.wait_ge(m["qhh"], m.n("qhh", 2 * c.groups))
                    if c.layer == 1 and b == 0:
                        pe.wait_ge(t["z"], t.n("z", 1))
                    def weigh(i, u):
                        if c.layer == 0:
                            pe.wait_ge(t["p"], t.n("p", i * 8 + u + 2))
                            if u == 0:
                                pe.wait_ge(t["v"], t.n("v", KT * i + KT))
                            for k in range(KT):
                                for j in range(2):
                                    p = u // 2
                                    last = mm(bank[p // 2][64 * j:64 * j + 64, S * (p % 2):S * (p % 2) + S],
                                              V[:, k, 64 * (u + j):64 * (u + j) + 64], P[:, (u + j) % 4, S * k:S * k + S],
                                              start=False, stop=False, skip_group_check=True, tile_position=(0, 64 * j))
                            last.then_inc(t["pfree"], 2)
                        else:
                            g, k = u // KT, u % KT
                            pe.wait_ge(t["p"], t.n("p", i * 16 + u + 1))
                            pe.wait_ge(t["v"], t.n("v", KT * i + k + 1)) if u < 4 else None
                            for j in range(4):
                                last = mm(bank[g // 2][32 * j:32 * j + 32, S * (g % 2):S * (g % 2) + S],
                                          Vp[:, k, 4 * g + j, :], P[:, u % 4, S * j:S * j + S],
                                          start=False, stop=False, skip_group_check=True, tile_position=(0, 32 * j))
                            last.then_inc(t["pfree"], 1)

                    def chunk(i, first=False):
                        def turn(f):
                            pe.wait_ge(t["cl"], t.n("cl", 2 * i + f))
                            turn_chunk(t, f, i, bank[2])

                        def values(k):
                            if k == 0:
                                pe.wait_ge(t["cl"], t.n("cl", 2 * i + 2))
                            pe.wait_ge(t["v"], t.n("v", KT * i + k))
                            cols = slice(128 * k, 128 * k + 128)
                            pairs = [(v[:, f, cols], w[:, f, 0:c.hid]) for f in range(2)
                                     for v, w in ((c_hi, wv_hi), (c_hi, wv_lo), (c_lo, wv_hi))]
                            three(bank[3][:, 0:c.hid], pairs).then_inc(t["vp"], 1)

                        def scores(u):
                            g = u // c.upg
                            if u % c.upg == 0:
                                pe.wait_ge(t["kl"], t.n("kl", i * c.groups + g + 1))
                            if u >= 2:
                                pe.wait_ge(t["p"], t.n("p", i * c.units + u - 1))
                            else:
                                pe.wait_ge(t["s"], t.n("s", i * c.units))
                                if u == 0:
                                    pe.wait_ge(t["p"], t.n("p", i * c.units))
                            hl, h1 = k_hl[g % 2], k_h1[g % 2]
                            if c.layer == 0:
                                for k in range(KT):
                                    o = score[u % 2][:, S * k:S * k + S]
                                    cols = slice(128 * k, 128 * k + 128)
                                    mm(o, hl[:, cols], q_hh[:, g, :], start=True, stop=False)
                                    last = mm(o, h1[:, cols], q_lm[0:65, g, :], start=False, stop=True)
                            else:
                                cols = slice(128 * (u % KT), 128 * (u % KT) + 128)
                                for j in range(0, 4, 2):
                                    h = 4 * g + j
                                    o = score[u % 2][:, S * j:S * j + 2 * S]
                                    mm(o, hl[:, cols], q_hh[:, h:h + 2, :], start=True, stop=False)
                                    last = mm(o, h1[:, cols], q_lm[0:65, h:h + 2, :], start=False, stop=True)
                            last.then_inc(t["s"], 1)

                        extra = {0: [lambda: turn(0)], 1: [lambda: turn(1)], 2: [lambda: values(0), lambda: values(1)],
                                 3: [lambda: values(2), lambda: values(3)]}
                        for u in range(c.units):
                            scores(u)
                            if not first:
                                if c.layer == 0 and u == 1:
                                    weigh(i - 1, 6)
                                if c.layer == 1 and u < 3:
                                    weigh(i - 1, 13 + u)
                            for e in extra.get(u, ()):
                                e()
                            if c.layer == 0 and u in (3, 5, 7) or c.layer == 1 and u >= 3:
                                weigh(i, u - 3)

                    chunk(0, first=True)
                    with pe.Fori(1, NCH) as i:
                        chunk(i)
                    for u in ((6,) if c.layer == 0 else (13, 14, 15)):
                        weigh(NCH - 1, u)
                    pe.wait_ge(t["p"], t.n("p", NCH * c.units))
                    if c.layer == 0:
                        pe.wait_ge(t["acc"], t.n("acc", NCH * 8 * KT))
                        for h in range(8):
                            p, j = h // 2, h % 2
                            last = mm(score[0][64 * j:64 * j + 64, S * p:S * p + S], ones[:, 0:64], acc_p[:, h, :],
                                      start=True, stop=True, tile_position=(0, 64 * j))
                        last.then_inc(t["d"], 1)
                    else:
                        pe.wait_ge(t["osb"], t.n("osb", 2))
                        for k in range(2):
                            last = mm(score[0][:, 512 * k:512 * k + 512], den_pick[:], P[:, 0, 512 * k:512 * k + 512], start=True, stop=True)
                        last.then_inc(t["d"], 1)
                if c.layer == 0:
                    pe.wait_ge(a["wo"], 16)
                pe.wait_ge(a["bias"], 16 if c.layer == 0 else 16 * 21)
                pe.wait_ge(ATT[c.layer, 1]["o"], ATT[c.layer, 1].n("o", 4))
                for n in range(TT):
                    if n >= 2:
                        pe.wait_ge(a["res"], n - 1)
                    for k in range(4):
                        mm(bank[2 + n % 2][:, 0:D], oT[:, k, 128 * n:128 * n + 128], wout[:, k, :], start=(k == 0), stop=False)
                    mm(bank[2 + n % 2][:, 0:D], ones[0:1, :], row[0:1, 0:D], start=False, stop=True).then_inc(a["op"], 1)


            def local_attention():
                pe.wait_ge(la["w"], 192)
                step = [0]

                def project(pairs, out=None):
                    n = step[0]
                    if n >= 2:
                        pe.wait_ge(la["pe"], n - 1)
                    dst = bank[2 + n % 2][:] if out is None else out
                    width = pairs[0][1].free_size()
                    for k, (l, r) in enumerate(pairs):
                        last = mm(bank[2 + n % 2][:, 0:width], l, r, start=(k == 0), stop=(k == len(pairs) - 1))
                    last.then_inc(la["pj"], 1)
                    step[0] += 1

                pe.wait_ge(LN[1]["xT"], LN[1].n("xT", 2))
                for w in (0, 1):
                    for m in range(2):
                        project([(la_wqkv[:, w, f, 128 * m:128 * m + 128], xnT[:, f, :]) for f in range(2)])
                project([(la_wg[:, 0, f, :], xnT[:, f, :]) for f in range(2)])
                for t in range(TT):
                    project([(xnT[:, f, 128 * t:128 * t + 128], la_wqkv[:, 2, f, :]) for f in range(2)])
                pe.wait_ge(la["g"], 1)
                for b in range(B):
                    project([(la_wg[:, 1, f, :], la_xp[:, f, b, 0, :]) for f in range(2)])
                for b in range(B):
                    project([(la_xp[:, f, b].rearrange("p c n -> p (c n)"), la_wg[:, 2, f, :]) for f in range(2)])
                pe.wait_ge(la["pe"], 13)
                pe.wait_ge(la["gt"], 1)
                for t in range(TT):
                    for f in range(2):
                        last = mm(bank[2][:, 32 * t:32 * t + 32], la_QT[:, f, 128 * t:128 * t + 128], la_G[:, f, :],
                                  start=(f == 0), stop=(f == 1))
                last.then_inc(la["gt"], 1)
                pe.wait_ge(la["g"], 2)
                bufs = quads = 0
                for t in range(TT):
                    b, keys = t // 2, 128 * la_keys[t]
                    pe.wait_ge(la["qp"], t + 1)
                    hpb = 1024 // keys
                    for n in range(la_bufs[t]):
                        if bufs >= 2:
                            pe.wait_ge(la["sb"], bufs - 1)
                        for h in range(hpb):
                            hh = n * hpb + h
                            last = mm(score[bufs % 2][:, keys * h:keys * h + keys], la_q[:, hh, :],
                                      la_KT[:, hh // 8, b * S:b * S + keys], start=True, stop=True)
                        last.then_inc(la["s"], 1)
                        bufs += 1
                    if t:
                        pe.wait_ge(la["res"], t)
                    for h in range(NHG):
                        last = mm(bank[1][:, LAT * h:LAT * h + LAT], la_gq[:, h, :], la_GKT[:, b * LAT:b * LAT + LAT], start=True, stop=True)
                    last.then_inc(la["o"], 1)
                    pe.wait_ge(la["e"], t + 1)
                    taken = (sum((q + 1) // 2 for q in la_quads[:t]), sum(q // 2 for q in la_quads[:t]))
                    for n in range(la_quads[t]):
                        pe.wait_ge(la["pta" if n % 2 else "ptd"], taken[n % 2] + n // 2)
                        for k in range(4):
                            if n < la_quads[t] - 1:
                                blk = 4 * n + k
                                src = la_S[:, blk // la_keys[t], 128 * (blk % la_keys[t]):128 * (blk % la_keys[t]) + 128]
                            else:
                                src = la_LS[:, 2 * k:2 * k + 2, :].rearrange("p h n -> p (h n)")
                            last = nc.tensor.transpose(bank[2 + n % 2][:, 128 * k:128 * k + 128], src, ident[:])
                        last.then_inc(la["tr"], 1)
                        quads += 1
                    pe.wait_ge(la["ptd"], taken[0] + (la_quads[t] + 1) // 2)
                    pe.wait_ge(la["pta"], taken[1] + la_quads[t] // 2)
                    nk = la_keys[t]
                    for h in range(NHL):
                        for k in range(nk):
                            blk = h * nk + k
                            mm(bank[0][:, 17 * h:17 * h + 17], la_PT[:, 128 * blk:128 * blk + 128], la_V[:, 2 * b + k, h, :],
                               start=(k == 0), stop=(k == nk - 1))
                    for h in range(0, NHG, 2):
                        last = mm(bank[0][:, 272 + 17 * h:306 + 17 * h], la_LPT[:, 64 * h:64 * h + 128],
                                  la_GV[:, b, h:h + 2, :].rearrange("p h d -> p (h d)"), start=True, stop=True)
                    last.then_inc(la["o"], 1)
                    pe.wait_ge(la["rq"], t + 1)
                    nc.tensor.transpose(bank[1][:, 0:128], la_rq, ident[:]).then_inc(la["rt"], 1)
                    pe.wait_ge(la["rtc"], t + 1)
                    mm(bank[1][:, 256:512], la_rqT, la_rout, start=True, stop=True).then_inc(la["rem"], 1)
                    pe.wait_ge(la["cb"], t + 1)
                    for f in range(2):
                        last = nc.tensor.transpose(bank[1][:, 128 * f:128 * f + 128], la_cb[:, 128 * f:128 * f + 128], ident[:])
                    last.then_inc(la["ct"], 1)
                    pe.wait_ge(la["ctc"], t + 1)
                    for f in range(2):
                        last = mm(bank[1][:, 256:512], la_cT[:, 128 * f:128 * f + 128], la_wout[:, f, :], start=(f == 0), stop=(f == 1))
                    last.then_inc(la["out"], 1)

            def logits(g, n, w):
                pe.wait_ge(LN[n]["xT"], LN[n].n("xT", 2))
                for t in range(TT):
                    for f in range(2):
                        last = mm(bank[2][:, E * t:E * t + E], xnT[:, f, 128 * t:128 * t + 128], w[:, f, :], start=(f == 0), stop=(f == 1))
                last.then_inc(g["lp"], 1)

            def dense_mixture():
                pe.wait_ge(gm["w"], 48)
                logits(gm, 2, gate_w)
                nc.tensor.transpose(bank[3][:, 0:64], b1n, ident[0:64, 0:64]).then_inc(gm["bt"], 1)
                pe.wait_ge(gm["cT"], 1)
                for t in range(TT):
                    last = nc.tensor.transpose(bank[2][0:8, 128 * t:128 * t + 128], comb[:, t, :], ident[:])
                last.then_inc(gm["cTc"], 1)
                pe.wait_ge(gm["b2"], 1)
                for t in range(TT):
                    last = mm(score[0][:, D * t:D * t + D], combT[:, 128 * t:128 * t + 128], b2sb, start=True, stop=True)
                last.then_inc(gm["done"], 1)
                pe.wait_ge(gm["done"], 2)
                with pe.Fori(0, E) as e:
                    pe.wait_ge(em["w1l"], em.n("w1l", e + 1))
                    for m in range(FM):
                        if m < 2:
                            pe.wait_ge(em["g"], em.n("g", FM * e))
                        else:
                            pe.wait_ge(em["g"], em.n("g", FM * e + m - 1))
                        cols = slice(128 * m, 128 * m + 128)
                        three(bank[m % 2][:], [(w[:, f, cols], r[:, f, :]) for f in range(2)
                                               for w, r in ((w1_hi, c_hi), (w1_hi, c_lo), (w1_lo, c_hi))]).then_inc(em["h"], 1)
                    pe.wait_ge(em["hl"], em.n("hl", FM * e + FM))
                    pe.wait_ge(em["w2l"], em.n("w2l", e + 1))
                    for t in range(TT):
                        if t < 2:
                            pe.wait_ge(em["acc"], em.n("acc", TT * e))
                        else:
                            pe.wait_ge(em["acc"], em.n("acc", TT * e + t - 1))
                        cols = slice(128 * t, 128 * t + 128)
                        three(bank[2 + t % 2][:, 0:D], [(h[:, k, cols], w[:, k, :]) for k in range(FM)
                                                        for h, w in ((h_hi, w2_hi), (h_hi, w2_lo), (h_lo, w2_hi))]).then_inc(em["y"], 1)

            def rwkv():
                pe.wait_ge(rw["w"], 64)
                pe.wait_ge(LN[4]["xT"], LN[4].n("xT", 2))
                for n in range(4):
                    if n >= 2:
                        pe.wait_ge(rw["trc"], n - 1)
                    for f in range(2):
                        for o in range(2):
                            last = nc.tensor.transpose(bank[n % 2][:, 256 * f + 128 * o:256 * f + 128 * o + 128],
                                                       rw_nat[:, n, o, 128 * f:128 * f + 128], ident[:])
                    last.then_inc(rw["tr"], 1)
                pe.wait_ge(rw["trc"], 4)
                for n, (w, src) in enumerate(((0, rw_xk), (1, rw_xv), (2, rw_xr))):
                    pe.wait_ge(rw["mx"], n + 1)
                    for m in range(2):
                        dst = (score[0][:, 512 * m:512 * m + 512], score[1][:, 512 * m:512 * m + 512], bank[2 + m][:])[n]
                        for f in range(2):
                            last = mm(dst, rw_W[:, w, f, 128 * m:128 * m + 128], src[:, f].rearrange("p b t -> p (b t)"),
                                      start=(f == 0), stop=(f == 1))
                        last.then_inc(rw["pj"], 1)
                pe.wait_ge(rw["o"], 1)
                for t in range(TT):
                    if t >= 2:
                        pe.wait_ge(rw["res"], t - 1)
                    b, u = t // 2, t % 2
                    for f in range(2):
                        last = mm(bank[t % 2][:, 0:D], rw_out[:, f, b, 128 * u:128 * u + 128], rw_W[:, 3, f, :], start=(f == 0), stop=(f == 1))
                    last.then_inc(rw["out"], 1)

            def chunk_mixture():
                pe.wait_ge(cm["wr"], cm.n("wr", 16))
                pe.wait_ge(LN[5]["xT"], LN[5].n("xT", 2))
                for f in range(2):
                    last = nc.tensor.transpose(bank[3][:, 8 * f:8 * f + 8], wr_nat[:, 128 * f:128 * f + 128], ident[0:8, 0:8])
                last.then_inc(cm["tr"], 1)
                pe.wait_ge(cm["trc"], cm.n("trc", 1))
                logits(cm, 5, gate_w)
                pe.wait_ge(cm["c"], cm.n("c", 1))
                pe.wait_ge(cm["iota"], cm.n("iota", 1))
                for t in range(TT):
                    for k in range(t + 1):
                        mm(bank[3][:, 8 * t:8 * t + 8], ones[:] if k < t else before, comb[:, k, :], start=(k == 0), stop=(k == t))
                for k in range(TT):
                    last = mm(bank[3][:, 32:40], ones[:], comb[:, k, :], start=(k == 0), stop=(k == TT - 1))
                last.then_inc(cm["c"], 1)
                pe.wait_ge(cm["pw"], cm.n("pw", TT))
                for n in range(4):
                    f, half = n // 2, n % 2
                    for t in range(TT):
                        last = mm(score[n // 2][:, 512 * half:512 * half + 512], xn[:, t, 128 * f:128 * f + 128],
                                  PA[:, t, 512 * half:512 * half + 512], start=(t == 0), stop=(t == TT - 1))
                    last.then_inc(cm["pm"], 1)
                for e in range(E):
                    pe.wait_ge(cm["trc"], cm.n("trc", e))
                    for t in range(TT):
                        last = nc.tensor.transpose(bank[2 + e % 2][:, 128 * t:128 * t + 128], PW[:, t, 128 * e:128 * e + 128], ident[:])
                    last.then_inc(cm["tr"], 1)
                pe.wait_ge(cm["trc"], cm.n("trc", 1 + E))
                pe.wait_ge(cm["pmc"], cm.n("pmc", 4))
                with pe.Fori(0, E) as e:
                    pe.wait_ge(cm["w"], cm.n("w", 16 * e + 16))
                    for m in range(FM):
                        if m < 2:
                            pe.wait_ge(cm["g"], cm.n("g", FM * e))
                        else:
                            pe.wait_ge(cm["g"], cm.n("g", FM * e + m - 1))
                        for f in range(2):
                            last = mm(bank[m % 2][:, 0:128], cw1[:, f, 128 * m:128 * m + 128], permT[:, f, bass.ts(e, 128)],
                                      start=(f == 0), stop=(f == 1))
                        last.then_inc(cm["h"], 1)
                    pe.wait_ge(cm["g"], cm.n("g", FM * e + FM))
                    pe.wait_ge(cm["w2"], cm.n("w2", 16 * e + 16))
                    pe.wait_ge(cm["yc"], cm.n("yc", e))
                    for k in range(FM):
                        last = mm(bank[2][:, 0:D], hT[:, k, :], cw2[:, k, :], start=(k == 0), stop=(k == FM - 1))
                    last.then_inc(cm["y"], 1)
                pe.wait_ge(cm["yc"], cm.n("yc", E))
                for t in range(TT):
                    if t >= 2:
                        pe.wait_ge(cm["res"], cm.n("res", t - 1))
                    for e in range(E):
                        last = mm(bank[t % 2][:, 0:D], PWT[:, e, 128 * t:128 * t + 128], yS[:, e, :], start=(e == 0), stop=(e == E - 1))
                    last.then_inc(cm["s"], 1)

            signal_ahead(pe, "pe")
            pe.wait_ge(const_ready, 1)
            layer_norm(0)
            cross(X0, 0)
            stage_end(pe, 1)
            if upto >= 2:
                layer_norm(1)
                local_attention()
                stage_end(pe, 2)
            if upto >= 3:
                layer_norm(2)
                dense_mixture()
                stage_end(pe, 3)
            if upto >= 4:
                layer_norm(3)
                cross(X1, 3)
                stage_end(pe, 4)
            if upto >= 5:
                layer_norm(4)
                rwkv()
                stage_end(pe, 5)
            if upto >= 6:
                layer_norm(5)
                chunk_mixture()
                stage_end(pe, 6)

        @block.vector
        def _(dve):
            v = nc.vector
            chain = [0]

            def link(i):
                chain[0] += 1
                i.then_inc(dve_chain, 1)
                dve.wait_ge(dve_chain, chain[0])

            def layer_norm(n):
                ln = LN[n]
                for t in range(TT):
                    last = v.bn_stats(stats[:, t, :], x[:, t, :])
                link(last)
                for t in range(TT):
                    last = v.bn_aggr(mv[:, t, :], stats[:, t, :])
                link(last)
                v.tensor_scalar(mv[:, :, 1], mv[:, :, 1], EPS, None, ALU.add).then_inc(ln["var"], 1)
                dve.wait_ge(ln["std"], ln.n("std", 1))
                link(v.reciprocal(rstd[:], rstd[:]))
                for t in range(TT):
                    v.tensor_scalar(xn[:, t, :], x[:, t, :], mv[:, t, 0:1], rstd[:, t:t + 1], ALU.subtract, ALU.mult).then_inc(ln["xn"], 1)
                dve.wait_ge(ln["tr"], ln.n("tr", 1))
                v.tensor_copy(xnT[:, 1, :], bank[1][:]).then_inc(ln["xT"], 1)
                dve.wait_ge(ln["xT"], ln.n("xT", 2))

            def context_low(ph, f, i, src):
                dve.wait_ge(ph["ch"], ph.n("ch", 2 * i + f + 1))
                v.tensor_tensor(c_lo[:, f, :], src[:], c_hi[:, f, :].bitcast(F32), ALU.subtract).then_inc(ph["cl"], 1)

            def cross(c, stage):
                a = CA[c.layer]
                if c.layer == 0:
                    for n, (hi, lo) in enumerate(((wk_hi, wk_lo), (wv_hi, wv_lo))):
                        dve.wait_ge(a["w0"], n + 1)
                        v.tensor_tensor(lo, w_raw[:, n + 1], hi.bitcast(F32), ALU.subtract).then_inc(a["whl"], 1)
                else:
                    link(v.memset(bias[:, 4:8], 0.0))
                    v.engine_nop().then_inc(a["pad"], 1)
                    link(v.memset(wo_pad, 0.0))
                    dve.wait_ge(a["w"], 64)
                    for o in range(2):
                        last = v.tensor_copy(wo_pad[:, o, :].rearrange("p (h d) -> p h d", d=32)[:, :, 0:16],
                                             wo_nat[:, o, :].rearrange("p (h d) -> p h d", d=16))
                    last.then_inc(a["pad"], 1)
                    for n, (hi, lo) in enumerate(((wk_hi, wk_lo), (wv_hi, wv_lo))):
                        dve.wait_ge(a["w0"], n + 1)
                        v.tensor_tensor(lo[:, :, 0:256], bank[(n + 1) % 2][:].rearrange("p (f n) -> p f n", f=2),
                                        hi[:, :, 0:256].bitcast(F32), ALU.subtract).then_inc(a["whl"], 1)
                    dve.wait_ge(a["bias"], 16 * 21)
                for n in range(c.tiles):
                    dve.wait_ge(a["qp"], n + 1)
                    if c.layer == 0:
                        v.tensor_scalar(qT[:, n, :], bank[2 + n % 2][:], c.scale, None, ALU.mult).then_inc(a["q"], 1)
                    else:
                        v.tensor_scalar(qT[:, 2 + n, :], bank[2 + n % 2][:], bias[:, n:n + 1], c.scale, ALU.add, ALU.mult).then_inc(a["q"], 1)
                dve.wait_ge(a["q"], c.tiles)
                if c.layer == 1:
                    dve.wait_ge(a["wop"], 1)
                    v.tensor_copy(wout, score[0][:].rearrange("p (k n) -> p k n", k=4)).then_inc(a["wop"], 1)
                mask = mask_half if c.layer == 0 else mask_16th
                qt0 = 0 if c.layer == 0 else 2
                for b in range(B):
                    m, t = MAXP[c.layer, b], ATT[c.layer, b]
                    toks = slice(b * S, b * S + S)
                    for h in range(c.heads):
                        v.tensor_scalar(q_hi[:, h, :], qT[:, qt0 + h // c.hpt, toks], mask[:, h % c.hpt:h % c.hpt + 1], None,
                                        ALU.mult).then_inc(m["qh"], 1)
                    dve.wait_ge(m["qh"], m.n("qh", c.heads))
                    for h in range(c.heads):
                        _, r = hidden_of(c, h // c.hpg)
                        v.scalar_tensor_tensor(out=q_lm[0:64, h, :], in0=qT[r:r + 64, qt0 + h // c.hpt, toks],
                                               scalar=mask[r:r + 64, h % c.hpt:h % c.hpt + 1], in1=q_hi[r:r + 64, h, :].bitcast(F32),
                                               op0=ALU.mult, op1=ALU.subtract).then_inc(m["ql"], 1)
                    def reduce(i, heads):
                        for h in heads:
                            dve.wait_ge(m["s"], m.n("s", i * c.heads + h + 1))
                            v.tensor_reduce(mx[:, bass.ds(i, 1), 2 * h:2 * h + 2], score[h % 2][:].rearrange("p (q k) -> p q k", q=2),
                                            AX.X, ALU.max).then_inc(m["red"], 1)
                    def low_both(i):
                        for f in range(2):
                            context_low(m, f, i, bank[f])

                    low_both(0)
                    ahead_of = c.heads - 3
                    with dve.Fori(0, NCH - 1) as i:
                        reduce(i, range(ahead_of))
                        low_both(i + 1)
                        reduce(i, range(ahead_of, c.heads))
                    reduce(NCH - 1, range(c.heads))
                    dve.wait_ge(m["red"], m.n("red", NCH * c.heads))
                    v.tensor_reduce(mneg[:, 0:2 * c.heads], mx[:, :, 0:2 * c.heads].rearrange("p c h -> p h c"), AX.X, ALU.max,
                                    negate=True).then_inc(m["m"], 1)
                    with dve.Fori(0, NCH) as i:
                        def split(g):
                            n = i * c.groups + g
                            tile, r = hidden_of(c, g)
                            src = Kst[c.layer][r:r + 64, tile, bass.ts(i, CHUNK)]
                            dve.wait_ge(t["s"], t.n("s", (n - 1) * c.upg))
                            v.tensor_copy(k_hl[g % 2][r:r + 64, :], src).then_inc(t["khi"], 1)
                            v.tensor_copy(k_h1[g % 2][0:64, :], src)
                            dve.wait_ge(t["khi"], t.n("khi", n + 1))
                            v.tensor_tensor(k_hl[g % 2][64 - r:128 - r, :], src, k_hl[g % 2][r:r + 64, :].bitcast(F32),
                                            ALU.subtract).then_inc(t["kl"], 1)

                        def values(k):
                            dve.wait_ge(t["vp"], t.n("vp", KT * i + k + 1))
                            if k == 0:
                                dve.wait_ge(t["pfree"], t.n("pfree", c.units * i + 4))
                            if c.layer == 0:
                                v.tensor_copy(V[:, k, :], bank[3][:]).then_inc(t["v"], 1)
                            else:
                                v.tensor_copy(Vp[:, k, :, 0:16], bank[3][:, 0:256].rearrange("p (h d) -> p h d", h=16)).then_inc(t["v"], 1)

                        low = lambda f: context_low(t, f, i, bank[2])
                        if c.layer == 0:
                            split(0), split(1), low(0), split(2), low(1), split(3), values(0), values(1)
                            split(4), values(2), split(5), values(3), split(6), split(7)
                        else:
                            split(0), low(0), low(1), split(1)
                            for k in range(KT):
                                values(k)
                            split(2), split(3)
                    dve.wait_ge(t["d"], t.n("d", 1))
                    dve.wait_ge(t["pfree"], t.n("pfree", NCH * c.units + 4))
                    if c.layer == 0:
                        v.reciprocal(P[:, 1, :], score[0][:]).then_inc(t["rd"], 1)
                        dve.wait_ge(t["rd"], t.n("rd", 1))
                        for k in range(4):
                            v.tensor_tensor(oT[:, k, toks], bank[k // 2][:, S * (k % 2):S * (k % 2) + S], P[:, 1, S * k:S * k + S],
                                            ALU.mult).then_inc(t["o"], 1)
                    else:
                        v.reciprocal(P[:, 1, :], score[0][:]).then_inc(t["rd"], 1)
                        dve.wait_ge(t["rd"], t.n("rd", 1))
                        for k in range(4):
                            link(v.tensor_tensor(oT[:, k, toks], bank[k // 2][:, S * (k % 2):S * (k % 2) + S], P[:, 1, S * k:S * k + S],
                                                 ALU.mult))
                            v.tensor_scalar(oT[:, k, toks], oT[:, k, toks], bias[:, 4 + k:5 + k], None, ALU.add).then_inc(t["o"], 1)
                for n in range(TT):
                    dve.wait_ge(a["op"], n + 1)
                    v.tensor_tensor(x[:, n, :], bank[2 + n % 2][:, 0:D], x[:, n, :], ALU.add).then_inc(a["res"], 1)


            def local_attention():
                link(v.tensor_reduce(la_xs, xnT.rearrange("p f (n g) -> p f n g", g=GRP), AX.X, ALU.add))
                for c in range(2):
                    last = v.tensor_scalar(la_xp[:, :, :, c, :], la_xs.rearrange("p f (b n) -> p f b n", b=B), 1.0 / GRP, None, ALU.mult)
                last.then_inc(la["g"], 1)
                dve.wait_ge(la["w"], 192)
                link(v.memset(la_G, 0.0))
                for f in range(2):
                    for w in range(2):
                        last = v.tensor_scalar(la_G[:, f, 16 * w + 8 * f:16 * w + 8 * f + 8], mask_16th[:], la_gcol[:, f, w:w + 1], None, ALU.mult)
                last.then_inc(la["gt"], 1)
                dsts = [(la_QT[:, 0, :], 512), (la_QT[:, 1, :], 512), (la_KT[:, 0, :], 512), (la_KT[:, 1, :], 512), (la_GQT, 512)]
                dsts += [(la_V[:, t, :, 0:HD], 256) for t in range(TT)]
                dsts += [(la_GKT[:, 64 * b:64 * b + 64], 64) for b in range(B)]
                dsts += [(la_GV[:, b, :, 0:HD], 128) for b in range(B)]
                dve.wait_ge(la["msk"], 1)
                for n, (dst, width) in enumerate(dsts):
                    dve.wait_ge(la["pj"], n + 1)
                    src = bank[2 + n % 2][:, 0:width]
                    if n in (5, 6, 7, 8, 11, 12):
                        src = src.rearrange("p (h d) -> p h d", d=HD)
                    if n < 11:
                        last = v.tensor_copy(dst, src)
                    else:
                        for r in (0, 1):
                            last = v.tensor_copy(dst[64 * r:64 * r + 64, r::2, :], src[64 * r:64 * r + 64, r::2, :])
                    last.then_inc(la["pe"], 1)
                dve.wait_ge(la["pe"], 13)
                bufs = quads = 0
                for t in range(TT):
                    b, u, keys, nk = t // 2, t % 2, 128 * la_keys[t], la_keys[t]
                    if t:
                        dve.wait_ge(la["o"], 2 * t)
                    for h in range(NHL):
                        v.tensor_scalar(la_q[:, h, :], la_QT[:, h // 8, 128 * t:128 * t + 128], mask_16th[:, h % 8:h % 8 + 1], None, ALU.mult)
                    for h in range(NHG):
                        last = v.tensor_scalar(la_gq[:, h, :], la_GQT[:, 128 * t:128 * t + 128], mask_16th[:, h:h + 1], None, ALU.mult)
                    last.then_inc(la["qp"], 1)
                    hpb = 1024 // keys
                    for n in range(la_bufs[t]):
                        dve.wait_ge(la["s"], bufs + 1)
                        v.scalar_tensor_tensor(out=la_S[:, n * hpb:n * hpb + hpb, 0:keys],
                                               in0=score[bufs % 2][:].rearrange("p (h k) -> p h k", h=hpb), scalar=HD ** -0.5,
                                               in1=bc(la_mask[:, 256 - keys:256], 1, hpb), op0=ALU.mult, op1=ALU.add).then_inc(la["sb"], 1)
                        bufs += 1
                    dve.wait_ge(la["sb"], bufs)
                    v.tensor_reduce(la_m[:, 0:NHL], la_S[:, :, 0:keys], AX.X, ALU.max, negate=True).then_inc(la["m"], 1)
                    dve.wait_ge(la["o"], 2 * t + 1)
                    link(v.scalar_tensor_tensor(out=la_LS, in0=bank[1][:].rearrange("p (h n) -> p h n", h=NHG), scalar=HD ** -0.5,
                                                in1=bc(la_lmask[:, u, :], 1, NHG), op0=ALU.mult, op1=ALU.add))
                    v.tensor_reduce(la_m[:, NHL:], la_LS, AX.X, ALU.max, negate=True).then_inc(la["m"], 1)
                    for n in range(0, la_quads[t], 2):
                        dve.wait_ge(la["tr"], quads + n + 1)
                        dst = la_LPT if n == la_quads[t] - 1 else la_PT[:, 512 * n:512 * n + 512]
                        v.tensor_copy(dst, bank[2 + n % 2][:]).then_inc(la["ptd"], 1)
                    quads += la_quads[t]
                    dve.wait_ge(la["o"], 2 * t + 2)
                    if t == 0:
                        dve.wait_ge(la["g"], 2)
                    O = bank[0][:, 0:408].rearrange("p (h d) -> p h d", d=17)
                    link(v.reciprocal(la_r, O[:, :, 16]))
                    v.tensor_tensor(la_rq.rearrange("p (h d) -> p h d", d=HD), O[:, NHL:, 0:HD], bc(la_r[:, NHL:], 2, HD), ALU.mult).then_inc(la["rq"], 1)
                    link(v.tensor_tensor(la_rs, la_r[:, 0:NHL], la_gate[:, t, 0:NHL], ALU.mult))
                    link(v.tensor_tensor(la_cb.rearrange("p (h d) -> p h d", d=HD), O[:, 0:NHL, 0:HD], bc(la_rs, 2, HD), ALU.mult))
                    dve.wait_ge(la["rt"], t + 1)
                    v.tensor_copy(la_rqT, bank[1][:, 0:128]).then_inc(la["rtc"], 1)
                    dve.wait_ge(la["rem"], t + 1)
                    rem = P[:, 3, 256:512].rearrange("p (h d) -> p h d", d=HD)
                    link(v.tensor_tensor(rem, bank[1][:, 256:512].rearrange("p (h d) -> p h d", d=HD), bc(la_gate[:, t, NHL:], 2, HD), ALU.mult))
                    v.tensor_tensor(la_cb, la_cb, P[:, 3, 256:512], ALU.add).then_inc(la["cb"], 1)
                    dve.wait_ge(la["ct"], t + 1)
                    v.tensor_copy(la_cT, bank[1][:, 0:256]).then_inc(la["ctc"], 1)
                    dve.wait_ge(la["out"], t + 1)
                    v.tensor_tensor(x[:, t, :], bank[1][:, 256:512], x[:, t, :], ALU.add).then_inc(la["res"], 1)

            def top_two(g):
                dve.wait_ge(g["lp"], 1)
                link(v.tensor_copy(lg, bank[2][:, 0:E * TT].rearrange("p (t e) -> p t e", t=TT)))
                for t in range(TT):
                    last = v.max(top8[:, t, :], lg[:, t, :])
                link(last)
                for t in range(TT):
                    last = v.max_index(idx8[:, t, :], top8[:, t, :], lg[:, t, :])
                link(last)
                link(v.tensor_copy(idxf, idx8))
                v.tensor_tensor(tw[:, 0, :], top8[:, :, 1], top8[:, :, 0], ALU.subtract).then_inc(g["t"], 1)
                dve.wait_ge(g["ex"], 1)
                link(v.tensor_scalar(tw[:, 0, :], tw[:, 1, :], 1.0, None, ALU.add))
                link(v.reciprocal(tw[:, 0, :], tw[:, 0, :]))
                link(v.tensor_tensor(tw[:, 1, :], tw[:, 0, :], tw[:, 1, :], ALU.mult))

            def dense_mixture():
                dve.wait_ge(gm["bt"], 1)
                v.tensor_copy(b1T, bank[3][:, 0:64]).then_inc(gm["btc"], 1)
                for f in range(2):
                    last = v.tensor_copy(c_hi[:, f, :], xnT[:, f, :])
                link(last)
                last = v.tensor_tensor(c_lo[:], xnT, c_hi[:].bitcast(F32), ALU.subtract)
                link(last)
                top_two(gm)
                for t in range(TT):
                    for k in range(2):
                        last = v.tensor_scalar(ohtmp[:, k, t, :], iota8[:], idxf[:, t, k:k + 1], tw[:, k, t:t + 1], ALU.is_equal, ALU.mult)
                link(last)
                v.tensor_tensor(comb, ohtmp[:, 0], ohtmp[:, 1], ALU.add).then_inc(gm["cT"], 1)
                dve.wait_ge(gm["cTc"], 1)
                v.tensor_copy(combT, bank[2][0:8, :]).then_inc(gm["b2"], 1)
                dve.wait_ge(gm["done"], 1)
                v.tensor_tensor(x[:], score[0][:].rearrange("p (t d) -> p t d", t=TT), x[:], ALU.add).then_inc(gm["done"], 1)
                dve.wait_ge(gm["done"], 2)
                with dve.Fori(0, E) as e:
                    dve.wait_ge(em["w1h"], em.n("w1h", e + 1))
                    v.tensor_tensor(w1_lo, w1raw, w1_hi.bitcast(F32), ALU.subtract).then_inc(em["w1l"], 1)
                    dve.wait_ge(em["w2h"], em.n("w2h", e + 1))
                    v.tensor_tensor(w2_lo, w2raw, w2_hi.bitcast(F32), ALU.subtract).then_inc(em["w2l"], 1)
                    dve.wait_ge(em["y"], em.n("y", TT * e))
                    for m in range(FM):
                        dve.wait_ge(em["g"], em.n("g", FM * e + m + 1))
                        v.tensor_copy(h_hi[:, m, :], h32[:, m, :]).then_inc(em["hh"], 1)
                        dve.wait_ge(em["hh"], em.n("hh", FM * e + m + 1))
                        v.tensor_tensor(h_lo[:, m, :], h32[:, m, :], h_hi[:, m, :].bitcast(F32), ALU.subtract).then_inc(em["hl"], 1)
                    for t in range(TT):
                        dve.wait_ge(em["y"], em.n("y", TT * e + t + 1))
                        dve.wait_ge(em["acc"], em.n("acc", TT * e))
                        v.scalar_tensor_tensor(out=x[:, t, :], in0=bank[2 + t % 2][:, 0:D], scalar=comb[:, t, bass.ds(e, 1)],
                                               in1=x[:, t, :], op0=ALU.mult, op1=ALU.add).then_inc(em["acc"], 1)

            def rwkv():
                full = lambda a: a.rearrange("p m b t -> p (m b t)")
                for n in range(4):
                    dve.wait_ge(rw["tr"], n + 1)
                    v.tensor_copy(rw_W[:, n], bank[n % 2][:].rearrange("p (f n) -> p f n", f=2)).then_inc(rw["trc"], 1)
                xt = xnT.rearrange("p f (b t) -> p f b t", b=B)
                v.memset(rw_xp[:, :, :, 0:1], 0.0)
                for f in range(2):
                    last = v.tensor_copy(rw_xp[:, f, :, 1:S], xt[:, f, :, 0:S - 1])
                link(last)
                link(v.tensor_tensor(full(rw_d), xnT.rearrange("p f t -> p (f t)"), full(rw_xp), ALU.subtract))
                dve.wait_ge(rw["v"], 160)
                for n, dst in enumerate((rw_xk, rw_xv, rw_xr)):
                    for f in range(2):
                        last = v.scalar_tensor_tensor(out=dst[:, f], in0=rw_d[:, f], scalar=rw_vec[:, 2 + n, f:f + 1],
                                                      in1=rw_xp[:, f], op0=ALU.mult, op1=ALU.add)
                    last.then_inc(rw["mx"], 1)
                dve.wait_ge(rw["we"], 1)
                link(v.tensor_scalar(rw_wexp, rw_wexp, -1.0, None, ALU.mult))
                v.memset(rw_o[:, :, :, 0:1], NEG)
                v.memset(rw_p[:, :, :, 0:1], 0.0)
                link(v.memset(rw_q[:, :, :, 0:1], 0.0))
                dve.wait_ge(rw["pj"], 4)
                v.tensor_copy(full(rw_k), score[0][:])
                link(v.tensor_copy(full(rw_v), score[1][:]))
                for m in range(2):
                    for b in range(B):
                        last = v.tensor_tensor_scan(rw_o[:, m, b, 1:S + 1], rw_wexp[:, m:m + 1].broadcast_to([128, S]), rw_k[:, m, b, :],
                                                    NEG, ALU.add, ALU.max)
                for m in range(2):
                    last = v.tensor_scalar(rw_Bc[:, m], rw_k[:, m], rw_vec[:, 1, m:m + 1], None, ALU.add)
                link(last)
                for m in range(2):
                    last = v.tensor_tensor(rw_no[:, m], rw_Bc[:, m], rw_o[:, m, :, 0:S], ALU.max)
                link(last)
                dve.wait_ge(rw["pj"], 6)
                for m in range(2):
                    v.tensor_tensor(rw_A[:, m], rw_o[:, m, :, 0:S], rw_no[:, m], ALU.subtract)
                    v.tensor_tensor(rw_Bc[:, m], rw_Bc[:, m], rw_no[:, m], ALU.subtract)
                    v.scalar_tensor_tensor(out=rw_A2[:, m], in0=rw_o[:, m, :, 0:S], scalar=rw_wexp[:, m:m + 1],
                                           in1=rw_o[:, m, :, 1:S + 1], op0=ALU.add, op1=ALU.subtract)
                    last = v.tensor_tensor(rw_B2[:, m], rw_k[:, m], rw_o[:, m, :, 1:S + 1], ALU.subtract)
                last.then_inc(rw["a"], 1)
                dve.wait_ge(rw["a2"], 1)
                link(v.tensor_tensor(full(rw_num), full(rw_B2), full(rw_v), ALU.mult))
                for m in range(2):
                    for b in range(B):
                        v.tensor_tensor_scan(rw_p[:, m, b, 1:S + 1], rw_A2[:, m, b, :], rw_num[:, m, b, :], 0.0, ALU.mult, ALU.add)
                        last = v.tensor_tensor_scan(rw_q[:, m, b, 1:S + 1], rw_A2[:, m, b, :], rw_B2[:, m, b, :], 0.0, ALU.mult, ALU.add)
                link(last)
                for m in range(2):
                    v.tensor_tensor(rw_num[:, m], rw_A[:, m], rw_p[:, m, :, 0:S], ALU.mult)
                    last = v.tensor_tensor(rw_den[:, m], rw_A[:, m], rw_q[:, m, :, 0:S], ALU.mult)
                link(last)
                v.tensor_tensor(full(rw_no), full(rw_Bc), full(rw_v), ALU.mult)
                link(v.tensor_tensor(full(rw_den), full(rw_den), full(rw_Bc), ALU.add))
                v.tensor_tensor(full(rw_num), full(rw_num), full(rw_no), ALU.add)
                link(v.reciprocal(full(rw_den), full(rw_den)))
                link(v.tensor_tensor(full(rw_num), full(rw_num), full(rw_den), ALU.mult))
                dve.wait_ge(rw["sr"], 2)
                v.tensor_tensor(full(rw_out), full(rw_num), full(rw_sr), ALU.mult).then_inc(rw["o"], 1)
                for t in range(TT):
                    dve.wait_ge(rw["out"], t + 1)
                    v.tensor_tensor(x[:, t, :], bank[t % 2][:, 0:D], x[:, t, :], ALU.add).then_inc(rw["res"], 1)

            def chunk_mixture():
                dve.wait_ge(cm["tr"], cm.n("tr", 1))
                v.tensor_copy(gate_w, bank[3][:, 0:16].rearrange("p (f e) -> p f e", f=2)).then_inc(cm["trc"], 1)
                top_two(cm)
                for t in range(TT):
                    for k in range(2):
                        last = v.tensor_scalar(ohtmp[:, k, t, :], iota8[:], idxf[:, t, k:k + 1], None, ALU.is_equal)
                link(last)
                v.tensor_tensor(comb, ohtmp[:, 0], ohtmp[:, 1], ALU.add).then_inc(cm["c"], 1)
                dve.wait_ge(cm["c"], cm.n("c", 2))
                link(v.tensor_copy(tot, bank[3][:, 32:40]))
                link(v.tensor_tensor_scan(incl, ones[:, 0:8], tot, 0.0, ALU.mult, ALU.add))
                link(v.tensor_tensor(incl, incl, tot, ALU.subtract))
                link(v.tensor_tensor(rank_e, bank[3][:, 0:32].rearrange("p (t e) -> p t e", t=TT), bc(incl, 1, TT), ALU.add))
                for k in range(2):
                    last = v.tensor_tensor(ohtmp[:, k], ohtmp[:, k], rank_e, ALU.mult)
                link(last)
                for k in range(2):
                    last = v.tensor_reduce(rank[:, k, :], ohtmp[:, k], AX.X, ALU.add)
                link(last)
                dve.wait_ge(cm["iota"], cm.n("iota", 1))
                for t in range(TT):
                    link(v.tensor_scalar(Ptmp[:, 0, :], iota_s, rank[:, 0, t:t + 1], None, ALU.is_equal))
                    v.scalar_tensor_tensor(out=PA[:, t, :], in0=iota_s, scalar=rank[:, 1, t:t + 1], in1=Ptmp[:, 0, :], op0=ALU.is_equal, op1=ALU.add)
                    link(v.tensor_scalar(Ptmp[:, 1, :], iota_s, rank[:, 1, t:t + 1], tw[:, 1, t:t + 1], ALU.is_equal, ALU.mult))
                    v.scalar_tensor_tensor(out=PW[:, t, :], in0=Ptmp[:, 0, :], scalar=tw[:, 0, t:t + 1], in1=Ptmp[:, 1, :],
                                           op0=ALU.mult, op1=ALU.add).then_inc(cm["pw"], 1)
                    dve.wait_ge(cm["pw"], cm.n("pw", t + 1))
                for n in range(4):
                    dve.wait_ge(cm["pm"], cm.n("pm", n + 1))
                    v.tensor_copy(permT[:, n // 2, 512 * (n % 2):512 * (n % 2) + 512], score[n // 2][:, 512 * (n % 2):512 * (n % 2) + 512]).then_inc(cm["pmc"], 1)
                for e in range(E):
                    dve.wait_ge(cm["tr"], cm.n("tr", e + 2))
                    v.tensor_copy(PWT[:, e, :], bank[2 + e % 2][:]).then_inc(cm["trc"], 1)
                with dve.Fori(0, E) as e:
                    dve.wait_ge(cm["y"], cm.n("y", e + 1))
                    v.tensor_copy(yS[:, bass.ds(e, 1), :].rearrange("p a d -> p (a d)"), bank[2][:, 0:D]).then_inc(cm["yc"], 1)
                for t in range(TT):
                    dve.wait_ge(cm["s"], cm.n("s", t + 1))
                    v.tensor_tensor(x[:, t, :], bank[t % 2][:, 0:D], x[:, t, :], ALU.add).then_inc(cm["res"], 1)

            signal_ahead(dve, "dve")
            dve.wait_ge(const_ready, 1)
            dve.wait_ge(x_in, 16)
            layer_norm(0)
            cross(X0, 0)
            stage_end(dve, 1)
            if upto >= 2:
                layer_norm(1)
                local_attention()
                stage_end(dve, 2)
            if upto >= 3:
                layer_norm(2)
                dense_mixture()
                stage_end(dve, 3)
            if upto >= 4:
                layer_norm(3)
                cross(X1, 3)
                stage_end(dve, 4)
            if upto >= 5:
                layer_norm(4)
                rwkv()
                stage_end(dve, 5)
            if upto >= 6:
                layer_norm(5)
                chunk_mixture()
                stage_end(dve, 6)


_INS = ['x', 'ctx_1024', 'L0_xattn_Wq', 'L0_xattn_Wk', 'L0_xattn_Wv', 'L0_xattn_Wo', 'L0_xattn_bo', 'L0_attn_wq', 'L0_attn_wk',
        'L0_attn_wv', 'L0_attn_wgq', 'L0_attn_wgk', 'L0_attn_wgv', 'L0_attn_r_out_w', 'L0_attn_gate_local_w',
        'L0_attn_gate_remote_w', 'L0_attn_w_out', 'L0_ffn_gate_w', 'L0_ffn_w1', 'L0_ffn_b1', 'L0_ffn_w2', 'L0_ffn_b2',
        'L1_xattn_wq', 'L1_xattn_bq', 'L1_xattn_wk', 'L1_xattn_bk', 'L1_xattn_wv', 'L1_xattn_bv', 'L1_xattn_wo', 'L1_xattn_bo',
        'L1_attn_w', 'L1_attn_u', 'L1_attn_mix_k', 'L1_attn_mix_v', 'L1_attn_mix_r', 'L1_attn_Wk', 'L1_attn_Wv', 'L1_attn_Wr',
        'L1_attn_Wo', 'L1_ffn_Wr', 'L1_ffn_W1', 'L1_ffn_W2']


def kernel(**inputs):
    import concourse.bacc as _bacc
    from concourse.bass_utils import run_bass_kernel_spmd as _run

    nc = _bacc.Bacc("TRN2", target_bir_lowering=False, num_devices=1)
    arrays, aps = {}, {}
    for name in _INS:
        a = np.ascontiguousarray(inputs[name])
        arrays[f"in_{name}"] = a
        aps[name] = nc.dram_tensor(f"in_{name}", a.shape, mybir.dt.from_np(a.dtype), kind="ExternalInput").ap()
    out = nc.dram_tensor("out_x", (B, S, D), F32, kind="ExternalOutput").ap()
    perceiver(nc, aps, out)
    r = _run(nc, [arrays], core_ids=[0])
    return r.results[0]["out_x"]
```

```python
import numpy as np
import concourse.bass as bass
from concourse import mybir
from contextlib import ExitStack

F32 = mybir.dt.float32
BF16 = mybir.dt.bfloat16
F32R = mybir.dt.float32r
U32 = mybir.dt.uint32
ALU = mybir.AluOpType
ACT = mybir.ActivationFunctionType
AX = mybir.AxisListType

B, S, D = 2, 256, 256
TOK = B * S
TT = TOK // 128
CTX = 4096
CHUNK = 512
NCH = CTX // CHUNK
KT = CHUNK // 128
EPS = 1e-5
NEG = -1e30
BLOCK_ENGINES = 4


class Cross:

    def __init__(self, layer, heads, dim):
        self.layer, self.heads, self.dim = layer, heads, dim
        self.hid = heads * dim
        self.tiles = self.hid // 128
        self.hpt = heads // self.tiles
        self.rows = 64 if dim == 64 else 32
        self.groups = self.hid // self.rows
        self.hpg = heads // self.groups
        self.scale = float(dim) ** -0.5
        self.units = heads if dim == 64 else heads // 4 * KT
        self.gps = 1 if dim == 64 else 2
        self.sets = self.groups // self.gps
        self.ups = self.units // self.sets
        self.direct = [h for h in range(heads) if dim == 64 or h % 2 == 0]
        self.running = [h for h in range(heads) if h not in self.direct]


X0 = Cross(0, 8, 64)
X1 = Cross(1, 16, 16)


def perceiver(nc, ins, out, upto=6):
    ctx = ExitStack()
    with ctx:
        def sb(name, shape, dt=F32):
            return ctx.enter_context(nc.sbuf_tensor(name, shape, dt))

        def sem(name):
            return ctx.enter_context(nc.semaphore(name))

        ident = sb("ident", [128, 128])
        ones = sb("ones", [128, 128])
        mask_half = sb("mask_half", [128, 2])
        mask_16th = sb("mask_16th", [128, 8])
        den_pick = sb("den_pick", [128, 128])
        iota8 = sb("iota8", [128, 8])
        zeros = sb("zeros", [128, 128], BF16)
        x = sb("x", [128, TT, D])
        q_hi = sb("q_hi", [128, 16, S], F32R)
        q_hh = sb("q_hh", [128, 16, S], F32R)
        q_lm = sb("q_lm", [128, 16, S], F32R)
        k_st = [sb(f"k_st{i}", [128, CHUNK], F32R) for i in range(4)]
        k_hl, k_h1 = k_st[0:2], k_st[2:4]
        c_hi = sb("c_hi", [128, 2, CHUNK], F32R)
        c_lo = sb("c_lo", [128, 2, CHUNK], F32R)
        k_max = [sb(f"k_max{i}", [128, CHUNK], F32R) for i in range(2)]
        w_split = sb("w_split", [128, 4, 1024], F32R)
        wk_hi, wk_lo, wv_hi, wv_lo = (w_split[:, n, :].rearrange("p (f n) -> p f n", f=2) for n in range(4))
        shift = sb("shift", [32, 128], F32R)
        c_in = sb("c_in", [128, KT, D])
        qT = sb("qT", [128, 4, TOK])
        V = sb("V", [128, KT, 512])
        P = sb("P", [128, 4, 1024])
        arena = sb("arena", [128, 20480])
        xn, xnT = P[:, 0, :].rearrange("p (t d) -> p t d", t=TT), P[:, 1, :].rearrange("p (f t) -> p f t", f=2)
        stats = sb("stats", [128, TT, 6])
        mv = sb("mv", [128, TT, 2])
        rstd = sb("rstd", [128, TT])
        mneg = sb("mneg", [128, 32])
        bias = sb("bias", [128, 16])
        row = sb("row", [1, 256])

        bank = [ctx.enter_context(nc.psum_tensor(f"bank{i}", [128, 512], F32)) for i in (0, 1)]
        score = [ctx.enter_context(nc.psum_tensor(f"score{i}", [128, 1024], F32)) for i in range(2)]
        bank += [ctx.enter_context(nc.psum_tensor(f"bank{i}", [128, 512], F32)) for i in (6, 7)]

        stage_done = sem("stage_done")
        const_ready = sem("const_ready")
        pool_chain, dve_chain, act_chain = sem("pool_chain"), sem("dve_chain"), sem("act_chain")
        x_in = sem("x_in")
        out_stored = sem("out_stored")
        def phase(name, keys):
            return {k: sem(f"{name}_{k}") for k in keys.split()}

        CA = {c.layer: phase(f"ca{c.layer}", "w w0 whl qp q wo wop op res bias" + (" wT wTc pad clear" if c.layer else "")) for c in (X0, X1)}
        class Phase:

            def __init__(self, sems, base):
                self.sems, self.base = sems, base

            def __getitem__(self, key):
                return self.sems[key]

            def n(self, key, count):
                return count + self.base[key]

        POOL_HEADS, DVE_HEADS = (0, 1, 2, 4, 6, 7), (3, 5)

        def summed(i, h):
            key, mine = ("acc", POOL_HEADS) if h in POOL_HEADS else ("accd", DVE_HEADS)
            return key, (i * len(mine) + mine.index(h) + 1) * KT

        def max_counts(c, b):
            return dict(qh=c.heads, qhh=2 * c.groups, ql=c.heads, ctx=16 * NCH, tr=2 * NCH, ch=2 * NCH, cl=2 * NCH,
                        kp=c.tiles * NCH, kev=c.tiles * NCH, s=c.heads * NCH, red=len(c.direct) * NCH,
                        cp=len(c.running) * NCH, rm=len(c.running) * NCH, low=c.layer,
                        m=1, mt=1, mr=1, md=16 if c.layer == 0 else 128)

        def att_counts(c, b):
            own = (dict(z=1, acc=len(POOL_HEADS) * KT * NCH, accd=len(DVE_HEADS) * KT * NCH, osb=0) if c.layer == 0
                   else dict(z=1 - b, acc=0, accd=0, osb=2))
            return dict(ctx=16 * NCH, tr=2 * NCH, ch=2 * NCH, cl=2 * NCH, vp=KT * NCH, v=KT * NCH, khi=c.groups * NCH,
                        kl=c.groups * NCH, kone=c.groups * NCH if c.layer == 0 else 0, s=c.units * NCH,
                        p=c.units * NCH, pfree=4 + c.units * NCH, d=1, rd=1, o=4, **own)

        ahead = {e: [] for e in ("sp", "pe", "act", "dve", "pool")}
        signals = dict(qh="dve", qhh="act", ql="dve", ctx="sp", tr="pe", ch="act", cl="dve", kp="pe", kev="act", s="pe",
                       red="dve", cp="act", rm="dve", low="pool", m="dve", mt="pe", mr="act", md="act", z="pool", vp="pe", v="dve", khi="dve", kl="dve", kone="act",
                       p="act", pfree="pe", acc="pool", accd="dve", d="pe", rd="dve", o="dve", osb="act")

        def once(name, looped, rest=""):
            sems = {k: sem(f"{name}_{k}") for k in (*looped, *rest.split())}
            for k, e in looped.items():
                ahead[e].append(sems[k])
            return Phase(sems, {k: int(k in looped) for k in sems})

        def signal_ahead(eng, name):
            for s in ahead[name]:
                eng.sem_inc(s, 1)

        def runs(name, counts):
            sems, base, made = {k: sem(f"{name}_{k}") for k in counts(X0, 0)}, {k: 1 for k in counts(X0, 0)}, {}
            for k in sems:
                ahead[signals[k]].append(sems[k])
            for c in (X0, X1):
                for b in range(B):
                    credit = {"s": c.hpt, "rm": len(c.running)} if name == "max" else {"s": c.ups, **(dict(
                        acc=len(POOL_HEADS) * KT, accd=len(DVE_HEADS) * KT) if c.layer == 0 else {})}
                    made[c.layer, b] = Phase(sems, {k: n + credit.get(k, 0) for k, n in base.items()})
                    for k, total in counts(c, b).items():
                        base[k] += total + credit.get(k, 0)
            return made

        ln_counts = dict(var=1, std=1, xn=TT, tr=1, xT=2)
        ln_sems = {k: sem(f"ln_{k}") for k in ln_counts}
        LN = [Phase(ln_sems, {k: n * total for k, total in ln_counts.items()}) for n in range(6)]
        MAXP, ATT = runs("max", max_counts), runs("att", att_counts)

        program = ctx.enter_context(nc.Block())

        def stage_end(eng, n):
            eng.drain().then_inc(stage_done, 1)
            eng.wait_ge(stage_done, BLOCK_ENGINES * n)

        def hidden_of(c, g):
            return divmod(c.rows * g, 128)

        TURNS = {0: (6, 7), 1: (12, 13)}

        def block(g, n):
            r = 32 * ((g + n) % 4)
            return slice(r, r + 32)

        Kst = {c.layer: arena[:, 0:c.tiles * CTX].rearrange("p (t k) -> p t k", t=c.tiles) for c in (X0, X1)}
        acc_p = arena[:, 16384:18432].rearrange("p (h q) -> p h q", h=8)
        mx = arena[:, 16384:16384 + NCH * 32].rearrange("p (c h) -> p c h", c=NCH)
        NR = len(X1.running)
        run_max = arena[:, 8192:8192 + 512 * NR].bitcast(BF16).rearrange("p (h n) -> p h n", h=NR)
        copied = arena[:, 8192 + 512 * NR:8192 + 512 * (NR + 2)].bitcast(BF16).rearrange("p (s n) -> p s n", s=2)

        def taken(c, i, h):
            key, mine = ("red", c.direct) if h in c.direct else ("cp", c.running)
            return key, i * len(mine) + mine.index(h) + 1
        oT = arena[:, 18432:20480].rearrange("p (k t) -> p k t", k=4)
        w_raw = arena[:, 0:3072].rearrange("p (w f n) -> p w f n", w=3, f=2)
        w_nat = arena[:, 4096:5632].rearrange("p (w o n) -> p w o n", w=3, o=2)
        wo_nat = c_in[:, 0:2, :]
        wo_pad = V[:, :, :].rearrange("p a n -> p (a n)")[:, 0:1024].rearrange("p (o k) -> p o k", o=2)
        wout = qT[:, 0:2, :].rearrange("p a t -> p (a t)").rearrange("p (k n) -> p k n", k=4)
        Vp = V[:, :, :].rearrange("p a (h d) -> p a h d", h=16)

        def bc(ap, axis, n):
            new = ap.unsqueeze(axis)
            shape = list(new.shape)
            shape[axis] = n
            return new.broadcast_to(shape)


        NHL, NHG, HD, LAT = 16, 8, 16, 64
        GRP = S // LAT
        la = {k: sem("la_" + k) for k in
              "w msk pj pe gt g qp s sb m e tr ptd pta o rq rt rtc rem cb ct ctc out res".split()}
        la_wqkv = arena[:, 0:1536].rearrange("p (w f n) -> p w f n", w=3, f=2)
        la_wg = arena[:, 1536:2304].rearrange("p (w f n) -> p w f n", w=3, f=2)
        la_rout = arena[:, 2304:2560]
        la_wout = arena[:, 2560:3072].rearrange("p (f n) -> p f n", f=2)
        la_KT = arena[:, 3072:4096].rearrange("p (f t) -> p f t", f=2)
        la_QT = arena[:, 4096:5120].rearrange("p (f t) -> p f t", f=2)
        la_GQT, la_GKT = arena[:, 5120:5632], arena[:, 5632:5760]
        la_gate = arena[:, 5760:5888].rearrange("p (t h) -> p t h", t=TT)
        la_V = arena[:, 5888:6976].rearrange("p (t h d) -> p t h d", t=TT, h=NHL)
        la_GV = arena[:, 6976:7248].rearrange("p (b h d) -> p b h d", b=B, h=NHG)
        la_q = arena[:, 7248:9296].rearrange("p (h q) -> p h q", h=NHL)
        la_gq = arena[:, 9296:10320].rearrange("p (h q) -> p h q", h=NHG)
        la_S = arena[:, 10320:14416].rearrange("p (h k) -> p h k", h=NHL)
        la_PT = arena[:, 14416:18512]
        la_mask = arena[:, 18512:18768]
        la_lmask = arena[:, 18768:18896].rearrange("p (u n) -> p u n", u=2)
        la_m = arena[:, 18896:18920]
        la_r = arena[:, 18920:18944]
        la_rs = arena[:, 18944:18960]
        la_cb, la_cT = arena[:, 18992:19248], arena[:, 19248:19504]
        la_rq, la_rqT = arena[:, 19504:19632], arena[:, 19632:19760]
        la_xp = arena[:, 19760:20272].rearrange("p (f b c n) -> p f b c n", f=2, b=B, c=2)
        la_xs = qT[:, 0, 0:256].rearrange("p (f n) -> p f n", f=2)
        la_LS = P[:, 2, 0:512].rearrange("p (h n) -> p h n", h=NHG)
        la_LPT = P[:, 2, 512:1024]
        la_G = P[:, 3, 0:64].rearrange("p (f h) -> p f h", f=2)
        la_gcol = bias[:, 0:4].rearrange("p (f w) -> p f w", f=2)
        la_keys = [1 if t % 2 == 0 else 2 for t in range(TT)]
        la_bufs = [NHL * k * 128 // 1024 for k in la_keys]
        la_quads = [NHL * k // 4 + 1 for k in la_keys]

        def upto_t(counts, t):
            return sum(counts[:t])

        E, F = 8, 1024
        FM = F // 128
        gm = {k: sem("gm_" + k) for k in "w lp t ex cT cTc b2 done bt btc".split()}
        em = once("em", dict(w="sp", w2="sp", w1h="act", w1l="dve", w2h="act", w2l="dve", h="pe", g="act", hh="dve", hl="dve", y="pe", acc="dve"))
        cm = once("cm", dict(w="sp", w2="sp", h="pe", g="act", y="pe", yc="dve"), "lp t ex c pw pm pmc tr trc s res iota wr")
        gate_w = arena[:, 0:16].rearrange("p (f e) -> p f e", f=2)
        lg = arena[:, 16:48].rearrange("p (t e) -> p t e", t=TT)
        top8 = arena[:, 48:80].rearrange("p (t e) -> p t e", t=TT)
        idx8 = arena[:, 80:112].bitcast(U32).rearrange("p (t e) -> p t e", t=TT)
        idxf = arena[:, 112:144].rearrange("p (t e) -> p t e", t=TT)
        tw = arena[:, 144:152].rearrange("p (k t) -> p k t", k=2)
        comb = arena[:, 152:184].rearrange("p (t e) -> p t e", t=TT)
        ohtmp = arena[:, 184:248].rearrange("p (k t e) -> p k t e", k=2, t=TT)
        rank_e = arena[:, 248:280].rearrange("p (t e) -> p t e", t=TT)
        rank = arena[:, 280:288].rearrange("p (k t) -> p k t", k=2)
        tot = arena[:, 288:296]
        incl = arena[:, 296:304]
        combT = arena[0:8, 512:1024]
        b2sb = arena[0:8, 1024:1280]
        b1n = arena[0:64, 1280:1408]
        b1T = arena[:, 1408:1472]
        wr_nat = arena[0:8, 1472:1728]
        w1raw = arena[:, 2048:4096].rearrange("p (f n) -> p f n", f=2)
        w2raw = arena[:, 4096:6144].rearrange("p (k n) -> p k n", k=FM)
        h32 = arena[:, 6144:10240].rearrange("p (m t) -> p m t", m=FM)
        w1_hi, w1_lo = (w_split[:, 2 * n:2 * n + 2, :] for n in range(2))
        w2_hi, w2_lo = (q_lm[:, 8 * n:8 * n + 8, :] for n in range(2))
        h_hi = q_hi[:].rearrange("p h q -> p (h q)").rearrange("p (m t) -> p m t", m=FM)
        h_lo = q_hh[:].rearrange("p h q -> p (h q)").rearrange("p (m t) -> p m t", m=FM)

        rw = {k: sem("rw_" + k) for k in "w v we tr trc mx pj ev sr a a2 o out res".split()}
        rw_nat = arena[:, 0:2048].rearrange("p (w o n) -> p w o n", w=4, o=2)
        rw_W = arena[:, 2048:4096].rearrange("p (w f n) -> p w f n", w=4, f=2)
        rw_xp, rw_d, rw_xk, rw_xv, rw_xr, rw_k, rw_v, rw_sr = (
            arena[:, 4096 + 1024 * n:5120 + 1024 * n].rearrange("p (m b t) -> p m b t", m=2, b=B) for n in range(8))
        rw_o, rw_p, rw_q = (arena[:, 12288 + 1028 * n:13316 + 1028 * n].rearrange("p (m b t) -> p m b t", m=2, b=B) for n in range(3))
        rw_no, rw_A, rw_Bc = (arena[:, 15372 + 1024 * n:16396 + 1024 * n].rearrange("p (m b t) -> p m b t", m=2, b=B) for n in range(3))
        rw_A2, rw_B2 = rw_xp, rw_d
        rw_num, rw_den, rw_out = rw_xk, rw_xv, rw_xr
        rw_vec = bias[:, 0:10].rearrange("p (n f) -> p n f", n=5)
        rw_wexp = bias[:, 10:12]

        SL = 2 * TOK
        cw1 = [arena[:, 4096 * n + 2048:4096 * n + 4096].rearrange("p (f n) -> p f n", f=2) for n in range(1)]
        cw1 = arena[:, 2048:4096].rearrange("p (f n) -> p f n", f=2)
        cw2 = arena[:, 4096:6144].rearrange("p (k n) -> p k n", k=FM)
        PA = arena[:, 6144:10240].rearrange("p (t s) -> p t s", t=TT)
        PW = arena[:, 10240:14336].rearrange("p (t s) -> p t s", t=TT)
        PWT = arena[:, 14336:18432].rearrange("p (e t) -> p e t", e=E)
        Ptmp = arena[:, 18432:20480].rearrange("p (n s) -> p n s", n=2)
        permT = qT[:, :, :].rearrange("p a t -> p (a t)").rearrange("p (f s) -> p f s", f=2)
        hT = c_in[:, :, :].rearrange("p a t -> p (a t)").rearrange("p (m s) -> p m s", m=FM)
        yS = V[:, :, :].rearrange("p a t -> p (a t)").rearrange("p (e d) -> p e d", e=E)
        iota_s = P[:, 2, :]
        before = P[:, 3, 0:128]

        @program.sync
        def _(sp):
            signal_ahead(sp, "sp")
            sp.dma_start(x[:], ins["x"].rearrange("b (u p) d -> p (b u) d", p=128)).then_inc(x_in, 16)

            def cross(c, stage):
                a = CA[c.layer]
                if c.layer == 0:
                    for n, w in enumerate(("Wq", "Wk", "Wv")):
                        sp.dma_start(w_raw[:, n], ins[f"L0_xattn_{w}"].rearrange("(f p) n -> p f n", p=128)).then_inc(a["w"], 16)
                    sp.dma_start(row[0:1, 0:D], ins["L0_xattn_bo"].rearrange("(a n) -> a n", a=1)).then_inc(a["bias"], 16)
                else:
                    sp.wait_ge(stage_done, BLOCK_ENGINES * stage)
                    for n, w in enumerate(("wq", "wk", "wv")):
                        sp.dma_start(w_nat[:, n], ins[f"L1_xattn_{w}"].rearrange("(o p) n -> p o n", p=128)).then_inc(a["w"], 16)
                    sp.dma_start(wo_nat, ins["L1_xattn_wo"].rearrange("(o p) n -> p o n", p=128)).then_inc(a["w"], 16)
                    sp.dma_start(row[0:1, 0:D], ins["L1_xattn_bo"].rearrange("(a n) -> a n", a=1)).then_inc(a["bias"], 16)
                    for n, w in enumerate(("bq", "bk")):
                        for f in range(2):
                            sp.dma_start(bias[:, 2 * n + f:2 * n + f + 1],
                                         ins[f"L1_xattn_{w}"][128 * f:128 * f + 128].rearrange("(p a) -> p a", a=1)).then_inc(a["bias"], 16)
                    sp.wait_ge(a["pad"], 1)
                    for g in range(4):
                        for j in range(4):
                            h = 4 * g + j
                            sp.dma_start(bias[32 * j:32 * j + 16, 4 + g:5 + g],
                                         ins["L1_xattn_bv"][16 * h:16 * h + 16].rearrange("(p a) -> p a", a=1)).then_inc(a["bias"], 16)
                for b in range(B):
                    chunks = ins["ctx_1024"][b].rearrange("(c k p) d -> c p k d", k=KT, p=128)
                    m, t = MAXP[c.layer, b], ATT[c.layer, b]
                    for ph in (m, t):
                        if ph is m and b == 0 and c.layer == 1:
                            sp.wait_ge(a["pad"], 2)
                        if ph is m and b == 1:
                            sp.wait_ge(ATT[c.layer, 0]["tr"], ATT[c.layer, 0].n("tr", 2 * NCH))
                        if ph is t:
                            sp.wait_ge(m["tr"], m.n("tr", 2 * NCH))
                        with sp.Fori(0, NCH) as i:
                            sp.wait_ge(ph["tr"], ph.n("tr", 2 * i))
                            sp.dma_start(c_in[:], chunks[bass.ds(i, 1), :, :, :].rearrange("a p k d -> p (a k) d")).then_inc(ph["ctx"], 16)
                    if b == 1 and c.layer == 0:
                        sp.wait_ge(MAXP[0, 1]["ql"], MAXP[0, 1].n("ql", c.heads))
                        sp.dma_start(wout, ins["L0_xattn_Wo"].rearrange("(k p) n -> p k n", p=128)).then_inc(a["wo"], 16)


            def stage_free(n):
                sp.wait_ge(stage_done, BLOCK_ENGINES * n)

            def local_attention():
                stage_free(1)
                for n, w in enumerate(("wq", "wk", "wv")):
                    sp.dma_start(la_wqkv[:, n], ins[f"L0_attn_{w}"].rearrange("(f p) n -> p f n", p=128)).then_inc(la["w"], 16)
                for n, w in enumerate(("wgq", "wgk", "wgv")):
                    sp.dma_start(la_wg[:, n], ins[f"L0_attn_{w}"].rearrange("(f p) n -> p f n", p=128)).then_inc(la["w"], 16)
                sp.dma_start(la_rout, ins["L0_attn_r_out_w"]).then_inc(la["w"], 16)
                sp.dma_start(la_wout, ins["L0_attn_w_out"].rearrange("(f p) n -> p f n", p=128)).then_inc(la["w"], 16)
                for n, w in enumerate(("gate_local_w", "gate_remote_w")):
                    for f in range(2):
                        sp.dma_start(la_gcol[:, f, n:n + 1],
                                     ins[f"L0_attn_{w}"][8 * f:8 * f + 8, :].rearrange("h (d a) -> (h d) a", a=1)).then_inc(la["w"], 16)

            def dense_mixture():
                stage_free(2)
                sp.dma_start(gate_w, ins["L0_ffn_gate_w"].rearrange("(f p) e -> p f e", p=128)).then_inc(gm["w"], 16)
                sp.dma_start(b2sb, ins["L0_ffn_b2"]).then_inc(gm["w"], 16)
                sp.dma_start(b1n, ins["L0_ffn_b1"].rearrange("e (m p) -> (e m) p", p=128)).then_inc(gm["w"], 16)
                w1d = ins["L0_ffn_w1"].rearrange("e (f p) n -> e p f n", p=128)
                w2d = ins["L0_ffn_w2"].rearrange("e (k p) n -> e p k n", p=128)
                with sp.Fori(0, E) as e:
                    sp.wait_ge(em["w1l"], em.n("w1l", e))
                    sp.dma_start(w1raw, w1d[bass.ds(e, 1)].rearrange("a p f n -> p (a f) n")).then_inc(em["w"], 16)
                    sp.wait_ge(em["w2l"], em.n("w2l", e))
                    sp.dma_start(w2raw, w2d[bass.ds(e, 1)].rearrange("a p k n -> p (a k) n")).then_inc(em["w2"], 16)

            def rwkv():
                stage_free(4)
                for n, w in enumerate(("Wk", "Wv", "Wr", "Wo")):
                    sp.dma_start(rw_nat[:, n], ins[f"L1_attn_{w}"].rearrange("(o p) n -> p o n", p=128)).then_inc(rw["w"], 16)
                for n, w in enumerate(("w", "u", "mix_k", "mix_v", "mix_r")):
                    for f in range(2):
                        sp.dma_start(rw_vec[:, n, f:f + 1], ins[f"L1_attn_{w}"][128 * f:128 * f + 128].rearrange("(p a) -> p a", a=1)).then_inc(rw["v"], 16)

            def chunk_mixture():
                stage_free(5)
                sp.dma_start(wr_nat, ins["L1_ffn_Wr"]).then_inc(cm["wr"], 16)
                w1d = ins["L1_ffn_W1"].rearrange("e (f p) n -> e p f n", p=128)
                w2d = ins["L1_ffn_W2"].rearrange("e (k p) n -> e p k n", p=128)
                with sp.Fori(0, E) as e:
                    sp.wait_ge(cm["h"], cm.n("h", FM * e))
                    sp.dma_start(cw1, w1d[bass.ds(e, 1)].rearrange("a p f n -> p (a f) n")).then_inc(cm["w"], 16)
                    sp.wait_ge(cm["y"], cm.n("y", e))
                    sp.dma_start(cw2, w2d[bass.ds(e, 1)].rearrange("a p k n -> p (a k) n")).then_inc(cm["w2"], 16)

            cross(X0, 0)
            if upto >= 2: local_attention()
            if upto >= 3: dense_mixture()
            if upto >= 4: cross(X1, 3)
            if upto >= 5: rwkv()
            if upto >= 6: chunk_mixture()
            sp.wait_ge(stage_done, BLOCK_ENGINES * upto)
            sp.dma_start(out.rearrange("b (u p) d -> p (b u) d", p=128), x[:]).then_inc(out_stored, 16)
            sp.wait_ge(out_stored, 16)

        @program.gpsimd
        def _(pool):
            chain = [0]

            def link(i):
                chain[0] += 1
                i.then_inc(pool_chain, 1)
                pool.wait_ge(pool_chain, chain[0])

            signal_ahead(pool, "pool")
            link(pool.memset(ident[:], 0.0))
            link(pool.affine_select(out=ident[:], in_=ident[:], compare_op=ALU.not_equal, fill=1.0,
                                    base=0, pattern=[[-1, 128]], channel_multiplier=1))
            link(pool.memset(ones[:], 1.0))
            link(pool.memset(zeros[:], 0.0))
            for tile, width in ((mask_half, 64), (mask_16th, 16)):
                n = 128 // width
                link(pool.memset(tile[:], 1.0))
                link(pool.affine_select(out=tile[:], in_=tile[:], compare_op=ALU.is_ge, fill=0.0,
                                        base=0, pattern=[[-width, n]], channel_multiplier=1))
                link(pool.affine_select(out=tile[:], in_=tile[:], compare_op=ALU.is_gt, fill=0.0,
                                        base=width, pattern=[[width, n]], channel_multiplier=-1))
            link(pool.memset(den_pick[:], 0.0))
            link(pool.affine_select(out=den_pick[:].rearrange("p (j d) -> p j d", j=4),
                                    in_=den_pick[:].rearrange("p (j d) -> p j d", j=4),
                                    compare_op=ALU.not_equal, fill=1.0, base=-16,
                                    pattern=[[-32, 4], [0, 32]], channel_multiplier=1))
            link(pool.iota(iota8[:], pattern=[[1, 8]], base=0, channel_multiplier=0,
                           allow_small_or_imprecise_dtypes=True))
            for i in range(2):
                pool.memset(k_h1[i][64:65, :].bitcast(F32), 1.0)
            pool.engine_nop().then_inc(const_ready, 1)

            def cross(c, stage):
                for b in range(B):
                    t = ATT[c.layer, b]
                    if c.layer == 1:
                        if b == 1:
                            pool.wait_ge(MAXP[1, 0]["m"], MAXP[1, 0].n("m", 1))
                        pool.memset(run_max, -3e38).then_inc(MAXP[1, b]["low"], 1)
                        pool.wait_ge(MAXP[1, b]["low"], MAXP[1, b].n("low", 1))
                    if c.layer == 0:
                        if b == 1:
                            pool.wait_ge(ATT[0, 0]["d"], ATT[0, 0].n("d", 1))
                        pool.sem_inc(t["acc"], len(POOL_HEADS) * KT)
                        pool.wait_ge(MAXP[0, b]["m"], MAXP[0, b].n("m", 1))
                        pool.memset(acc_p, 0.0).then_inc(t["z"], 1)
                    if c.layer == 1 and b == 0:
                        link(pool.memset(q_hh[:].bitcast(F32), 0.0))
                        for g in range(4):
                            link(pool.memset(k_st[g][block(g, 3), :].bitcast(F32), 0.0))
                            link(pool.memset(k_st[g][block(g, 3).start:block(g, 3).start + 1, :].bitcast(F32), 1.0))
                        pool.engine_nop().then_inc(CA[1]["clear"], 1)
                        pool.wait_ge(CA[1]["wop"], 1)
                        link(pool.memset(V[:], 0.0))
                        pool.memset(Vp[:, :, :, 16:17], 1.0).then_inc(t["z"], 1)
                    if c.layer == 1:
                        continue
                    pool.wait_ge(t["z"], t.n("z", 1))
                    with pool.Fori(0, NCH) as i:
                        for u in POOL_HEADS:
                            pool.wait_ge(t["p"], t.n("p", i * 8 + u + 1))
                            for k in range(KT):
                                pool.wait_ge(t["acc"], t.n("acc", summed(i, u)[1] - KT + k))
                                pool.tensor_tensor(acc_p[:, u, :], acc_p[:, u, :],
                                                   P[:, u % 4, k * S:(k + 1) * S], ALU.add).then_inc(t["acc"], 1)

            def local_attention():
                diag, off = la_mask[:, 128:256], la_mask[:, 0:128]
                link(pool.memset(la_mask, 0.0))
                link(pool.affine_select(out=diag, in_=diag, compare_op=ALU.is_ge, fill=NEG, base=0,
                                        pattern=[[-1, 128]], channel_multiplier=1))
                link(pool.affine_select(out=diag, in_=diag, compare_op=ALU.is_gt, fill=NEG, base=64,
                                        pattern=[[1, 128]], channel_multiplier=-1))
                link(pool.affine_select(out=off, in_=off, compare_op=ALU.is_gt, fill=NEG, base=-64,
                                        pattern=[[1, 128]], channel_multiplier=-1))
                link(pool.memset(la_lmask, 0.0))
                link(pool.affine_select(out=la_lmask, in_=la_lmask, compare_op=ALU.is_ge, fill=NEG, base=0,
                                        pattern=[[128, 2], [-GRP, LAT]], channel_multiplier=1))
                pool.memset(la_V[:, :, :, HD:HD + 1], 1.0)
                link(pool.memset(la_GV, 0.0))
                for r in (0, 1):
                    last = pool.memset(la_GV[64 * r:64 * r + 64, :, r::2, HD:HD + 1], 1.0)
                last.then_inc(la["msk"], 1)

            def chunk_mixture():
                link(pool.iota(iota_s, pattern=[[1, SL]], base=0, channel_multiplier=0, allow_small_or_imprecise_dtypes=True))
                link(pool.memset(before, 1.0))
                pool.affine_select(out=before, in_=before, compare_op=ALU.is_gt, fill=0.0, base=0,
                                   pattern=[[1, 128]], channel_multiplier=-1).then_inc(cm["iota"], 1)

            pool.wait_ge(const_ready, 1)
            cross(X0, 0)
            stage_end(pool, 1)
            if upto >= 2:
                local_attention()
                stage_end(pool, 2)
            if upto >= 3: stage_end(pool, 3)
            if upto >= 4:
                cross(X1, 3)
                stage_end(pool, 4)
            if upto >= 5: stage_end(pool, 5)
            if upto >= 6:
                chunk_mixture()
                stage_end(pool, 6)

        @program.scalar
        def _(act):
            chain = [0]

            def link(i):
                chain[0] += 1
                i.then_inc(act_chain, 1)
                act.wait_ge(act_chain, chain[0])

            def layer_norm(n):
                ln = LN[n]
                act.wait_ge(ln["var"], ln.n("var", 1))
                act.activation(rstd[:], mv[:, :, 1], ACT.Sqrt).then_inc(ln["std"], 1)
                act.wait_ge(ln["tr"], ln.n("tr", 1))
                act.activation(xnT[:, 0, :], bank[0][:], ACT.Copy).then_inc(ln["xT"], 1)

            def context_high(c, ph, f, i, dst):
                act.wait_ge(ph["tr"], ph.n("tr", 2 * i + f + 1))
                act.activation(c_hi[:, f, :], dst[:], ACT.Copy).then_inc(ph["ch"], 1)

            def cross(c, stage):
                a = CA[c.layer]
                if c.layer == 0:
                    act.wait_ge(a["w"], 48)
                    srcs = [w_raw[:, 1], w_raw[:, 2]]
                    for n, (src, hi) in enumerate(zip(srcs, (wk_hi, wv_hi))):
                        act.activation(hi, src, ACT.Copy).then_inc(a["w0"], 1)
                else:
                    for n in range(3):
                        act.wait_ge(a["wT"], n + 1)
                        pt = bank[n % 2]
                        if n == 0:
                            act.activation(w_raw[:, 0, 0, :], pt[:], ACT.Copy).then_inc(a["wTc"], 1)
                        else:
                            hi = (wk_hi, wv_hi)[n - 1]
                            act.activation(hi[:, :, 0:256], pt[:].rearrange("p (f n) -> p f n", f=2), ACT.Copy).then_inc(a["w0"], 1)
                for b in range(B):
                    m, t = MAXP[c.layer, b], ATT[c.layer, b]
                    for h0 in range(0, c.heads, c.hpg):
                        g = h0 // c.hpg
                        _, r = hidden_of(c, g)
                        act.wait_ge(m["qh"], m.n("qh", h0 + c.hpg))
                        if b == 1 and g == 0:
                            act.wait_ge(ATT[c.layer, 0]["s"], ATT[c.layer, 0].n("s", NCH * c.units))
                        if c.layer == 1 and b == 0 and g == 0:
                            act.wait_ge(a["clear"], 1)
                        for dst in (slice(0, 64), slice(64, 128)) if c.layer == 0 else (block(g, 0), block(g, 2)):
                            act.activation(q_hh[dst, h0:h0 + c.hpg, :],
                                           q_hi[r:r + c.rows, h0:h0 + c.hpg, :].bitcast(F32), ACT.Copy).then_inc(m["qhh"], 1)
                    if b == 1:
                        act.wait_ge(ATT[c.layer, 0]["vp"], ATT[c.layer, 0].n("vp", KT * NCH))
                    def high(i):
                        act.wait_ge(m["kp"], m.n("kp", c.tiles * i))
                        for f in range(2):
                            context_high(c, m, f, i, bank[f])

                    def keep(i, tiles):
                        for n in tiles:
                            act.wait_ge(m["kp"], m.n("kp", c.tiles * i + n + 1))
                            act.wait_ge(m["s"], m.n("s", (c.tiles * i + n - 1) * c.hpt))
                            src = bank[2 + n % 2][:]
                            dst = Kst[c.layer][:, n, bass.ts(i, CHUNK)]
                            if c.layer == 0:
                                act.activation(dst, src, ACT.Copy)
                                act.activation(k_max[n % 2][:], src, ACT.Copy).then_inc(m["kev"], 1)
                            else:
                                act.activation(dst, src, ACT.Identity, bias=bias[:, 2 + n:3 + n])
                                act.activation(k_max[n % 2][:], src, ACT.Identity, bias=bias[:, 2 + n:3 + n]).then_inc(m["kev"], 1)

                    def copy_out(i, heads):
                        for h in heads:
                            if h in c.running:
                                n = c.running.index(h)
                                act.wait_ge(m["s"], m.n("s", i * c.heads + h + 1))
                                act.wait_ge(m["rm"], m.n("rm", i * NR + n - 1))
                                act.activation(copied[:, n % 2, :], score[h % 2][:], ACT.Copy).then_inc(m["cp"], 1)

                    def chunk(i, last=False):
                        keep(i, range(1, c.tiles))
                        copy_out(i, range(8))
                        if not last:
                            high(i + 1)
                            copy_out(i, range(8, 14))
                            keep(i + 1, range(1))
                            copy_out(i, range(14, 16))
                        else:
                            copy_out(i, range(8, 16))

                    high(0)
                    keep(0, range(1))
                    with act.Fori(0, NCH - 1) as i:
                        chunk(i)
                    chunk(NCH - 1, last=True)
                    act.wait_ge(m["mt"], m.n("mt", 1))
                    act.activation(shift[0:2 * c.heads, :], bank[0][0:2 * c.heads, 0:128], ACT.Copy).then_inc(m["mr"], 1)
                    act.wait_ge(m["mr"], m.n("mr", 1))
                    if c.layer == 0:
                        act.dma_start(q_lm[64:65, 0:c.heads, :].rearrange("a h q -> a (h q)").bitcast(F32),
                                     shift[0:2 * c.heads, :].bitcast(F32)).then_inc(m["md"], 16)
                    else:
                        for g in range(c.groups):
                            r = block(g, 3).start
                            act.dma_start(q_hh[r:r + 1, 2 * g:2 * g + 2, :].rearrange("a h q -> a (h q)").bitcast(F32),
                                         shift[4 * g:4 * g + 4, :].bitcast(F32)).then_inc(m["md"], 16)
                    def keys(i, g):
                        tile, r = hidden_of(c, g)
                        act.activation(k_h1[g % 2][0:64, :], Kst[0][r:r + 64, tile, bass.ts(i, CHUNK)], ACT.Copy).then_inc(t["kone"], 1)

                    def chunk(i, last=False):
                        for u in range(c.units):
                            n = i * c.units + u
                            act.wait_ge(t["s"], t.n("s", n + 1))
                            act.wait_ge(t["pfree"], t.n("pfree", n + 1))
                            if c.layer == 0:
                                key, count = summed(i if u >= 4 else i - 1, (u - 4) % 8)
                                act.wait_ge(t[key], t.n(key, count))
                            act.activation(P[:, u % 4, :], score[u % 2][:], ACT.Exp).then_inc(t["p"], 1)
                            if c.layer == 0 and u < 6:
                                keys(i, u + 2)
                            elif c.layer == 0 and not last:
                                keys(i + 1, u - 6)
                            if u in TURNS[c.layer] and not last:
                                if u == TURNS[c.layer][0]:
                                    act.wait_ge(t["vp"], t.n("vp", KT * i + KT))
                                context_high(c, t, u - TURNS[c.layer][0], i + 1, bank[2])

                    for f in range(2):
                        context_high(c, t, f, 0, bank[2])
                    if c.layer == 0:
                        keys(0, 0)
                        keys(0, 1)
                    with act.Fori(0, NCH - 1) as i:
                        chunk(i)
                    chunk(NCH - 1, last=True)
                    if c.layer == 1:
                        act.wait_ge(t["pfree"], t.n("pfree", NCH * c.units + 4))
                        for k in range(2):
                            act.activation(P[:, 0, 512 * k:512 * k + 512], bank[k][:], ACT.Copy).then_inc(t["osb"], 1)


            def local_attention():
                act.wait_ge(la["gt"], 2)
                act.activation(la_gate, bank[2][:, 0:128].rearrange("p (t h) -> p t h", t=TT), ACT.Sigmoid).then_inc(la["g"], 1)
                for t in range(TT):
                    keys, quads = 128 * la_keys[t], upto_t(la_quads, t)
                    act.wait_ge(la["m"], 2 * t + 2)
                    for h in range(NHL):
                        last = act.activation(la_S[:, h, 0:keys], la_S[:, h, 0:keys], ACT.Exp, bias=la_m[:, h:h + 1])
                    for h in range(NHG):
                        last = act.activation(la_LS[:, h, :], la_LS[:, h, :], ACT.Exp, bias=la_m[:, NHL + h:NHL + h + 1])
                    last.then_inc(la["e"], 1)
                    for n in range(1, la_quads[t], 2):
                        act.wait_ge(la["tr"], quads + n + 1)
                        dst = la_LPT if n == la_quads[t] - 1 else la_PT[:, 512 * n:512 * n + 512]
                        act.activation(dst, bank[2 + n % 2][:], ACT.Copy).then_inc(la["pta"], 1)

            def dense_mixture():
                act.wait_ge(gm["t"], 1)
                act.activation(tw[:, 1, :], tw[:, 0, :], ACT.Exp).then_inc(gm["ex"], 1)
                def high_w1(e):
                    act.wait_ge(em["w"], em.n("w", 16 * e + 16))
                    act.wait_ge(em["h"], em.n("h", FM * e))
                    act.activation(w1_hi, w1raw, ACT.Copy).then_inc(em["w1h"], 1)

                def expert(e, last=False):
                    for m in range(FM):
                        act.wait_ge(em["h"], em.n("h", FM * e + m + 1))
                        act.wait_ge(em["hl"], em.n("hl", FM * e))
                        act.activation(h32[:, m, :], bank[m % 2][:], ACT.Gelu, bias=b1T[:, bass.ds(e * FM + m, 1)]).then_inc(em["g"], 1)
                        if m == 1:
                            act.wait_ge(em["w2"], em.n("w2", 16 * e + 16))
                            act.wait_ge(em["y"], em.n("y", TT * e))
                            act.activation(w2_hi, w2raw, ACT.Copy).then_inc(em["w2h"], 1)
                    if not last:
                        high_w1(e + 1)

                high_w1(0)
                with act.Fori(0, E - 1) as e:
                    expert(e)
                expert(E - 1, last=True)

            def rwkv():
                act.wait_ge(rw["v"], 160)
                act.activation(rw_wexp, rw_vec[:, 0, :], ACT.Exp).then_inc(rw["we"], 1)
                act.wait_ge(rw["pj"], 6)
                for m in range(2):
                    act.activation(rw_sr[:, m].rearrange("p b t -> p (b t)"), bank[2 + m][:], ACT.Sigmoid).then_inc(rw["sr"], 1)
                act.wait_ge(rw["a"], 1)
                act.activation(rw_A[:], rw_A[:], ACT.Exp)
                act.activation(rw_Bc[:], rw_Bc[:], ACT.Exp)
                act.activation(rw_A2[:], rw_A2[:], ACT.Exp)
                act.activation(rw_B2[:], rw_B2[:], ACT.Exp).then_inc(rw["a2"], 1)

            def chunk_mixture():
                act.wait_ge(cm["t"], cm.n("t", 1))
                act.activation(tw[:, 1, :], tw[:, 0, :], ACT.Exp).then_inc(cm["ex"], 1)
                with act.Fori(0, E) as e:
                    for m in range(FM):
                        act.wait_ge(cm["h"], cm.n("h", FM * e + m + 1))
                        act.wait_ge(cm["y"], cm.n("y", e))
                        act.activation(hT[:, m, :], bank[m % 2][:, 0:128], ACT.Gelu).then_inc(cm["g"], 1)

            signal_ahead(act, "act")
            act.wait_ge(const_ready, 1)
            layer_norm(0)
            cross(X0, 0)
            stage_end(act, 1)
            if upto >= 2:
                layer_norm(1)
                local_attention()
                stage_end(act, 2)
            if upto >= 3:
                layer_norm(2)
                dense_mixture()
                stage_end(act, 3)
            if upto >= 4:
                layer_norm(3)
                cross(X1, 3)
                stage_end(act, 4)
            if upto >= 5:
                layer_norm(4)
                rwkv()
                stage_end(act, 5)
            if upto >= 6:
                layer_norm(5)
                chunk_mixture()
                stage_end(act, 6)

        @program.tensor
        def _(pe):
            mm = nc.tensor.matmul

            def layer_norm(n):
                ln = LN[n]
                pe.wait_ge(ln["xn"], ln.n("xn", TT))
                for f in range(2):
                    for t in range(TT):
                        last = nc.tensor.transpose(bank[f][:, 128 * t:128 * t + 128], xn[:, t, 128 * f:128 * f + 128], ident[:])
                last.then_inc(ln["tr"], 1)

            def turn_chunk(ph, f, i, dst):
                if f == 0:
                    pe.wait_ge(ph["ctx"], ph.n("ctx", 16 * i + 16))
                for k in range(KT):
                    last = nc.tensor.transpose(dst[:, 128 * k:128 * k + 128], c_in[:, k, 128 * f:128 * f + 128], ident[:])
                last.then_inc(ph["tr"], 1)

            def three(dst, pairs):
                for n, (l, r) in enumerate(pairs):
                    last = mm(dst, l, r, start=(n == 0), stop=(n == len(pairs) - 1))
                return last

            def cross(c, stage):
                a = CA[c.layer]
                if c.layer == 1:
                    pe.wait_ge(a["w"], 64)
                    pe.wait_ge(LN[3]["xT"], LN[3].n("xT", 2))
                    for n in range(3):
                        if n >= 2:
                            pe.wait_ge(a["wTc"], 1)
                        for f in range(2):
                            for o in range(2):
                                last = nc.tensor.transpose(bank[n % 2][:, 256 * f + 128 * o:256 * f + 128 * o + 128],
                                                           w_nat[:, n, o, 128 * f:128 * f + 128], ident[:])
                        last.then_inc(a["wT"], 1)
                else:
                    pe.wait_ge(a["w"], 48)
                    pe.wait_ge(LN[0]["xT"], LN[0].n("xT", 2))
                wq = w_raw[:, 0] if c.layer == 0 else w_raw[:, 0, 0, :].rearrange("p (f n) -> p f n", f=2)
                for n in range(c.tiles):
                    if n >= 2:
                        pe.wait_ge(a["q"], n - 1)
                    for f in range(2):
                        last = mm(bank[2 + n % 2][:], wq[:, f, 128 * n:128 * n + 128], xnT[:, f, :], start=(f == 0), stop=(f == 1))
                    last.then_inc(a["qp"], 1)
                if c.layer == 1:
                    pe.wait_ge(a["pad"], 2)
                    for k in range(4):
                        for o in range(2):
                            last = nc.tensor.transpose(score[0][:, 256 * k + 128 * o:256 * k + 128 * o + 128],
                                                       wo_pad[:, o, 128 * k:128 * k + 128], ident[:])
                    last.then_inc(a["wop"], 1)
                for b in range(B):
                    m, t = MAXP[c.layer, b], ATT[c.layer, b]
                    pe.sem_inc(m["s"], c.hpt)
                    pe.wait_ge(m["qh"], m.n("qh", c.heads))
                    if b == 0:
                        pe.wait_ge(a["whl"], 2)
                        pe.wait_ge(a["q"], c.tiles)
                        if c.layer == 1:
                            pe.wait_ge(a["wop"], 2)
                    if b == 1:
                        pe.wait_ge(ATT[c.layer, 0]["o"], ATT[c.layer, 0].n("o", 4))
                    def turn_both(i):
                        pe.wait_ge(m["cl"], m.n("cl", 2 * i))
                        turn_chunk(m, 0, i, bank[0])
                        turn_chunk(m, 1, i, bank[1])

                    def project(i, n):
                        if n == 0:
                            pe.wait_ge(m["cl"], m.n("cl", 2 * i + 2))
                        if n < 2:
                            pe.wait_ge(m["kev"], m.n("kev", c.tiles * i))
                        else:
                            pe.wait_ge(m["kev"], m.n("kev", c.tiles * i + n - 1))
                        cols = slice(128 * n, 128 * n + 128)
                        pairs = [(w[:, f, cols], v[:, f, :]) for f in range(2)
                                 for w, v in ((wk_hi, c_hi), (wk_hi, c_lo), (wk_lo, c_hi))]
                        three(bank[2 + n % 2][:], pairs).then_inc(m["kp"], 1)

                    def maxima(i, n, heads):
                        pe.wait_ge(m["kev"], m.n("kev", c.tiles * i + n + 1))
                        for j in heads:
                            h = n * c.hpt + j
                            if h >= 2:
                                key, count = taken(c, i, h - 2)
                            elif c.layer == 0:
                                key, count = "red", i * c.heads
                            else:
                                key, count = taken(c, i - 1, h + c.heads - 2)
                            pe.wait_ge(m[key], m.n(key, count))
                            for qt in range(2):
                                last = mm(score[h % 2][:, 512 * qt:512 * qt + 512], q_hi[:, h, 128 * qt:128 * qt + 128],
                                          k_max[n % 2][:], start=True, stop=True)
                            last.then_inc(m["s"], 1)

                    def chunk(i, last=False):
                        for n in range(1, c.tiles):
                            project(i, n)
                            maxima(i, n - 1, range(c.hpt))
                        if last:
                            maxima(i, c.tiles - 1, range(c.hpt))
                        else:
                            turn_both(i + 1)
                            maxima(i, c.tiles - 1, range(c.hpt - 1) if c.layer == 0 else range(c.hpt - 2))
                            project(i + 1, 0)
                            maxima(i, c.tiles - 1, range(c.hpt - 1, c.hpt) if c.layer == 0 else range(c.hpt - 2, c.hpt))

                    turn_both(0)
                    project(0, 0)
                    with pe.Fori(0, NCH - 1) as i:
                        chunk(i)
                    chunk(NCH - 1, last=True)
                    pe.wait_ge(m["m"], m.n("m", 1))
                    nc.tensor.transpose(bank[0][0:2 * c.heads, 0:128], mneg[:, 0:2 * c.heads], ident[:]).then_inc(m["mt"], 1)
                    def turn(i, f):
                        pe.wait_ge(t["cl"], t.n("cl", 2 * i + f))
                        turn_chunk(t, f, i, bank[2])

                    turn(0, 0), turn(0, 1)
                    pe.wait_ge(m["mr"], m.n("mr", 1))
                    pe.sem_inc(t["s"], c.ups)
                    pe.sem_inc(t["pfree"], 4)
                    for k in range(2):
                        for n in range(4):
                            mm(bank[k][:, 128 * n:128 * n + 128], zeros[:], zeros[:], start=(n == 0), stop=False, skip_group_check=True)
                    pe.wait_ge(m["md"], m.n("md", 16 if c.layer == 0 else 128))
                    pe.wait_ge(m["ql"], m.n("ql", c.heads))
                    pe.wait_ge(m["qhh"], m.n("qhh", 2 * c.groups))
                    if c.layer == 1 and b == 0:
                        pe.wait_ge(t["z"], t.n("z", 1))
                    def weigh(i, u):
                        if c.layer == 0:
                            pe.wait_ge(t["p"], t.n("p", i * 8 + u + 2))
                            if u == 0:
                                pe.wait_ge(t["v"], t.n("v", KT * i + KT))
                            for k in range(KT):
                                for j in range(2):
                                    p = u // 2
                                    last = mm(bank[p // 2][64 * j:64 * j + 64, S * (p % 2):S * (p % 2) + S],
                                              V[:, k, 64 * (u + j):64 * (u + j) + 64], P[:, (u + j) % 4, S * k:S * k + S],
                                              start=False, stop=False, skip_group_check=True, tile_position=(0, 64 * j))
                            last.then_inc(t["pfree"], 2)
                        else:
                            g, k = u // KT, u % KT
                            pe.wait_ge(t["p"], t.n("p", i * 16 + u + 1))
                            pe.wait_ge(t["v"], t.n("v", KT * i + k + 1)) if u < 4 else None
                            for j in range(4):
                                last = mm(bank[g // 2][32 * j:32 * j + 32, S * (g % 2):S * (g % 2) + S],
                                          Vp[:, k, 4 * g + j, :], P[:, u % 4, S * j:S * j + S],
                                          start=False, stop=False, skip_group_check=True, tile_position=(0, 32 * j))
                            last.then_inc(t["pfree"], 1)

                    def chunk(i, first=False, last=False):
                        def values(k):
                            if k == 0:
                                pe.wait_ge(t["cl"], t.n("cl", 2 * i + 2))
                            pe.wait_ge(t["v"], t.n("v", KT * i + k))
                            cols = slice(128 * k, 128 * k + 128)
                            pairs = [(v[:, f, cols], w[:, f, 0:c.hid]) for f in range(2)
                                     for v, w in ((c_hi, wv_hi), (c_hi, wv_lo), (c_lo, wv_hi))]
                            three(bank[3][:, 0:c.hid], pairs).then_inc(t["vp"], 1)

                        def scores(u):
                            g = u // c.ups
                            if u % c.ups == 0:
                                pe.wait_ge(t["kl"], t.n("kl", i * c.groups + c.gps * (g + 1)))
                                if c.layer == 0:
                                    pe.wait_ge(t["kone"], t.n("kone", i * 8 + g + 1))
                            if u >= 2:
                                pe.wait_ge(t["p"], t.n("p", i * c.units + u - 1))
                            else:
                                pe.wait_ge(t["s"], t.n("s", i * c.units))
                                if u == 0:
                                    pe.wait_ge(t["p"], t.n("p", i * c.units))
                            if c.layer == 0:
                                hl, h1 = k_hl[g % 2], k_h1[g % 2]
                                for k in range(KT):
                                    o = score[u % 2][:, S * k:S * k + S]
                                    cols = slice(128 * k, 128 * k + 128)
                                    mm(o, hl[:, cols], q_hh[:, g, :], start=True, stop=False)
                                    last = mm(o, h1[0:65, cols], q_lm[0:65, g, :], start=False, stop=True)
                            else:
                                cols = slice(128 * (u % KT), 128 * (u % KT) + 128)
                                for j in range(0, 4, 2):
                                    h = 4 * g + j
                                    o = score[u % 2][:, S * j:S * j + 2 * S]
                                    last = mm(o, k_st[h // 2 % 4][:, cols], q_hh[:, h:h + 2, :], start=True, stop=True)
                            last.then_inc(t["s"], 1)

                        for u in range(c.units):
                            scores(u)
                            if c.layer == 0:
                                if u == 1 and not first:
                                    weigh(i - 1, 6)
                                if 1 <= u <= KT:
                                    values(u - 1)
                                if u in (4, 5, 7):
                                    weigh(i, {4: 0, 5: 2, 7: 4}[u])
                            else:
                                if u < 3 and not first:
                                    weigh(i - 1, 13 + u)
                                if u < KT:
                                    values(u)
                                if u >= 3:
                                    weigh(i, u - 3)
                            if u in TURNS[c.layer] and not last:
                                turn(i + 1, u - TURNS[c.layer][0])

                    chunk(0, first=True)
                    with pe.Fori(1, NCH - 1) as i:
                        chunk(i)
                    chunk(NCH - 1, last=True)
                    for u in ((6,) if c.layer == 0 else (13, 14, 15)):
                        weigh(NCH - 1, u)
                    pe.wait_ge(t["p"], t.n("p", NCH * c.units))
                    if c.layer == 0:
                        for h in (POOL_HEADS[-1], DVE_HEADS[-1]):
                            key, count = summed(NCH - 1, h)
                            pe.wait_ge(t[key], t.n(key, count))
                        for h in range(8):
                            p, j = h // 2, h % 2
                            last = mm(score[0][64 * j:64 * j + 64, S * p:S * p + S], ones[:, 0:64], acc_p[:, h, :],
                                      start=True, stop=True, tile_position=(0, 64 * j))
                        last.then_inc(t["d"], 1)
                    else:
                        pe.wait_ge(t["osb"], t.n("osb", 2))
                        for k in range(2):
                            last = mm(score[0][:, 512 * k:512 * k + 512], den_pick[:], P[:, 0, 512 * k:512 * k + 512], start=True, stop=True)
                        last.then_inc(t["d"], 1)
                if c.layer == 0:
                    pe.wait_ge(a["wo"], 16)
                pe.wait_ge(a["bias"], 16 if c.layer == 0 else 16 * 21)
                pe.wait_ge(ATT[c.layer, 1]["o"], ATT[c.layer, 1].n("o", 4))
                for n in range(TT):
                    if n >= 2:
                        pe.wait_ge(a["res"], n - 1)
                    for k in range(4):
                        mm(bank[2 + n % 2][:, 0:D], oT[:, k, 128 * n:128 * n + 128], wout[:, k, :], start=(k == 0), stop=False)
                    mm(bank[2 + n % 2][:, 0:D], ones[0:1, :], row[0:1, 0:D], start=False, stop=True).then_inc(a["op"], 1)


            def local_attention():
                pe.wait_ge(la["w"], 192)
                step = [0]

                def project(pairs, out=None):
                    n = step[0]
                    if n >= 2:
                        pe.wait_ge(la["pe"], n - 1)
                    dst = bank[2 + n % 2][:] if out is None else out
                    width = pairs[0][1].free_size()
                    for k, (l, r) in enumerate(pairs):
                        last = mm(bank[2 + n % 2][:, 0:width], l, r, start=(k == 0), stop=(k == len(pairs) - 1))
                    last.then_inc(la["pj"], 1)
                    step[0] += 1

                pe.wait_ge(LN[1]["xT"], LN[1].n("xT", 2))
                for w in (0, 1):
                    for m in range(2):
                        project([(la_wqkv[:, w, f, 128 * m:128 * m + 128], xnT[:, f, :]) for f in range(2)])
                project([(la_wg[:, 0, f, :], xnT[:, f, :]) for f in range(2)])
                for t in range(TT):
                    project([(xnT[:, f, 128 * t:128 * t + 128], la_wqkv[:, 2, f, :]) for f in range(2)])
                pe.wait_ge(la["g"], 1)
                for b in range(B):
                    project([(la_wg[:, 1, f, :], la_xp[:, f, b, 0, :]) for f in range(2)])
                for b in range(B):
                    project([(la_xp[:, f, b].rearrange("p c n -> p (c n)"), la_wg[:, 2, f, :]) for f in range(2)])
                pe.wait_ge(la["pe"], 13)
                pe.wait_ge(la["gt"], 1)
                for t in range(TT):
                    for f in range(2):
                        last = mm(bank[2][:, 32 * t:32 * t + 32], la_QT[:, f, 128 * t:128 * t + 128], la_G[:, f, :],
                                  start=(f == 0), stop=(f == 1))
                last.then_inc(la["gt"], 1)
                pe.wait_ge(la["g"], 2)
                bufs = quads = 0
                for t in range(TT):
                    b, keys = t // 2, 128 * la_keys[t]
                    pe.wait_ge(la["qp"], t + 1)
                    hpb = 1024 // keys
                    for n in range(la_bufs[t]):
                        if bufs >= 2:
                            pe.wait_ge(la["sb"], bufs - 1)
                        for h in range(hpb):
                            hh = n * hpb + h
                            last = mm(score[bufs % 2][:, keys * h:keys * h + keys], la_q[:, hh, :],
                                      la_KT[:, hh // 8, b * S:b * S + keys], start=True, stop=True)
                        last.then_inc(la["s"], 1)
                        bufs += 1
                    if t:
                        pe.wait_ge(la["res"], t)
                    for h in range(NHG):
                        last = mm(bank[1][:, LAT * h:LAT * h + LAT], la_gq[:, h, :], la_GKT[:, b * LAT:b * LAT + LAT], start=True, stop=True)
                    last.then_inc(la["o"], 1)
                    pe.wait_ge(la["e"], t + 1)
                    taken = (sum((q + 1) // 2 for q in la_quads[:t]), sum(q // 2 for q in la_quads[:t]))
                    for n in range(la_quads[t]):
                        pe.wait_ge(la["pta" if n % 2 else "ptd"], taken[n % 2] + n // 2)
                        for k in range(4):
                            if n < la_quads[t] - 1:
                                blk = 4 * n + k
                                src = la_S[:, blk // la_keys[t], 128 * (blk % la_keys[t]):128 * (blk % la_keys[t]) + 128]
                            else:
                                src = la_LS[:, 2 * k:2 * k + 2, :].rearrange("p h n -> p (h n)")
                            last = nc.tensor.transpose(bank[2 + n % 2][:, 128 * k:128 * k + 128], src, ident[:])
                        last.then_inc(la["tr"], 1)
                        quads += 1
                    pe.wait_ge(la["ptd"], taken[0] + (la_quads[t] + 1) // 2)
                    pe.wait_ge(la["pta"], taken[1] + la_quads[t] // 2)
                    nk = la_keys[t]
                    for h in range(NHL):
                        for k in range(nk):
                            blk = h * nk + k
                            mm(bank[0][:, 17 * h:17 * h + 17], la_PT[:, 128 * blk:128 * blk + 128], la_V[:, 2 * b + k, h, :],
                               start=(k == 0), stop=(k == nk - 1))
                    for h in range(0, NHG, 2):
                        last = mm(bank[0][:, 272 + 17 * h:306 + 17 * h], la_LPT[:, 64 * h:64 * h + 128],
                                  la_GV[:, b, h:h + 2, :].rearrange("p h d -> p (h d)"), start=True, stop=True)
                    last.then_inc(la["o"], 1)
                    pe.wait_ge(la["rq"], t + 1)
                    nc.tensor.transpose(bank[1][:, 0:128], la_rq, ident[:]).then_inc(la["rt"], 1)
                    pe.wait_ge(la["rtc"], t + 1)
                    mm(bank[1][:, 256:512], la_rqT, la_rout, start=True, stop=True).then_inc(la["rem"], 1)
                    pe.wait_ge(la["cb"], t + 1)
                    for f in range(2):
                        last = nc.tensor.transpose(bank[1][:, 128 * f:128 * f + 128], la_cb[:, 128 * f:128 * f + 128], ident[:])
                    last.then_inc(la["ct"], 1)
                    pe.wait_ge(la["ctc"], t + 1)
                    for f in range(2):
                        last = mm(bank[1][:, 256:512], la_cT[:, 128 * f:128 * f + 128], la_wout[:, f, :], start=(f == 0), stop=(f == 1))
                    last.then_inc(la["out"], 1)

            def logits(g, n, w):
                pe.wait_ge(LN[n]["xT"], LN[n].n("xT", 2))
                for t in range(TT):
                    for f in range(2):
                        last = mm(bank[2][:, E * t:E * t + E], xnT[:, f, 128 * t:128 * t + 128], w[:, f, :], start=(f == 0), stop=(f == 1))
                last.then_inc(g["lp"], 1)

            def dense_mixture():
                pe.wait_ge(gm["w"], 48)
                logits(gm, 2, gate_w)
                nc.tensor.transpose(bank[3][:, 0:64], b1n, ident[0:64, 0:64]).then_inc(gm["bt"], 1)
                pe.wait_ge(gm["cT"], 1)
                for t in range(TT):
                    last = nc.tensor.transpose(bank[2][0:8, 128 * t:128 * t + 128], comb[:, t, :], ident[:])
                last.then_inc(gm["cTc"], 1)
                pe.wait_ge(gm["b2"], 1)
                for t in range(TT):
                    last = mm(score[0][:, D * t:D * t + D], combT[:, 128 * t:128 * t + 128], b2sb, start=True, stop=True)
                last.then_inc(gm["done"], 1)
                pe.wait_ge(gm["done"], 2)
                with pe.Fori(0, E) as e:
                    pe.wait_ge(em["w1l"], em.n("w1l", e + 1))
                    for m in range(FM):
                        if m < 2:
                            pe.wait_ge(em["g"], em.n("g", FM * e))
                        else:
                            pe.wait_ge(em["g"], em.n("g", FM * e + m - 1))
                        cols = slice(128 * m, 128 * m + 128)
                        three(bank[m % 2][:], [(w[:, f, cols], r[:, f, :]) for f in range(2)
                                               for w, r in ((w1_hi, c_hi), (w1_hi, c_lo), (w1_lo, c_hi))]).then_inc(em["h"], 1)
                    pe.wait_ge(em["w2l"], em.n("w2l", e + 1))
                    for t in range(TT):
                        if t < 2:
                            pe.wait_ge(em["acc"], em.n("acc", TT * e))
                        else:
                            pe.wait_ge(em["acc"], em.n("acc", TT * e + t - 1))
                        cols = slice(128 * t, 128 * t + 128)
                        for k in range(FM):
                            if t == 0:
                                pe.wait_ge(em["hl"], em.n("hl", FM * e + k + 1))
                            for n, (h, w) in enumerate(((h_hi, w2_hi), (h_hi, w2_lo), (h_lo, w2_hi))):
                                last = mm(bank[2 + t % 2][:, 0:D], h[:, k, cols], w[:, k, :],
                                          start=(k == 0 and n == 0), stop=(k == FM - 1 and n == 2))
                        last.then_inc(em["y"], 1)

            def rwkv():
                pe.wait_ge(rw["w"], 64)
                pe.wait_ge(LN[4]["xT"], LN[4].n("xT", 2))
                for n in range(4):
                    if n >= 2:
                        pe.wait_ge(rw["trc"], n - 1)
                    for f in range(2):
                        for o in range(2):
                            last = nc.tensor.transpose(bank[n % 2][:, 256 * f + 128 * o:256 * f + 128 * o + 128],
                                                       rw_nat[:, n, o, 128 * f:128 * f + 128], ident[:])
                    last.then_inc(rw["tr"], 1)
                pe.wait_ge(rw["trc"], 4)
                for n, (w, src) in enumerate(((0, rw_xk), (1, rw_xv), (2, rw_xr))):
                    pe.wait_ge(rw["mx"], n + 1)
                    for m in range(2):
                        dst = (score[0][:, 512 * m:512 * m + 512], score[1][:, 512 * m:512 * m + 512], bank[2 + m][:])[n]
                        for f in range(2):
                            last = mm(dst, rw_W[:, w, f, 128 * m:128 * m + 128], src[:, f].rearrange("p b t -> p (b t)"),
                                      start=(f == 0), stop=(f == 1))
                        last.then_inc(rw["pj"], 1)
                pe.wait_ge(rw["o"], 1)
                for t in range(TT):
                    if t >= 2:
                        pe.wait_ge(rw["res"], t - 1)
                    b, u = t // 2, t % 2
                    for f in range(2):
                        last = mm(bank[t % 2][:, 0:D], rw_out[:, f, b, 128 * u:128 * u + 128], rw_W[:, 3, f, :], start=(f == 0), stop=(f == 1))
                    last.then_inc(rw["out"], 1)

            def chunk_mixture():
                pe.wait_ge(cm["wr"], cm.n("wr", 16))
                pe.wait_ge(LN[5]["xT"], LN[5].n("xT", 2))
                for f in range(2):
                    last = nc.tensor.transpose(bank[3][:, 8 * f:8 * f + 8], wr_nat[:, 128 * f:128 * f + 128], ident[0:8, 0:8])
                last.then_inc(cm["tr"], 1)
                pe.wait_ge(cm["trc"], cm.n("trc", 1))
                logits(cm, 5, gate_w)
                pe.wait_ge(cm["c"], cm.n("c", 1))
                pe.wait_ge(cm["iota"], cm.n("iota", 1))
                for t in range(TT):
                    for k in range(t + 1):
                        mm(bank[3][:, 8 * t:8 * t + 8], ones[:] if k < t else before, comb[:, k, :], start=(k == 0), stop=(k == t))
                for k in range(TT):
                    last = mm(bank[3][:, 32:40], ones[:], comb[:, k, :], start=(k == 0), stop=(k == TT - 1))
                last.then_inc(cm["c"], 1)
                pe.wait_ge(cm["pw"], cm.n("pw", TT))
                for n in range(4):
                    f, half = n // 2, n % 2
                    for t in range(TT):
                        last = mm(score[n // 2][:, 512 * half:512 * half + 512], xn[:, t, 128 * f:128 * f + 128],
                                  PA[:, t, 512 * half:512 * half + 512], start=(t == 0), stop=(t == TT - 1))
                    last.then_inc(cm["pm"], 1)
                for e in range(E):
                    pe.wait_ge(cm["trc"], cm.n("trc", e))
                    for t in range(TT):
                        last = nc.tensor.transpose(bank[2 + e % 2][:, 128 * t:128 * t + 128], PW[:, t, 128 * e:128 * e + 128], ident[:])
                    last.then_inc(cm["tr"], 1)
                pe.wait_ge(cm["trc"], cm.n("trc", 1 + E))
                pe.wait_ge(cm["pmc"], cm.n("pmc", 4))
                with pe.Fori(0, E) as e:
                    pe.wait_ge(cm["w"], cm.n("w", 16 * e + 16))
                    for m in range(FM):
                        if m < 2:
                            pe.wait_ge(cm["g"], cm.n("g", FM * e))
                        else:
                            pe.wait_ge(cm["g"], cm.n("g", FM * e + m - 1))
                        for f in range(2):
                            last = mm(bank[m % 2][:, 0:128], cw1[:, f, 128 * m:128 * m + 128], permT[:, f, bass.ts(e, 128)],
                                      start=(f == 0), stop=(f == 1))
                        last.then_inc(cm["h"], 1)
                    pe.wait_ge(cm["g"], cm.n("g", FM * e + FM))
                    pe.wait_ge(cm["w2"], cm.n("w2", 16 * e + 16))
                    pe.wait_ge(cm["yc"], cm.n("yc", e))
                    for k in range(FM):
                        last = mm(bank[2][:, 0:D], hT[:, k, :], cw2[:, k, :], start=(k == 0), stop=(k == FM - 1))
                    last.then_inc(cm["y"], 1)
                pe.wait_ge(cm["yc"], cm.n("yc", E))
                for t in range(TT):
                    if t >= 2:
                        pe.wait_ge(cm["res"], cm.n("res", t - 1))
                    for e in range(E):
                        last = mm(bank[t % 2][:, 0:D], PWT[:, e, 128 * t:128 * t + 128], yS[:, e, :], start=(e == 0), stop=(e == E - 1))
                    last.then_inc(cm["s"], 1)

            signal_ahead(pe, "pe")
            pe.wait_ge(const_ready, 1)
            layer_norm(0)
            cross(X0, 0)
            stage_end(pe, 1)
            if upto >= 2:
                layer_norm(1)
                local_attention()
                stage_end(pe, 2)
            if upto >= 3:
                layer_norm(2)
                dense_mixture()
                stage_end(pe, 3)
            if upto >= 4:
                layer_norm(3)
                cross(X1, 3)
                stage_end(pe, 4)
            if upto >= 5:
                layer_norm(4)
                rwkv()
                stage_end(pe, 5)
            if upto >= 6:
                layer_norm(5)
                chunk_mixture()
                stage_end(pe, 6)

        @program.vector
        def _(dve):
            v = nc.vector
            chain = [0]

            def link(i):
                chain[0] += 1
                i.then_inc(dve_chain, 1)
                dve.wait_ge(dve_chain, chain[0])

            def layer_norm(n):
                ln = LN[n]
                for t in range(TT):
                    last = v.bn_stats(stats[:, t, :], x[:, t, :])
                link(last)
                for t in range(TT):
                    last = v.bn_aggr(mv[:, t, :], stats[:, t, :])
                link(last)
                v.tensor_scalar(mv[:, :, 1], mv[:, :, 1], EPS, None, ALU.add).then_inc(ln["var"], 1)
                dve.wait_ge(ln["std"], ln.n("std", 1))
                link(v.reciprocal(rstd[:], rstd[:]))
                for t in range(TT):
                    v.tensor_scalar(xn[:, t, :], x[:, t, :], mv[:, t, 0:1], rstd[:, t:t + 1], ALU.subtract, ALU.mult).then_inc(ln["xn"], 1)
                dve.wait_ge(ln["tr"], ln.n("tr", 1))
                v.tensor_copy(xnT[:, 1, :], bank[1][:]).then_inc(ln["xT"], 1)
                dve.wait_ge(ln["xT"], ln.n("xT", 2))

            def context_low(ph, f, i, src):
                dve.wait_ge(ph["ch"], ph.n("ch", 2 * i + f + 1))
                v.tensor_tensor(c_lo[:, f, :], src[:], c_hi[:, f, :].bitcast(F32), ALU.subtract).then_inc(ph["cl"], 1)

            def cross(c, stage):
                a = CA[c.layer]
                if c.layer == 0:
                    for n, (hi, lo) in enumerate(((wk_hi, wk_lo), (wv_hi, wv_lo))):
                        dve.wait_ge(a["w0"], n + 1)
                        v.tensor_tensor(lo, w_raw[:, n + 1], hi.bitcast(F32), ALU.subtract).then_inc(a["whl"], 1)
                else:
                    link(v.memset(bias[:, 4:8], 0.0))
                    v.engine_nop().then_inc(a["pad"], 1)
                    link(v.memset(wo_pad, 0.0))
                    dve.wait_ge(a["w"], 64)
                    for o in range(2):
                        last = v.tensor_copy(wo_pad[:, o, :].rearrange("p (h d) -> p h d", d=32)[:, :, 0:16],
                                             wo_nat[:, o, :].rearrange("p (h d) -> p h d", d=16))
                    last.then_inc(a["pad"], 1)
                    for n, (hi, lo) in enumerate(((wk_hi, wk_lo), (wv_hi, wv_lo))):
                        dve.wait_ge(a["w0"], n + 1)
                        v.tensor_tensor(lo[:, :, 0:256], bank[(n + 1) % 2][:].rearrange("p (f n) -> p f n", f=2),
                                        hi[:, :, 0:256].bitcast(F32), ALU.subtract).then_inc(a["whl"], 1)
                    dve.wait_ge(a["bias"], 16 * 21)
                for n in range(c.tiles):
                    dve.wait_ge(a["qp"], n + 1)
                    if c.layer == 0:
                        v.tensor_scalar(qT[:, n, :], bank[2 + n % 2][:], c.scale, None, ALU.mult).then_inc(a["q"], 1)
                    else:
                        v.tensor_scalar(qT[:, 2 + n, :], bank[2 + n % 2][:], bias[:, n:n + 1], c.scale, ALU.add, ALU.mult).then_inc(a["q"], 1)
                dve.wait_ge(a["q"], c.tiles)
                if c.layer == 1:
                    dve.wait_ge(a["wop"], 1)
                    v.tensor_copy(wout, score[0][:].rearrange("p (k n) -> p k n", k=4)).then_inc(a["wop"], 1)
                mask = mask_half if c.layer == 0 else mask_16th
                qt0 = 0 if c.layer == 0 else 2
                for b in range(B):
                    m, t = MAXP[c.layer, b], ATT[c.layer, b]
                    toks = slice(b * S, b * S + S)
                    for h in range(c.heads):
                        v.tensor_scalar(q_hi[:, h, :], qT[:, qt0 + h // c.hpt, toks], mask[:, h % c.hpt:h % c.hpt + 1], None,
                                        ALU.mult).then_inc(m["qh"], 1)
                    dve.wait_ge(m["qh"], m.n("qh", c.heads))
                    if c.layer == 1 and b == 0:
                        dve.wait_ge(a["clear"], 1)
                    for h in range(c.heads):
                        g = h // c.hpg
                        _, r = hidden_of(c, g)
                        rows = slice(r, r + c.rows)
                        v.scalar_tensor_tensor(out=q_lm[0:64, h, :] if c.layer == 0 else q_hh[block(g, 1), h, :],
                                               in0=qT[rows, qt0 + h // c.hpt, toks],
                                               scalar=mask[rows, h % c.hpt:h % c.hpt + 1], in1=q_hi[rows, h, :].bitcast(F32),
                                               op0=ALU.mult, op1=ALU.subtract).then_inc(m["ql"], 1)
                    def reduce(i, heads):
                        for h in heads:
                            if h in c.direct:
                                dve.wait_ge(m["s"], m.n("s", i * c.heads + h + 1))
                                v.tensor_reduce(mx[:, bass.ds(i, 1), 2 * h:2 * h + 2], score[h % 2][:].rearrange("p (q k) -> p q k", q=2),
                                                AX.X, ALU.max).then_inc(m["red"], 1)
                            else:
                                n = c.running.index(h)
                                if n == 0:
                                    dve.wait_ge(m["low"], m.n("low", 1))
                                dve.wait_ge(m["rm"], m.n("rm", (i - 1) * NR + n + 1))
                                dve.wait_ge(m["cp"], m.n("cp", i * NR + n + 1))
                                v.tensor_tensor(run_max[:, n, :], run_max[:, n, :], copied[:, n % 2, :], ALU.max).then_inc(m["rm"], 1)

                    def low_both(i):
                        for f in range(2):
                            context_low(m, f, i, bank[f])

                    low_both(0)
                    if c.layer == 1:
                        dve.sem_inc(m["rm"], NR)
                    order = list(range(c.heads)) if c.layer == 0 else [0] + [h for n in range(2, c.heads, 2) for h in (n, n - 1)] + [15]
                    ahead_of = 5 if c.layer == 0 else 10
                    with dve.Fori(0, NCH - 1) as i:
                        reduce(i, order[:ahead_of])
                        low_both(i + 1)
                        reduce(i, order[ahead_of:])
                    reduce(NCH - 1, order)
                    dve.wait_ge(m["red"], m.n("red", NCH * len(c.direct)))
                    if c.layer == 0:
                        v.tensor_reduce(mneg[:, 0:2 * c.heads], mx[:, :, 0:2 * c.heads].rearrange("p c h -> p h c"), AX.X, ALU.max,
                                        negate=True).then_inc(m["m"], 1)
                    else:
                        pair = mneg[:].rearrange("p (g s) -> p g s", s=4)
                        v.tensor_reduce(pair[:, :, 0:2], mx.rearrange("p c (g s) -> p g s c", s=4)[:, :, 0:2, :], AX.X, ALU.max, negate=True)
                        dve.wait_ge(m["rm"], m.n("rm", NCH * NR))
                        halves = run_max.rearrange("p h (q k) -> p (h q) k", q=2)
                        for width in (256, 128, 64):
                            link(v.tensor_tensor(halves[:, :, 0:width], halves[:, :, 0:width], halves[:, :, width:2 * width], ALU.max))
                        v.tensor_reduce(pair[:, :, 2:4], halves[:, :, 0:64].rearrange("p (g s) k -> p g s k", s=2), AX.X, ALU.max,
                                        negate=True).then_inc(m["m"], 1)
                    if c.layer == 0:
                        dve.sem_inc(t["accd"], len(DVE_HEADS) * KT)

                    def split(i, g):
                        n = i * c.groups + g
                        tile, r = hidden_of(c, g)
                        src = Kst[c.layer][r:r + c.rows, tile, bass.ts(i, CHUNK)]
                        if c.layer == 0:
                            high, rest = k_hl[g % 2][r:r + 64, :], k_hl[g % 2][64 - r:128 - r, :]
                        else:
                            high, rest = k_st[g % 4][block(g, 0), :], k_st[g % 4][block(g, 2), :]
                        dve.wait_ge(t["s"], t.n("s", (i * c.sets + g // c.gps - 1) * c.ups))
                        v.tensor_copy(high, src).then_inc(t["khi"], 1)
                        if c.layer == 1:
                            v.tensor_copy(k_st[g % 4][block(g, 1), :], src)
                        dve.wait_ge(t["khi"], t.n("khi", n + 1))
                        v.tensor_tensor(rest, src, high.bitcast(F32), ALU.subtract).then_inc(t["kl"], 1)

                    def values(i, k):
                        dve.wait_ge(t["vp"], t.n("vp", KT * i + k + 1))
                        if c.layer == 1:
                            dve.wait_ge(t["pfree"], t.n("pfree", c.units * i + k + 1))
                        elif k == 0:
                            dve.wait_ge(t["pfree"], t.n("pfree", c.units * i + 4))
                        if c.layer == 0:
                            v.tensor_copy(V[:, k, :], bank[3][:]).then_inc(t["v"], 1)
                        else:
                            v.tensor_copy(Vp[:, k, :, 0:16], bank[3][:, 0:256].rearrange("p (h d) -> p h d", h=16)).then_inc(t["v"], 1)

                    def sums(i, u):
                        dve.wait_ge(t["p"], t.n("p", i * 8 + u + 1))
                        for k in range(KT):
                            dve.wait_ge(t["accd"], t.n("accd", summed(i, u)[1] - KT + k))
                            v.tensor_tensor(acc_p[:, u, :], acc_p[:, u, :],
                                            P[:, u % 4, k * S:(k + 1) * S], ALU.add).then_inc(t["accd"], 1)

                    def begin(i):
                        if c.layer == 0:
                            for n in range(2):
                                context_low(t, n, i, bank[2])
                                split(i, n)
                        else:
                            split(i, 0), split(i, 1)
                            context_low(t, 0, i, bank[2]), context_low(t, 1, i, bank[2])

                    def chunk(i, last=False):
                        split(i, 2), split(i, 3)
                        for k in range(KT):
                            values(i, k)
                            if c.layer == 0 and k < 3:
                                split(i, 4 + k)
                        if c.layer == 0:
                            sums(i, 3), split(i, 7)
                        else:
                            for g in range(4, 8):
                                split(i, g)
                        if not last:
                            begin(i + 1)
                        if c.layer == 0:
                            sums(i, 5)

                    begin(0)
                    if c.layer == 0:
                        dve.wait_ge(t["z"], t.n("z", 1))
                    with dve.Fori(0, NCH - 1) as i:
                        chunk(i)
                    chunk(NCH - 1, last=True)
                    dve.wait_ge(t["d"], t.n("d", 1))
                    dve.wait_ge(t["pfree"], t.n("pfree", NCH * c.units + 4))
                    if c.layer == 0:
                        v.reciprocal(P[:, 1, :], score[0][:]).then_inc(t["rd"], 1)
                        dve.wait_ge(t["rd"], t.n("rd", 1))
                        for k in range(4):
                            v.tensor_tensor(oT[:, k, toks], bank[k // 2][:, S * (k % 2):S * (k % 2) + S], P[:, 1, S * k:S * k + S],
                                            ALU.mult).then_inc(t["o"], 1)
                    else:
                        v.reciprocal(P[:, 1, :], score[0][:]).then_inc(t["rd"], 1)
                        dve.wait_ge(t["rd"], t.n("rd", 1))
                        for k in range(4):
                            link(v.tensor_tensor(oT[:, k, toks], bank[k // 2][:, S * (k % 2):S * (k % 2) + S], P[:, 1, S * k:S * k + S],
                                                 ALU.mult))
                            v.tensor_scalar(oT[:, k, toks], oT[:, k, toks], bias[:, 4 + k:5 + k], None, ALU.add).then_inc(t["o"], 1)
                for n in range(TT):
                    dve.wait_ge(a["op"], n + 1)
                    v.tensor_tensor(x[:, n, :], bank[2 + n % 2][:, 0:D], x[:, n, :], ALU.add).then_inc(a["res"], 1)


            def local_attention():
                link(v.tensor_reduce(la_xs, xnT.rearrange("p f (n g) -> p f n g", g=GRP), AX.X, ALU.add))
                for c in range(2):
                    last = v.tensor_scalar(la_xp[:, :, :, c, :], la_xs.rearrange("p f (b n) -> p f b n", b=B), 1.0 / GRP, None, ALU.mult)
                last.then_inc(la["g"], 1)
                dve.wait_ge(la["w"], 192)
                link(v.memset(la_G, 0.0))
                for f in range(2):
                    for w in range(2):
                        last = v.tensor_scalar(la_G[:, f, 16 * w + 8 * f:16 * w + 8 * f + 8], mask_16th[:], la_gcol[:, f, w:w + 1], None, ALU.mult)
                last.then_inc(la["gt"], 1)
                dsts = [(la_QT[:, 0, :], 512), (la_QT[:, 1, :], 512), (la_KT[:, 0, :], 512), (la_KT[:, 1, :], 512), (la_GQT, 512)]
                dsts += [(la_V[:, t, :, 0:HD], 256) for t in range(TT)]
                dsts += [(la_GKT[:, 64 * b:64 * b + 64], 64) for b in range(B)]
                dsts += [(la_GV[:, b, :, 0:HD], 128) for b in range(B)]
                dve.wait_ge(la["msk"], 1)
                for n, (dst, width) in enumerate(dsts):
                    dve.wait_ge(la["pj"], n + 1)
                    src = bank[2 + n % 2][:, 0:width]
                    if n in (5, 6, 7, 8, 11, 12):
                        src = src.rearrange("p (h d) -> p h d", d=HD)
                    if n < 11:
                        last = v.tensor_copy(dst, src)
                    else:
                        for r in (0, 1):
                            last = v.tensor_copy(dst[64 * r:64 * r + 64, r::2, :], src[64 * r:64 * r + 64, r::2, :])
                    last.then_inc(la["pe"], 1)
                dve.wait_ge(la["pe"], 13)
                bufs = quads = 0
                for t in range(TT):
                    b, u, keys, nk = t // 2, t % 2, 128 * la_keys[t], la_keys[t]
                    if t:
                        dve.wait_ge(la["o"], 2 * t)
                    for h in range(NHL):
                        v.tensor_scalar(la_q[:, h, :], la_QT[:, h // 8, 128 * t:128 * t + 128], mask_16th[:, h % 8:h % 8 + 1], None, ALU.mult)
                    for h in range(NHG):
                        last = v.tensor_scalar(la_gq[:, h, :], la_GQT[:, 128 * t:128 * t + 128], mask_16th[:, h:h + 1], None, ALU.mult)
                    last.then_inc(la["qp"], 1)
                    hpb = 1024 // keys
                    for n in range(la_bufs[t]):
                        dve.wait_ge(la["s"], bufs + 1)
                        v.scalar_tensor_tensor(out=la_S[:, n * hpb:n * hpb + hpb, 0:keys],
                                               in0=score[bufs % 2][:].rearrange("p (h k) -> p h k", h=hpb), scalar=HD ** -0.5,
                                               in1=bc(la_mask[:, 256 - keys:256], 1, hpb), op0=ALU.mult, op1=ALU.add).then_inc(la["sb"], 1)
                        bufs += 1
                    dve.wait_ge(la["sb"], bufs)
                    v.tensor_reduce(la_m[:, 0:NHL], la_S[:, :, 0:keys], AX.X, ALU.max, negate=True).then_inc(la["m"], 1)
                    dve.wait_ge(la["o"], 2 * t + 1)
                    link(v.scalar_tensor_tensor(out=la_LS, in0=bank[1][:].rearrange("p (h n) -> p h n", h=NHG), scalar=HD ** -0.5,
                                                in1=bc(la_lmask[:, u, :], 1, NHG), op0=ALU.mult, op1=ALU.add))
                    v.tensor_reduce(la_m[:, NHL:], la_LS, AX.X, ALU.max, negate=True).then_inc(la["m"], 1)
                    for n in range(0, la_quads[t], 2):
                        dve.wait_ge(la["tr"], quads + n + 1)
                        dst = la_LPT if n == la_quads[t] - 1 else la_PT[:, 512 * n:512 * n + 512]
                        v.tensor_copy(dst, bank[2 + n % 2][:]).then_inc(la["ptd"], 1)
                    quads += la_quads[t]
                    dve.wait_ge(la["o"], 2 * t + 2)
                    if t == 0:
                        dve.wait_ge(la["g"], 2)
                    O = bank[0][:, 0:408].rearrange("p (h d) -> p h d", d=17)
                    link(v.reciprocal(la_r, O[:, :, 16]))
                    v.tensor_tensor(la_rq.rearrange("p (h d) -> p h d", d=HD), O[:, NHL:, 0:HD], bc(la_r[:, NHL:], 2, HD), ALU.mult).then_inc(la["rq"], 1)
                    link(v.tensor_tensor(la_rs, la_r[:, 0:NHL], la_gate[:, t, 0:NHL], ALU.mult))
                    link(v.tensor_tensor(la_cb.rearrange("p (h d) -> p h d", d=HD), O[:, 0:NHL, 0:HD], bc(la_rs, 2, HD), ALU.mult))
                    dve.wait_ge(la["rt"], t + 1)
                    v.tensor_copy(la_rqT, bank[1][:, 0:128]).then_inc(la["rtc"], 1)
                    dve.wait_ge(la["rem"], t + 1)
                    rem = P[:, 3, 256:512].rearrange("p (h d) -> p h d", d=HD)
                    link(v.tensor_tensor(rem, bank[1][:, 256:512].rearrange("p (h d) -> p h d", d=HD), bc(la_gate[:, t, NHL:], 2, HD), ALU.mult))
                    v.tensor_tensor(la_cb, la_cb, P[:, 3, 256:512], ALU.add).then_inc(la["cb"], 1)
                    dve.wait_ge(la["ct"], t + 1)
                    v.tensor_copy(la_cT, bank[1][:, 0:256]).then_inc(la["ctc"], 1)
                    dve.wait_ge(la["out"], t + 1)
                    v.tensor_tensor(x[:, t, :], bank[1][:, 256:512], x[:, t, :], ALU.add).then_inc(la["res"], 1)

            def top_two(g):
                dve.wait_ge(g["lp"], 1)
                link(v.tensor_copy(lg, bank[2][:, 0:E * TT].rearrange("p (t e) -> p t e", t=TT)))
                for t in range(TT):
                    last = v.max(top8[:, t, :], lg[:, t, :])
                link(last)
                for t in range(TT):
                    last = v.max_index(idx8[:, t, :], top8[:, t, :], lg[:, t, :])
                link(last)
                link(v.tensor_copy(idxf, idx8))
                v.tensor_tensor(tw[:, 0, :], top8[:, :, 1], top8[:, :, 0], ALU.subtract).then_inc(g["t"], 1)
                dve.wait_ge(g["ex"], 1)
                link(v.tensor_scalar(tw[:, 0, :], tw[:, 1, :], 1.0, None, ALU.add))
                link(v.reciprocal(tw[:, 0, :], tw[:, 0, :]))
                link(v.tensor_tensor(tw[:, 1, :], tw[:, 0, :], tw[:, 1, :], ALU.mult))

            def dense_mixture():
                dve.wait_ge(gm["bt"], 1)
                v.tensor_copy(b1T, bank[3][:, 0:64]).then_inc(gm["btc"], 1)
                for f in range(2):
                    last = v.tensor_copy(c_hi[:, f, :], xnT[:, f, :])
                link(last)
                last = v.tensor_tensor(c_lo[:], xnT, c_hi[:].bitcast(F32), ALU.subtract)
                link(last)
                top_two(gm)
                for t in range(TT):
                    for k in range(2):
                        last = v.tensor_scalar(ohtmp[:, k, t, :], iota8[:], idxf[:, t, k:k + 1], tw[:, k, t:t + 1], ALU.is_equal, ALU.mult)
                link(last)
                v.tensor_tensor(comb, ohtmp[:, 0], ohtmp[:, 1], ALU.add).then_inc(gm["cT"], 1)
                dve.wait_ge(gm["cTc"], 1)
                v.tensor_copy(combT, bank[2][0:8, :]).then_inc(gm["b2"], 1)
                dve.wait_ge(gm["done"], 1)
                v.tensor_tensor(x[:], score[0][:].rearrange("p (t d) -> p t d", t=TT), x[:], ALU.add).then_inc(gm["done"], 1)
                dve.wait_ge(gm["done"], 2)
                def low_w1(e):
                    dve.wait_ge(em["w1h"], em.n("w1h", e + 1))
                    v.tensor_tensor(w1_lo, w1raw, w1_hi.bitcast(F32), ALU.subtract).then_inc(em["w1l"], 1)

                def expert(e, last=False):
                    dve.wait_ge(em["y"], em.n("y", TT * e))
                    for m in range(FM):
                        dve.wait_ge(em["g"], em.n("g", FM * e + m + 1))
                        v.tensor_copy(h_hi[:, m, :], h32[:, m, :]).then_inc(em["hh"], 1)
                        dve.wait_ge(em["hh"], em.n("hh", FM * e + m + 1))
                        v.tensor_tensor(h_lo[:, m, :], h32[:, m, :], h_hi[:, m, :].bitcast(F32), ALU.subtract).then_inc(em["hl"], 1)
                        if m == 3:
                            dve.wait_ge(em["w2h"], em.n("w2h", e + 1))
                            v.tensor_tensor(w2_lo, w2raw, w2_hi.bitcast(F32), ALU.subtract).then_inc(em["w2l"], 1)
                    if not last:
                        low_w1(e + 1)
                    for t in range(TT):
                        dve.wait_ge(em["y"], em.n("y", TT * e + t + 1))
                        dve.wait_ge(em["acc"], em.n("acc", TT * e))
                        v.scalar_tensor_tensor(out=x[:, t, :], in0=bank[2 + t % 2][:, 0:D], scalar=comb[:, t, bass.ds(e, 1)],
                                               in1=x[:, t, :], op0=ALU.mult, op1=ALU.add).then_inc(em["acc"], 1)

                low_w1(0)
                with dve.Fori(0, E - 1) as e:
                    expert(e)
                expert(E - 1, last=True)

            def rwkv():
                full = lambda a: a.rearrange("p m b t -> p (m b t)")
                for n in range(4):
                    dve.wait_ge(rw["tr"], n + 1)
                    v.tensor_copy(rw_W[:, n], bank[n % 2][:].rearrange("p (f n) -> p f n", f=2)).then_inc(rw["trc"], 1)
                xt = xnT.rearrange("p f (b t) -> p f b t", b=B)
                v.memset(rw_xp[:, :, :, 0:1], 0.0)
                for f in range(2):
                    last = v.tensor_copy(rw_xp[:, f, :, 1:S], xt[:, f, :, 0:S - 1])
                link(last)
                link(v.tensor_tensor(full(rw_d), xnT.rearrange("p f t -> p (f t)"), full(rw_xp), ALU.subtract))
                dve.wait_ge(rw["v"], 160)
                for n, dst in enumerate((rw_xk, rw_xv, rw_xr)):
                    for f in range(2):
                        last = v.scalar_tensor_tensor(out=dst[:, f], in0=rw_d[:, f], scalar=rw_vec[:, 2 + n, f:f + 1],
                                                      in1=rw_xp[:, f], op0=ALU.mult, op1=ALU.add)
                    last.then_inc(rw["mx"], 1)
                dve.wait_ge(rw["we"], 1)
                link(v.tensor_scalar(rw_wexp, rw_wexp, -1.0, None, ALU.mult))
                v.memset(rw_o[:, :, :, 0:1], NEG)
                v.memset(rw_p[:, :, :, 0:1], 0.0)
                link(v.memset(rw_q[:, :, :, 0:1], 0.0))
                dve.wait_ge(rw["pj"], 4)
                v.tensor_copy(full(rw_k), score[0][:])
                link(v.tensor_copy(full(rw_v), score[1][:]))
                for m in range(2):
                    for b in range(B):
                        last = v.tensor_tensor_scan(rw_o[:, m, b, 1:S + 1], rw_wexp[:, m:m + 1].broadcast_to([128, S]), rw_k[:, m, b, :],
                                                    NEG, ALU.add, ALU.max)
                for m in range(2):
                    last = v.tensor_scalar(rw_Bc[:, m], rw_k[:, m], rw_vec[:, 1, m:m + 1], None, ALU.add)
                link(last)
                for m in range(2):
                    last = v.tensor_tensor(rw_no[:, m], rw_Bc[:, m], rw_o[:, m, :, 0:S], ALU.max)
                link(last)
                dve.wait_ge(rw["pj"], 6)
                for m in range(2):
                    v.tensor_tensor(rw_A[:, m], rw_o[:, m, :, 0:S], rw_no[:, m], ALU.subtract)
                    v.tensor_tensor(rw_Bc[:, m], rw_Bc[:, m], rw_no[:, m], ALU.subtract)
                    v.scalar_tensor_tensor(out=rw_A2[:, m], in0=rw_o[:, m, :, 0:S], scalar=rw_wexp[:, m:m + 1],
                                           in1=rw_o[:, m, :, 1:S + 1], op0=ALU.add, op1=ALU.subtract)
                    last = v.tensor_tensor(rw_B2[:, m], rw_k[:, m], rw_o[:, m, :, 1:S + 1], ALU.subtract)
                last.then_inc(rw["a"], 1)
                dve.wait_ge(rw["a2"], 1)
                link(v.tensor_tensor(full(rw_num), full(rw_B2), full(rw_v), ALU.mult))
                for m in range(2):
                    for b in range(B):
                        v.tensor_tensor_scan(rw_p[:, m, b, 1:S + 1], rw_A2[:, m, b, :], rw_num[:, m, b, :], 0.0, ALU.mult, ALU.add)
                        last = v.tensor_tensor_scan(rw_q[:, m, b, 1:S + 1], rw_A2[:, m, b, :], rw_B2[:, m, b, :], 0.0, ALU.mult, ALU.add)
                link(last)
                for m in range(2):
                    v.tensor_tensor(rw_num[:, m], rw_A[:, m], rw_p[:, m, :, 0:S], ALU.mult)
                    last = v.tensor_tensor(rw_den[:, m], rw_A[:, m], rw_q[:, m, :, 0:S], ALU.mult)
                link(last)
                v.tensor_tensor(full(rw_no), full(rw_Bc), full(rw_v), ALU.mult)
                link(v.tensor_tensor(full(rw_den), full(rw_den), full(rw_Bc), ALU.add))
                v.tensor_tensor(full(rw_num), full(rw_num), full(rw_no), ALU.add)
                link(v.reciprocal(full(rw_den), full(rw_den)))
                link(v.tensor_tensor(full(rw_num), full(rw_num), full(rw_den), ALU.mult))
                dve.wait_ge(rw["sr"], 2)
                v.tensor_tensor(full(rw_out), full(rw_num), full(rw_sr), ALU.mult).then_inc(rw["o"], 1)
                for t in range(TT):
                    dve.wait_ge(rw["out"], t + 1)
                    v.tensor_tensor(x[:, t, :], bank[t % 2][:, 0:D], x[:, t, :], ALU.add).then_inc(rw["res"], 1)

            def chunk_mixture():
                dve.wait_ge(cm["tr"], cm.n("tr", 1))
                v.tensor_copy(gate_w, bank[3][:, 0:16].rearrange("p (f e) -> p f e", f=2)).then_inc(cm["trc"], 1)
                top_two(cm)
                for t in range(TT):
                    for k in range(2):
                        last = v.tensor_scalar(ohtmp[:, k, t, :], iota8[:], idxf[:, t, k:k + 1], None, ALU.is_equal)
                link(last)
                v.tensor_tensor(comb, ohtmp[:, 0], ohtmp[:, 1], ALU.add).then_inc(cm["c"], 1)
                dve.wait_ge(cm["c"], cm.n("c", 2))
                link(v.tensor_copy(tot, bank[3][:, 32:40]))
                link(v.tensor_tensor_scan(incl, ones[:, 0:8], tot, 0.0, ALU.mult, ALU.add))
                link(v.tensor_tensor(incl, incl, tot, ALU.subtract))
                link(v.tensor_tensor(rank_e, bank[3][:, 0:32].rearrange("p (t e) -> p t e", t=TT), bc(incl, 1, TT), ALU.add))
                for k in range(2):
                    last = v.tensor_tensor(ohtmp[:, k], ohtmp[:, k], rank_e, ALU.mult)
                link(last)
                for k in range(2):
                    last = v.tensor_reduce(rank[:, k, :], ohtmp[:, k], AX.X, ALU.add)
                link(last)
                dve.wait_ge(cm["iota"], cm.n("iota", 1))
                for t in range(TT):
                    link(v.tensor_scalar(Ptmp[:, 0, :], iota_s, rank[:, 0, t:t + 1], None, ALU.is_equal))
                    v.scalar_tensor_tensor(out=PA[:, t, :], in0=iota_s, scalar=rank[:, 1, t:t + 1], in1=Ptmp[:, 0, :], op0=ALU.is_equal, op1=ALU.add)
                    link(v.tensor_scalar(Ptmp[:, 1, :], iota_s, rank[:, 1, t:t + 1], tw[:, 1, t:t + 1], ALU.is_equal, ALU.mult))
                    v.scalar_tensor_tensor(out=PW[:, t, :], in0=Ptmp[:, 0, :], scalar=tw[:, 0, t:t + 1], in1=Ptmp[:, 1, :],
                                           op0=ALU.mult, op1=ALU.add).then_inc(cm["pw"], 1)
                    dve.wait_ge(cm["pw"], cm.n("pw", t + 1))
                for n in range(4):
                    dve.wait_ge(cm["pm"], cm.n("pm", n + 1))
                    v.tensor_copy(permT[:, n // 2, 512 * (n % 2):512 * (n % 2) + 512], score[n // 2][:, 512 * (n % 2):512 * (n % 2) + 512]).then_inc(cm["pmc"], 1)
                for e in range(E):
                    dve.wait_ge(cm["tr"], cm.n("tr", e + 2))
                    v.tensor_copy(PWT[:, e, :], bank[2 + e % 2][:]).then_inc(cm["trc"], 1)
                with dve.Fori(0, E) as e:
                    dve.wait_ge(cm["y"], cm.n("y", e + 1))
                    v.tensor_copy(yS[:, bass.ds(e, 1), :].rearrange("p a d -> p (a d)"), bank[2][:, 0:D]).then_inc(cm["yc"], 1)
                for t in range(TT):
                    dve.wait_ge(cm["s"], cm.n("s", t + 1))
                    v.tensor_tensor(x[:, t, :], bank[t % 2][:, 0:D], x[:, t, :], ALU.add).then_inc(cm["res"], 1)

            signal_ahead(dve, "dve")
            dve.wait_ge(const_ready, 1)
            dve.wait_ge(x_in, 16)
            layer_norm(0)
            cross(X0, 0)
            stage_end(dve, 1)
            if upto >= 2:
                layer_norm(1)
                local_attention()
                stage_end(dve, 2)
            if upto >= 3:
                layer_norm(2)
                dense_mixture()
                stage_end(dve, 3)
            if upto >= 4:
                layer_norm(3)
                cross(X1, 3)
                stage_end(dve, 4)
            if upto >= 5:
                layer_norm(4)
                rwkv()
                stage_end(dve, 5)
            if upto >= 6:
                layer_norm(5)
                chunk_mixture()
                stage_end(dve, 6)


_INS = ['x', 'ctx_1024', 'L0_xattn_Wq', 'L0_xattn_Wk', 'L0_xattn_Wv', 'L0_xattn_Wo', 'L0_xattn_bo', 'L0_attn_wq', 'L0_attn_wk',
        'L0_attn_wv', 'L0_attn_wgq', 'L0_attn_wgk', 'L0_attn_wgv', 'L0_attn_r_out_w', 'L0_attn_gate_local_w',
        'L0_attn_gate_remote_w', 'L0_attn_w_out', 'L0_ffn_gate_w', 'L0_ffn_w1', 'L0_ffn_b1', 'L0_ffn_w2', 'L0_ffn_b2',
        'L1_xattn_wq', 'L1_xattn_bq', 'L1_xattn_wk', 'L1_xattn_bk', 'L1_xattn_wv', 'L1_xattn_bv', 'L1_xattn_wo', 'L1_xattn_bo',
        'L1_attn_w', 'L1_attn_u', 'L1_attn_mix_k', 'L1_attn_mix_v', 'L1_attn_mix_r', 'L1_attn_Wk', 'L1_attn_Wv', 'L1_attn_Wr',
        'L1_attn_Wo', 'L1_ffn_Wr', 'L1_ffn_W1', 'L1_ffn_W2']


def kernel(**inputs):
    import concourse.bacc as _bacc
    from concourse.bass_utils import run_bass_kernel_spmd as _run

    nc = _bacc.Bacc("TRN2", target_bir_lowering=False, num_devices=1)
    arrays, aps = {}, {}
    for name in _INS:
        a = np.ascontiguousarray(inputs[name])
        arrays[f"in_{name}"] = a
        aps[name] = nc.dram_tensor(f"in_{name}", a.shape, mybir.dt.from_np(a.dtype), kind="ExternalInput").ap()
    out = nc.dram_tensor("out_x", (B, S, D), F32, kind="ExternalOutput").ap()
    perceiver(nc, aps, out)
    r = _run(nc, [arrays], core_ids=[0])
    return r.results[0]["out_x"]
```

```python
import numpy as np
import concourse.bass as bass
from concourse import mybir
from contextlib import ExitStack

F32 = mybir.dt.float32
BF16 = mybir.dt.bfloat16
F32R = mybir.dt.float32r
U32 = mybir.dt.uint32
ALU = mybir.AluOpType
ACT = mybir.ActivationFunctionType
AX = mybir.AxisListType

B, S, D = 2, 256, 256
TOK = B * S
TT = TOK // 128
CTX = 4096
CHUNK = 512
NCH = CTX // CHUNK
KT = CHUNK // 128
EPS = 1e-5
NEG = -1e30
STAGES = 6
BLOCK_ENGINES = 4


class Cross:

    def __init__(self, layer, heads, dim):
        self.layer, self.heads, self.dim = layer, heads, dim
        self.hid = heads * dim
        self.tiles = self.hid // 128
        self.hpt = heads // self.tiles
        self.rows = 64 if dim == 64 else 32
        self.groups = self.hid // self.rows
        self.hpg = heads // self.groups
        self.scale = float(dim) ** -0.5
        self.units = heads if dim == 64 else heads // 4 * KT
        self.gps = 1 if dim == 64 else 2
        self.sets = self.groups // self.gps
        self.ups = self.units // self.sets
        self.running = 0 if dim == 64 else heads


X0 = Cross(0, 8, 64)
X1 = Cross(1, 16, 16)


def perceiver(nc, ins, out):
    ctx = ExitStack()
    with ctx:
        def sb(name, shape, dt=F32):
            return ctx.enter_context(nc.sbuf_tensor(name, shape, dt))

        def sem(name):
            return ctx.enter_context(nc.semaphore(name))

        ident = sb("ident", [128, 128])
        ones = sb("ones", [128, 128])
        mask_half = sb("mask_half", [128, 2])
        mask_16th = sb("mask_16th", [128, 8])
        den_pick = sb("den_pick", [128, 128])
        iota8 = sb("iota8", [128, 8])
        zeros = sb("zeros", [128, 128], BF16)
        x = sb("x", [128, TT, D])
        q_hi = sb("q_hi", [128, 16, S], F32R)
        q_hh = sb("q_hh", [128, 16, S], F32R)
        q_lm = sb("q_lm", [128, 16, S], F32R)
        k_st = [sb(f"k_st{i}", [128, CHUNK], F32R) for i in range(4)]
        k_hl, k_h1 = k_st[0:2], k_st[2:4]
        c_hi = sb("c_hi", [128, 2, CHUNK], F32R)
        c_lo = sb("c_lo", [128, 2, CHUNK], F32R)
        k_max = [sb(f"k_max{i}", [128, CHUNK], F32R) for i in range(2)]
        w_split = sb("w_split", [128, 4, 1024], F32R)
        wk_hi, wk_lo, wv_hi, wv_lo = (w_split[:, n, :].rearrange("p (f n) -> p f n", f=2) for n in range(4))
        shift = sb("shift", [32, 128], F32R)
        c_in = sb("c_in", [128, KT, D])
        qT = sb("qT", [128, 4, TOK])
        V = sb("V", [128, KT, 512])
        P = sb("P", [128, 4, 1024])
        arena = sb("arena", [128, 20480])
        xn, xnT = P[:, 0, :].rearrange("p (t d) -> p t d", t=TT), P[:, 1, :].rearrange("p (f t) -> p f t", f=2)
        stats = sb("stats", [128, TT, 6])
        mv = sb("mv", [128, TT, 2])
        rstd = sb("rstd", [128, TT])
        mneg = sb("mneg", [128, 32])
        bias = sb("bias", [128, 16])
        row = sb("row", [1, 256])

        bank = [ctx.enter_context(nc.psum_tensor(f"bank{i}", [128, 512], F32)) for i in (0, 1)]
        score = [ctx.enter_context(nc.psum_tensor(f"score{i}", [128, 1024], F32)) for i in range(2)]
        bank += [ctx.enter_context(nc.psum_tensor(f"bank{i}", [128, 512], F32)) for i in (6, 7)]

        stage_done = sem("stage_done")
        const_ready = sem("const_ready")
        pool_chain, dve_chain, act_chain = sem("pool_chain"), sem("dve_chain"), sem("act_chain")
        x_in = sem("x_in")
        out_stored = sem("out_stored")
        def phase(name, keys):
            return {k: sem(f"{name}_{k}") for k in keys.split()}

        CA = {c.layer: phase(f"ca{c.layer}", "w w0 whl qp q wo wop op res bias" + (" wT wTc pad clear" if c.layer else "")) for c in (X0, X1)}
        class Phase:

            def __init__(self, sems, base):
                self.sems, self.base = sems, base

            def __getitem__(self, key):
                return self.sems[key]

            def n(self, key, count):
                return count + self.base[key]

        POOL_HEADS, DVE_HEADS = (0, 1, 2, 4, 6, 7), (3, 5)

        def summed(i, h):
            key, mine = ("acc", POOL_HEADS) if h in POOL_HEADS else ("accd", DVE_HEADS)
            return key, (i * len(mine) + mine.index(h) + 1) * KT

        def max_counts(c, b):
            return dict(qh=c.heads, qhh=2 * c.groups, ql=c.heads, ctx=16 * NCH, tr=2 * NCH, ch=2 * NCH, cl=2 * NCH,
                        kp=c.tiles * NCH, kev=c.tiles * NCH, s=c.heads * NCH, red=c.heads * NCH,
                        cp=c.running * NCH, rm=c.running * NCH, low=c.layer,
                        m=1, mt=1, mr=1, md=16 if c.layer == 0 else 128)

        def att_counts(c, b):
            own = (dict(z=1, acc=len(POOL_HEADS) * KT * NCH, accd=len(DVE_HEADS) * KT * NCH, osb=0) if c.layer == 0
                   else dict(z=1 - b, acc=0, accd=0, osb=2))
            return dict(ctx=16 * NCH, tr=2 * NCH, ch=2 * NCH, cl=2 * NCH, vp=KT * NCH, v=KT * NCH, khi=c.groups * NCH,
                        kl=c.groups * NCH, kone=c.groups * NCH if c.layer == 0 else 0, s=c.units * NCH,
                        p=c.units * NCH, pfree=4 + c.units * NCH, d=1, rd=1, o=4, **own)

        ahead = {e: [] for e in ("sp", "pe", "act", "dve", "pool")}
        signals = dict(qh="dve", qhh="pool", ql="dve", ctx="sp", tr="pe", ch="act", cl="dve", kp="pe", kev="act", s="pe",
                       red="dve", cp="act", rm="dve", low="pool", m="dve", mt="pe", mr="act", md="act", z="pool", vp="pe", v="dve", khi="dve", kl="dve", kone="act",
                       p="act", pfree="pe", acc="pool", accd="dve", d="pe", rd="dve", o="dve", osb="act")

        def once(name, looped, rest=""):
            sems = {k: sem(f"{name}_{k}") for k in (*looped, *rest.split())}
            for k, e in looped.items():
                ahead[e].append(sems[k])
            return Phase(sems, {k: int(k in looped) for k in sems})

        def signal_ahead(eng, name):
            for s in ahead[name]:
                eng.sem_inc(s, 1)

        def runs(name, counts):
            sems, base, made = {k: sem(f"{name}_{k}") for k in counts(X0, 0)}, {k: 1 for k in counts(X0, 0)}, {}
            for k in sems:
                ahead[signals[k]].append(sems[k])
            for c in (X0, X1):
                for b in range(B):
                    credit = {"s": c.hpt, "rm": c.running, "cp": c.running, "red": c.heads} if name == "max" else {"s": c.ups, **(dict(
                        acc=len(POOL_HEADS) * KT, accd=len(DVE_HEADS) * KT) if c.layer == 0 else {})}
                    made[c.layer, b] = Phase(sems, {k: n + credit.get(k, 0) for k, n in base.items()})
                    for k, total in counts(c, b).items():
                        base[k] += total + credit.get(k, 0)
            return made

        ln_counts = dict(var=1, std=1, xn=TT, tr=1, xT=2)
        ln_sems = {k: sem(f"ln_{k}") for k in ln_counts}
        LN = [Phase(ln_sems, {k: n * total for k, total in ln_counts.items()}) for n in range(6)]
        MAXP, ATT = runs("max", max_counts), runs("att", att_counts)

        program = ctx.enter_context(nc.Block())

        def stage_end(eng, n):
            eng.drain().then_inc(stage_done, 1)
            eng.wait_ge(stage_done, BLOCK_ENGINES * n)

        def hidden_of(c, g):
            return divmod(c.rows * g, 128)

        TURNS = {0: (6, 7), 1: (12, 13)}

        def block(g, n):
            r = 32 * ((g + n) % 4)
            return slice(r, r + 32)

        Kst = {c.layer: arena[:, 0:c.tiles * CTX].rearrange("p (t k) -> p t k", t=c.tiles) for c in (X0, X1)}
        acc_p = arena[:, 16384:18432].rearrange("p (h q) -> p h q", h=8)
        mx = arena[:, 16384:16384 + NCH * 32].rearrange("p (c h) -> p c h", c=NCH)
        NR = X1.running
        run_max = arena[:, 8192:8192 + 256 * NR].bitcast(BF16).rearrange("p (h n) -> p h n", h=NR)
        copied = arena[:, 8192 + 256 * NR:8192 + 256 * (NR + 2)].bitcast(BF16).rearrange("p (s n) -> p s n", s=2)

        def max_buffer(c, h, qt):
            a, b = (h % 2, qt) if c.layer == 0 else (qt, h % 2)
            return score[a][:, 512 * b:512 * b + 512]
        oT = arena[:, 18432:20480].rearrange("p (k t) -> p k t", k=4)
        w_raw = arena[:, 0:3072].rearrange("p (w f n) -> p w f n", w=3, f=2)
        w_nat = arena[:, 4096:5632].rearrange("p (w o n) -> p w o n", w=3, o=2)
        wo_nat = c_in[:, 0:2, :]
        wo_pad = V[:, :, :].rearrange("p a n -> p (a n)")[:, 0:1024].rearrange("p (o k) -> p o k", o=2)
        wout = qT[:, 0:2, :].rearrange("p a t -> p (a t)").rearrange("p (k n) -> p k n", k=4)
        Vp = V[:, :, :].rearrange("p a (h d) -> p a h d", h=16)

        def bc(ap, axis, n):
            new = ap.unsqueeze(axis)
            shape = list(new.shape)
            shape[axis] = n
            return new.broadcast_to(shape)


        NHL, NHG, HD, LAT = 16, 8, 16, 64
        GRP = S // LAT
        la = {k: sem("la_" + k) for k in
              "w msk pj pe gt g qp s sb m e tr ptd pta o rq rt rtc rem cb ct ctc out res".split()}
        la_wqkv = arena[:, 0:1536].rearrange("p (w f n) -> p w f n", w=3, f=2)
        la_wg = arena[:, 1536:2304].rearrange("p (w f n) -> p w f n", w=3, f=2)
        la_rout = arena[:, 2304:2560]
        la_wout = arena[:, 2560:3072].rearrange("p (f n) -> p f n", f=2)
        la_KT = arena[:, 3072:4096].rearrange("p (f t) -> p f t", f=2)
        la_QT = arena[:, 4096:5120].rearrange("p (f t) -> p f t", f=2)
        la_GQT, la_GKT = arena[:, 5120:5632], arena[:, 5632:5760]
        la_gate = arena[:, 5760:5888].rearrange("p (t h) -> p t h", t=TT)
        la_V = arena[:, 5888:6976].rearrange("p (t h d) -> p t h d", t=TT, h=NHL)
        la_GV = arena[:, 6976:7248].rearrange("p (b h d) -> p b h d", b=B, h=NHG)
        la_q = arena[:, 7248:9296].rearrange("p (h q) -> p h q", h=NHL)
        la_gq = arena[:, 9296:10320].rearrange("p (h q) -> p h q", h=NHG)
        la_S = [V[:, :, :].rearrange("p a n -> p (a n)").rearrange("p (h k) -> p h k", h=NHL),
                arena[:, 10320:14416].rearrange("p (h k) -> p h k", h=NHL)]
        la_PT = arena[:, 14416:18512]
        la_mask = arena[:, 18512:18768]
        la_lmask = arena[:, 18768:18896].rearrange("p (u n) -> p u n", u=2)
        la_m = [arena[:, 18896:18920], arena[:, 18960:18984]]
        la_r = arena[:, 18920:18944]
        la_rs = arena[:, 18944:18960]
        la_cb, la_cT = arena[:, 18992:19248], arena[:, 19248:19504]
        la_rq, la_rqT = arena[:, 19504:19632], arena[:, 19632:19760]
        la_xp = arena[:, 19760:20272].rearrange("p (f b c n) -> p f b c n", f=2, b=B, c=2)
        la_xs = qT[:, 0, 0:256].rearrange("p (f n) -> p f n", f=2)
        la_LS = [w.rearrange("p (h n) -> p h n", h=NHG) for w in (P[:, 2, 0:512], P[:, 3, 512:1024])]
        la_LPT = P[:, 2, 512:1024]
        la_G = P[:, 3, 0:64].rearrange("p (f h) -> p f h", f=2)
        la_gcol = bias[:, 0:4].rearrange("p (f w) -> p f w", f=2)
        la_keys = [1 if t % 2 == 0 else 2 for t in range(TT)]
        la_bufs = [NHL * k * 128 // 1024 for k in la_keys]
        la_quads = [NHL * k // 4 + 1 for k in la_keys]

        la_o_latent = [1, 2, 4, 6]
        la_o_values = [3, 5, 7, 8]

        def upto_t(counts, t):
            return sum(counts[:t])

        E, F = 8, 1024
        FM = F // 128
        gm = {k: sem("gm_" + k) for k in "w lp t ex cT cTc b2 done bt btc".split()}
        em = once("em", dict(w="sp", w2="sp", w1h="act", w1l="dve", w2h="act", w2l="dve", h="pe", g="act", hh="dve", hl="dve", y="pe", acc="dve"))
        cm = once("cm", dict(a0="sp", a1="sp", b0="sp", b1="sp", h="pe", g="act", y="pe", yc="dve"), "lp t ex c xh xl pa pw pm pmc tr trc s res iota wr")
        gate_w = arena[:, 0:16].rearrange("p (f e) -> p f e", f=2)
        lg = arena[:, 16:48].rearrange("p (t e) -> p t e", t=TT)
        top8 = arena[:, 48:80].rearrange("p (t e) -> p t e", t=TT)
        idx8 = arena[:, 80:112].bitcast(U32).rearrange("p (t e) -> p t e", t=TT)
        idxf = arena[:, 112:144].rearrange("p (t e) -> p t e", t=TT)
        tw = arena[:, 144:152].rearrange("p (k t) -> p k t", k=2)
        comb = arena[:, 152:184].rearrange("p (t e) -> p t e", t=TT)
        ohtmp = arena[:, 184:248].rearrange("p (k t e) -> p k t e", k=2, t=TT)
        rank_e = arena[:, 248:280].rearrange("p (t e) -> p t e", t=TT)
        rank = arena[:, 280:288].rearrange("p (k t) -> p k t", k=2)
        tot = arena[:, 288:320]
        incl = arena[:, 320:352]
        combT = arena[0:8, 512:1024]
        b2sb = arena[0:8, 1024:1280]
        b1n = arena[0:64, 1280:1408]
        b1T = arena[:, 1408:1472]
        wr_nat = arena[0:8, 1472:1728]
        w1raw = arena[:, 2048:4096].rearrange("p (f n) -> p f n", f=2)
        w2raw = arena[:, 4096:6144].rearrange("p (k n) -> p k n", k=FM)
        h32 = arena[:, 6144:10240].rearrange("p (m t) -> p m t", m=FM)
        w1_hi, w1_lo = (w_split[:, 2 * n:2 * n + 2, :] for n in range(2))
        w2_hi, w2_lo = (q_lm[:, 8 * n:8 * n + 8, :] for n in range(2))
        h_hi = q_hi[:].rearrange("p h q -> p (h q)").rearrange("p (m t) -> p m t", m=FM)
        h_lo = q_hh[:].rearrange("p h q -> p (h q)").rearrange("p (m t) -> p m t", m=FM)

        rw = {k: sem("rw_" + k) for k in "w v we tr trc mx pj sr a a2 o out res".split()}
        rw_nat = arena[:, 0:2048].rearrange("p (w o n) -> p w o n", w=4, o=2)
        rw_W = arena[:, 2048:4096].rearrange("p (w f n) -> p w f n", w=4, f=2)
        rw_xp, rw_d, rw_xk, rw_xv, rw_xr, rw_k, rw_v, rw_sr = (
            arena[:, 4096 + 1024 * n:5120 + 1024 * n].rearrange("p (m b t) -> p m b t", m=2, b=B) for n in range(8))
        rw_o, rw_p, rw_q = (arena[:, 12288 + 1028 * n:13316 + 1028 * n].rearrange("p (m b t) -> p m b t", m=2, b=B) for n in range(3))
        rw_no, rw_A, rw_Bc = (arena[:, 15372 + 1024 * n:16396 + 1024 * n].rearrange("p (m b t) -> p m b t", m=2, b=B) for n in range(3))
        rw_A2, rw_B2 = rw_xp, rw_d
        rw_num, rw_den, rw_out = rw_xk, rw_xv, rw_xr
        rw_vec = bias[:, 0:10].rearrange("p (n f) -> p n f", n=5)
        rw_wexp = bias[:, 10:12]

        SL = 2 * TOK
        slots = [arena[:, 2048 + 4096 * n:6144 + 4096 * n] for n in range(2)]
        cw1 = [w[:, 0:2048].rearrange("p (f n) -> p f n", f=2) for w in slots]
        cw2 = [w[:, 2048:4096].rearrange("p (k n) -> p k n", k=FM) for w in slots]
        PA = q_lm[:].rearrange("p (t a) q -> p t (a q)", t=TT)
        xn_hi, xn_lo = (c[:].rearrange("p a n -> p (a n)").rearrange("p (t d) -> p t d", t=TT) for c in (c_hi, c_lo))
        PW = arena[:, 10240:14336].rearrange("p (t s) -> p t s", t=TT)
        PWT = arena[:, 14336:18432].rearrange("p (e t) -> p e t", e=E)
        Ptmp = arena[:, 18432:20480].rearrange("p (n s) -> p n s", n=2)
        permT = qT[:, :, :].rearrange("p a t -> p (a t)").rearrange("p (f s) -> p f s", f=2)
        hT = [h.rearrange("p (m s) -> p m s", m=FM) for h in (c_in[:, :, :].rearrange("p a t -> p (a t)"), P[:, 1, :])]
        yS = V[:, :, :].rearrange("p a t -> p (a t)").rearrange("p (e d) -> p e d", e=E)
        iota_s = P[:, 2, :]
        before = P[:, 3, 0:128]

        @program.sync
        def _(sp):
            signal_ahead(sp, "sp")
            sp.dma_start(x[:], ins["x"].rearrange("b (u p) d -> p (b u) d", p=128)).then_inc(x_in, 16)

            def cross(c, stage):
                a = CA[c.layer]
                if c.layer == 0:
                    for n, w in enumerate(("Wq", "Wk", "Wv")):
                        sp.dma_start(w_raw[:, n], ins[f"L0_xattn_{w}"].rearrange("(f p) n -> p f n", p=128)).then_inc(a["w"], 16)
                    sp.dma_start(row[0:1, 0:D], ins["L0_xattn_bo"].rearrange("(a n) -> a n", a=1)).then_inc(a["bias"], 16)
                else:
                    sp.wait_ge(stage_done, BLOCK_ENGINES * stage)
                    for n, w in enumerate(("wq", "wk", "wv")):
                        sp.dma_start(w_nat[:, n], ins[f"L1_xattn_{w}"].rearrange("(o p) n -> p o n", p=128)).then_inc(a["w"], 16)
                    sp.dma_start(wo_nat, ins["L1_xattn_wo"].rearrange("(o p) n -> p o n", p=128)).then_inc(a["w"], 16)
                    sp.dma_start(row[0:1, 0:D], ins["L1_xattn_bo"].rearrange("(a n) -> a n", a=1)).then_inc(a["bias"], 16)
                    for n, w in enumerate(("bq", "bk")):
                        for f in range(2):
                            sp.dma_start(bias[:, 2 * n + f:2 * n + f + 1],
                                         ins[f"L1_xattn_{w}"][128 * f:128 * f + 128].rearrange("(p a) -> p a", a=1)).then_inc(a["bias"], 16)
                    sp.wait_ge(a["pad"], 1)
                    for g in range(4):
                        for j in range(4):
                            h = 4 * g + j
                            sp.dma_start(bias[32 * j:32 * j + 16, 4 + g:5 + g],
                                         ins["L1_xattn_bv"][16 * h:16 * h + 16].rearrange("(p a) -> p a", a=1)).then_inc(a["bias"], 16)
                for b in range(B):
                    chunks = ins["ctx_1024"][b].rearrange("(c k p) d -> c p k d", k=KT, p=128)
                    m, t = MAXP[c.layer, b], ATT[c.layer, b]
                    for ph in (m, t):
                        if ph is m and b == 0 and c.layer == 1:
                            sp.wait_ge(a["pad"], 2)
                        if ph is m and b == 1:
                            sp.wait_ge(ATT[c.layer, 0]["tr"], ATT[c.layer, 0].n("tr", 2 * NCH))
                        if ph is t:
                            sp.wait_ge(m["tr"], m.n("tr", 2 * NCH))
                        with sp.Fori(0, NCH) as i:
                            sp.wait_ge(ph["tr"], ph.n("tr", 2 * i))
                            sp.dma_start(c_in[:], chunks[bass.ds(i, 1), :, :, :].rearrange("a p k d -> p (a k) d")).then_inc(ph["ctx"], 16)
                    if b == 1 and c.layer == 0:
                        sp.wait_ge(MAXP[0, 1]["ql"], MAXP[0, 1].n("ql", c.heads))
                        sp.dma_start(wout, ins["L0_xattn_Wo"].rearrange("(k p) n -> p k n", p=128)).then_inc(a["wo"], 16)


            def stage_free(n):
                sp.wait_ge(stage_done, BLOCK_ENGINES * n)

            def local_attention():
                stage_free(1)
                for n, w in enumerate(("wq", "wk", "wv")):
                    sp.dma_start(la_wqkv[:, n], ins[f"L0_attn_{w}"].rearrange("(f p) n -> p f n", p=128)).then_inc(la["w"], 16)
                for n, w in enumerate(("wgq", "wgk", "wgv")):
                    sp.dma_start(la_wg[:, n], ins[f"L0_attn_{w}"].rearrange("(f p) n -> p f n", p=128)).then_inc(la["w"], 16)
                sp.dma_start(la_rout, ins["L0_attn_r_out_w"]).then_inc(la["w"], 16)
                sp.dma_start(la_wout, ins["L0_attn_w_out"].rearrange("(f p) n -> p f n", p=128)).then_inc(la["w"], 16)
                for n, w in enumerate(("gate_local_w", "gate_remote_w")):
                    for f in range(2):
                        sp.dma_start(la_gcol[:, f, n:n + 1],
                                     ins[f"L0_attn_{w}"][8 * f:8 * f + 8, :].rearrange("h (d a) -> (h d) a", a=1)).then_inc(la["w"], 16)

            def dense_mixture():
                stage_free(2)
                sp.dma_start(gate_w, ins["L0_ffn_gate_w"].rearrange("(f p) e -> p f e", p=128)).then_inc(gm["w"], 16)
                sp.dma_start(b2sb, ins["L0_ffn_b2"]).then_inc(gm["w"], 16)
                sp.dma_start(b1n, ins["L0_ffn_b1"].rearrange("e (m p) -> (e m) p", p=128)).then_inc(gm["w"], 16)
                w1d = ins["L0_ffn_w1"].rearrange("e (f p) n -> e p f n", p=128)
                w2d = ins["L0_ffn_w2"].rearrange("e (k p) n -> e p k n", p=128)
                with sp.Fori(0, E) as e:
                    sp.wait_ge(em["w1l"], em.n("w1l", e))
                    sp.dma_start(w1raw, w1d[bass.ds(e, 1)].rearrange("a p f n -> p (a f) n")).then_inc(em["w"], 16)
                    sp.wait_ge(em["w2l"], em.n("w2l", e))
                    sp.dma_start(w2raw, w2d[bass.ds(e, 1)].rearrange("a p k n -> p (a k) n")).then_inc(em["w2"], 16)

            def rwkv():
                stage_free(4)
                for n, w in enumerate(("Wk", "Wv", "Wr", "Wo")):
                    sp.dma_start(rw_nat[:, n], ins[f"L1_attn_{w}"].rearrange("(o p) n -> p o n", p=128)).then_inc(rw["w"], 16)
                for n, w in enumerate(("w", "u", "mix_k", "mix_v", "mix_r")):
                    for f in range(2):
                        sp.dma_start(rw_vec[:, n, f:f + 1], ins[f"L1_attn_{w}"][128 * f:128 * f + 128].rearrange("(p a) -> p a", a=1)).then_inc(rw["v"], 16)

            def first_weights(e, n):
                w1d = ins["L1_ffn_W1"].rearrange("e (f p) n -> e p f n", p=128)
                sp.dma_start(cw1[n], w1d[bass.ds(e, 1)].rearrange("a p f n -> p (a f) n")).then_inc(cm[f"a{n}"], 16)

            def second_weights(e, n):
                w2d = ins["L1_ffn_W2"].rearrange("e (k p) n -> e p k n", p=128)
                sp.dma_start(cw2[n], w2d[bass.ds(e, 1)].rearrange("a p k n -> p (a k) n")).then_inc(cm[f"b{n}"], 16)

            def chunk_mixture():
                stage_free(5)
                sp.dma_start(wr_nat, ins["L1_ffn_Wr"]).then_inc(cm["wr"], 16)
                for n in range(2):
                    first_weights(n, n), second_weights(n, n)

                def first(e, n):
                    sp.wait_ge(cm["h"], cm.n("h", 2 * (e - 1)))
                    first_weights(e, n)

                def second(e, n):
                    sp.wait_ge(cm["y"], cm.n("y", e - 1))
                    second_weights(e, n)

                first(2, 0)
                with sp.Fori(0, E // 2 - 2) as i:
                    first(i * 2 + 3, 1), second(i * 2 + 2, 0)
                    first(i * 2 + 4, 0), second(i * 2 + 3, 1)
                first(E - 1, 1), second(E - 2, 0), second(E - 1, 1)

            cross(X0, 0)
            local_attention()
            dense_mixture()
            cross(X1, 3)
            rwkv()
            chunk_mixture()
            sp.wait_ge(stage_done, BLOCK_ENGINES * STAGES)
            sp.dma_start(out.rearrange("b (u p) d -> p (b u) d", p=128), x[:]).then_inc(out_stored, 16)
            sp.wait_ge(out_stored, 16)

        @program.gpsimd
        def _(pool):
            chain = [0]

            def link(i):
                chain[0] += 1
                i.then_inc(pool_chain, 1)
                pool.wait_ge(pool_chain, chain[0])

            signal_ahead(pool, "pool")
            link(pool.memset(ident[:], 0.0))
            link(pool.affine_select(out=ident[:], in_=ident[:], compare_op=ALU.not_equal, fill=1.0,
                                    base=0, pattern=[[-1, 128]], channel_multiplier=1))
            link(pool.memset(ones[:], 1.0))
            link(pool.memset(zeros[:], 0.0))
            for tile, width in ((mask_half, 64), (mask_16th, 16)):
                n = 128 // width
                link(pool.memset(tile[:], 1.0))
                link(pool.affine_select(out=tile[:], in_=tile[:], compare_op=ALU.is_ge, fill=0.0,
                                        base=0, pattern=[[-width, n]], channel_multiplier=1))
                link(pool.affine_select(out=tile[:], in_=tile[:], compare_op=ALU.is_gt, fill=0.0,
                                        base=width, pattern=[[width, n]], channel_multiplier=-1))
            link(pool.memset(den_pick[:], 0.0))
            link(pool.affine_select(out=den_pick[:].rearrange("p (j d) -> p j d", j=4),
                                    in_=den_pick[:].rearrange("p (j d) -> p j d", j=4),
                                    compare_op=ALU.not_equal, fill=1.0, base=-16,
                                    pattern=[[-32, 4], [0, 32]], channel_multiplier=1))
            link(pool.iota(iota8[:], pattern=[[1, 8]], base=0, channel_multiplier=0,
                           allow_small_or_imprecise_dtypes=True))
            for i in range(2):
                pool.memset(k_h1[i][64:65, :].bitcast(F32), 1.0)
            pool.engine_nop().then_inc(const_ready, 1)

            def cross(c, stage):
                for b in range(B):
                    t = ATT[c.layer, b]
                    if c.layer == 1 and b == 0:
                        link(pool.memset(q_hh[:].bitcast(F32), 0.0))
                        for g in range(4):
                            link(pool.memset(k_st[g][block(g, 3), :].bitcast(F32), 0.0))
                            link(pool.memset(k_st[g][block(g, 3).start:block(g, 3).start + 1, :].bitcast(F32), 1.0))
                        pool.engine_nop().then_inc(CA[1]["clear"], 1)
                    if c.layer == 1:
                        if b == 1:
                            pool.wait_ge(MAXP[1, 0]["m"], MAXP[1, 0].n("m", 1))
                        pool.memset(run_max, -3e38).then_inc(MAXP[1, b]["low"], 1)
                        pool.wait_ge(MAXP[1, b]["low"], MAXP[1, b].n("low", 1))
                    m, copies = MAXP[c.layer, b], 0
                    for g in range(c.groups):
                        _, r = hidden_of(c, g)
                        h0 = c.hpg * g
                        pool.wait_ge(m["qh"], m.n("qh", h0 + c.hpg))
                        if b == 1 and g == 0:
                            pool.wait_ge(ATT[c.layer, 0]["s"], ATT[c.layer, 0].n("s", NCH * c.units))
                        for dst in (slice(0, 64), slice(64, 128)) if c.layer == 0 else (block(g, 0), block(g, 2)):
                            pool.tensor_copy(q_hh[dst, h0:h0 + c.hpg, :],
                                             q_hi[r:r + c.rows, h0:h0 + c.hpg, :].bitcast(F32)).then_inc(m["qhh"], 1)
                            copies += 1
                            pool.wait_ge(m["qhh"], m.n("qhh", copies))
                    if c.layer == 0:
                        if b == 1:
                            pool.wait_ge(ATT[0, 0]["d"], ATT[0, 0].n("d", 1))
                        pool.sem_inc(t["acc"], len(POOL_HEADS) * KT)
                        pool.wait_ge(MAXP[0, b]["m"], MAXP[0, b].n("m", 1))
                        pool.memset(acc_p, 0.0).then_inc(t["z"], 1)
                    if c.layer == 1 and b == 0:
                        pool.wait_ge(CA[1]["wop"], 1)
                        link(pool.memset(V[:], 0.0))
                        pool.memset(Vp[:, :, :, 16:17], 1.0).then_inc(t["z"], 1)
                    if c.layer == 1:
                        continue
                    pool.wait_ge(t["z"], t.n("z", 1))
                    with pool.Fori(0, NCH) as i:
                        for u in POOL_HEADS:
                            pool.wait_ge(t["p"], t.n("p", i * 8 + u + 1))
                            for k in range(KT):
                                pool.wait_ge(t["acc"], t.n("acc", summed(i, u)[1] - KT + k))
                                pool.tensor_tensor(acc_p[:, u, :], acc_p[:, u, :],
                                                   P[:, u % 4, k * S:(k + 1) * S], ALU.add).then_inc(t["acc"], 1)

            def local_attention():
                diag, off = la_mask[:, 128:256], la_mask[:, 0:128]
                link(pool.memset(la_mask, 0.0))
                link(pool.affine_select(out=diag, in_=diag, compare_op=ALU.is_ge, fill=NEG, base=0,
                                        pattern=[[-1, 128]], channel_multiplier=1))
                link(pool.affine_select(out=diag, in_=diag, compare_op=ALU.is_gt, fill=NEG, base=64,
                                        pattern=[[1, 128]], channel_multiplier=-1))
                link(pool.affine_select(out=off, in_=off, compare_op=ALU.is_gt, fill=NEG, base=-64,
                                        pattern=[[1, 128]], channel_multiplier=-1))
                link(pool.memset(la_lmask, 0.0))
                link(pool.affine_select(out=la_lmask, in_=la_lmask, compare_op=ALU.is_ge, fill=NEG, base=0,
                                        pattern=[[128, 2], [-GRP, LAT]], channel_multiplier=1))
                pool.memset(la_V[:, :, :, HD:HD + 1], 1.0)
                link(pool.memset(la_GV, 0.0))
                for r in (0, 1):
                    last = pool.memset(la_GV[64 * r:64 * r + 64, :, r::2, HD:HD + 1], 1.0)
                last.then_inc(la["msk"], 1)

            def chunk_mixture():
                link(pool.iota(iota_s, pattern=[[1, SL]], base=0, channel_multiplier=0, allow_small_or_imprecise_dtypes=True))
                link(pool.memset(before, 1.0))
                pool.affine_select(out=before, in_=before, compare_op=ALU.is_gt, fill=0.0, base=0,
                                   pattern=[[1, 128]], channel_multiplier=-1).then_inc(cm["iota"], 1)

            pool.wait_ge(const_ready, 1)
            cross(X0, 0)
            stage_end(pool, 1)
            local_attention()
            stage_end(pool, 2)
            stage_end(pool, 3)
            cross(X1, 3)
            stage_end(pool, 4)
            stage_end(pool, 5)
            chunk_mixture()
            stage_end(pool, 6)

        @program.scalar
        def _(act):
            chain = [0]

            def link(i):
                chain[0] += 1
                i.then_inc(act_chain, 1)
                act.wait_ge(act_chain, chain[0])

            def layer_norm(n):
                ln = LN[n]
                act.wait_ge(ln["var"], ln.n("var", 1))
                act.activation(rstd[:], mv[:, :, 1], ACT.Sqrt).then_inc(ln["std"], 1)
                act.wait_ge(ln["tr"], ln.n("tr", 1))
                act.activation(xnT[:, 0, :], bank[0][:], ACT.Copy).then_inc(ln["xT"], 1)

            def context_high(c, ph, f, i, dst):
                act.wait_ge(ph["tr"], ph.n("tr", 2 * i + f + 1))
                act.activation(c_hi[:, f, :], dst[:], ACT.Copy).then_inc(ph["ch"], 1)

            def cross(c, stage):
                a = CA[c.layer]
                if c.layer == 0:
                    act.wait_ge(a["w"], 48)
                    srcs = [w_raw[:, 1], w_raw[:, 2]]
                    for n, (src, hi) in enumerate(zip(srcs, (wk_hi, wv_hi))):
                        act.activation(hi, src, ACT.Copy).then_inc(a["w0"], 1)
                else:
                    for n in range(3):
                        act.wait_ge(a["wT"], n + 1)
                        pt = bank[n % 2]
                        if n == 0:
                            act.activation(w_raw[:, 0, 0, :], pt[:], ACT.Copy).then_inc(a["wTc"], 1)
                        else:
                            hi = (wk_hi, wv_hi)[n - 1]
                            act.activation(hi[:, :, 0:256], pt[:].rearrange("p (f n) -> p f n", f=2), ACT.Copy).then_inc(a["w0"], 1)
                for b in range(B):
                    m, t = MAXP[c.layer, b], ATT[c.layer, b]
                    if b == 1:
                        act.wait_ge(ATT[c.layer, 0]["vp"], ATT[c.layer, 0].n("vp", KT * NCH))
                    def high(i):
                        act.wait_ge(m["kp"], m.n("kp", c.tiles * i))
                        for f in range(2):
                            context_high(c, m, f, i, bank[f])

                    def keep(i, tiles):
                        for n in tiles:
                            act.wait_ge(m["kp"], m.n("kp", c.tiles * i + n + 1))
                            act.wait_ge(m["s"], m.n("s", (c.tiles * i + n - 1) * c.hpt))
                            src = bank[2 + n % 2][:]
                            dst = Kst[c.layer][:, n, bass.ts(i, CHUNK)]
                            if c.layer == 0:
                                act.activation(dst, src, ACT.Copy)
                                act.activation(k_max[n % 2][:], src, ACT.Copy).then_inc(m["kev"], 1)
                            else:
                                act.activation(dst, src, ACT.Identity, bias=bias[:, 2 + n:3 + n])
                                act.activation(k_max[n % 2][:], src, ACT.Identity, bias=bias[:, 2 + n:3 + n]).then_inc(m["kev"], 1)

                    def copy_out(i, heads):
                        for h in heads if c.layer == 1 else ():
                            act.wait_ge(m["s"], m.n("s", i * c.heads + h + 1))
                            act.wait_ge(m["rm"], m.n("rm", i * NR + h - 1))
                            act.activation(copied[:, h % 2, :], max_buffer(c, h, 1), ACT.Copy).then_inc(m["cp"], 1)

                    def chunk(i, last=False):
                        keep(i, range(1, c.tiles))
                        copy_out(i, range(8))
                        if not last:
                            high(i + 1)
                            copy_out(i, range(8, 14))
                            keep(i + 1, range(1))
                            copy_out(i, range(14, 16))
                        else:
                            copy_out(i, range(8, 16))

                    if c.layer == 1:
                        act.sem_inc(m["cp"], NR)
                    high(0)
                    keep(0, range(1))
                    with act.Fori(0, NCH - 1) as i:
                        chunk(i)
                    chunk(NCH - 1, last=True)
                    act.wait_ge(m["mt"], m.n("mt", 1))
                    act.activation(shift[0:2 * c.heads, :], bank[0][0:2 * c.heads, 0:128], ACT.Copy).then_inc(m["mr"], 1)
                    act.wait_ge(m["mr"], m.n("mr", 1))
                    if c.layer == 0:
                        act.dma_start(q_lm[64:65, 0:c.heads, :].rearrange("a h q -> a (h q)").bitcast(F32),
                                     shift[0:2 * c.heads, :].bitcast(F32)).then_inc(m["md"], 16)
                    else:
                        for g in range(c.groups):
                            r = block(g, 3).start
                            act.dma_start(q_hh[r:r + 1, 2 * g:2 * g + 2, :].rearrange("a h q -> a (h q)").bitcast(F32),
                                         shift[4 * g:4 * g + 4, :].bitcast(F32)).then_inc(m["md"], 16)
                    def keys(i, g):
                        tile, r = hidden_of(c, g)
                        act.activation(k_h1[g % 2][0:64, :], Kst[0][r:r + 64, tile, bass.ts(i, CHUNK)], ACT.Copy).then_inc(t["kone"], 1)

                    def chunk(i, last=False):
                        for u in range(c.units):
                            n = i * c.units + u
                            act.wait_ge(t["s"], t.n("s", n + 1))
                            act.wait_ge(t["pfree"], t.n("pfree", n + 1))
                            if c.layer == 0:
                                key, count = summed(i if u >= 4 else i - 1, (u - 4) % 8)
                                act.wait_ge(t[key], t.n(key, count))
                            act.activation(P[:, u % 4, :], score[u % 2][:], ACT.Exp).then_inc(t["p"], 1)
                            if c.layer == 0 and u < 6:
                                keys(i, u + 2)
                            elif c.layer == 0 and not last:
                                keys(i + 1, u - 6)
                            if u in TURNS[c.layer] and not last:
                                if u == TURNS[c.layer][0]:
                                    act.wait_ge(t["vp"], t.n("vp", KT * i + KT))
                                context_high(c, t, u - TURNS[c.layer][0], i + 1, bank[2])

                    for f in range(2):
                        context_high(c, t, f, 0, bank[2])
                    if c.layer == 0:
                        keys(0, 0)
                        keys(0, 1)
                    with act.Fori(0, NCH - 1) as i:
                        chunk(i)
                    chunk(NCH - 1, last=True)
                    if c.layer == 1:
                        act.wait_ge(t["pfree"], t.n("pfree", NCH * c.units + 4))
                        for k in range(2):
                            act.activation(P[:, 0, 512 * k:512 * k + 512], bank[k][:], ACT.Copy).then_inc(t["osb"], 1)


            def local_attention():
                act.wait_ge(la["gt"], 2)
                act.activation(la_gate, bank[2][:, 0:128].rearrange("p (t h) -> p t h", t=TT), ACT.Sigmoid).then_inc(la["g"], 1)
                for t in range(TT):
                    keys, quads = 128 * la_keys[t], upto_t(la_quads, t)
                    act.wait_ge(la["m"], 2 * t + 2)
                    for h in range(NHL):
                        last = act.activation(la_S[t % 2][:, h, 0:keys], la_S[t % 2][:, h, 0:keys], ACT.Exp, bias=la_m[t % 2][:, h:h + 1])
                    for h in range(NHG):
                        last = act.activation(la_LS[t % 2][:, h, :], la_LS[t % 2][:, h, :], ACT.Exp, bias=la_m[t % 2][:, NHL + h:NHL + h + 1])
                    last.then_inc(la["e"], 1)
                    for n in range(1, la_quads[t], 2):
                        act.wait_ge(la["tr"], quads + n + 1)
                        dst = la_LPT if n == la_quads[t] - 1 else la_PT[:, 512 * n:512 * n + 512]
                        act.activation(dst, bank[2 + n % 2][:], ACT.Copy).then_inc(la["pta"], 1)

            def dense_mixture():
                act.wait_ge(gm["t"], 1)
                act.activation(tw[:, 1, :], tw[:, 0, :], ACT.Exp).then_inc(gm["ex"], 1)
                def high_w1(e):
                    act.wait_ge(em["w"], em.n("w", 16 * e + 16))
                    act.wait_ge(em["h"], em.n("h", FM * e))
                    act.activation(w1_hi, w1raw, ACT.Copy).then_inc(em["w1h"], 1)

                def expert(e, last=False):
                    for m in range(FM):
                        act.wait_ge(em["h"], em.n("h", FM * e + m + 1))
                        act.wait_ge(em["hl"], em.n("hl", FM * e))
                        act.activation(h32[:, m, :], bank[m % 2][:], ACT.Gelu, bias=b1T[:, bass.ds(e * FM + m, 1)]).then_inc(em["g"], 1)
                        if m == 1:
                            act.wait_ge(em["w2"], em.n("w2", 16 * e + 16))
                            act.wait_ge(em["y"], em.n("y", TT * e))
                            act.activation(w2_hi, w2raw, ACT.Copy).then_inc(em["w2h"], 1)
                    if not last:
                        high_w1(e + 1)

                high_w1(0)
                with act.Fori(0, E - 1) as e:
                    expert(e)
                expert(E - 1, last=True)

            def rwkv():
                act.wait_ge(rw["v"], 160)
                act.activation(rw_wexp, rw_vec[:, 0, :], ACT.Exp).then_inc(rw["we"], 1)
                act.wait_ge(rw["pj"], 6)
                for m in range(2):
                    act.activation(rw_sr[:, m].rearrange("p b t -> p (b t)"), bank[2 + m][:], ACT.Sigmoid).then_inc(rw["sr"], 1)
                act.wait_ge(rw["a"], 1)
                act.activation(rw_A[:], rw_A[:], ACT.Exp)
                act.activation(rw_Bc[:], rw_Bc[:], ACT.Exp)
                act.activation(rw_A2[:], rw_A2[:], ACT.Exp)
                act.activation(rw_B2[:], rw_B2[:], ACT.Exp).then_inc(rw["a2"], 1)

            def chunk_mixture():
                act.wait_ge(LN[5]["xn"], LN[5].n("xn", TT))
                act.activation(xn_hi, xn, ACT.Copy).then_inc(cm["xh"], 1)
                act.wait_ge(cm["t"], cm.n("t", 1))
                act.activation(tw[:, 1, :], tw[:, 0, :], ACT.Exp).then_inc(cm["ex"], 1)
                for n in range(4):
                    act.wait_ge(cm["pm"], cm.n("pm", n + 1))
                    act.activation(permT[:, n // 2, 512 * (n % 2):512 * (n % 2) + 512], score[n // 2][:, 512 * (n % 2):512 * (n % 2) + 512],
                                   ACT.Copy).then_inc(cm["pmc"], 1)

                def hidden(e, n, first=False):
                    if not first:
                        act.wait_ge(cm["y"], cm.n("y", e - 1))
                    for half in range(2):
                        act.wait_ge(cm["h"], cm.n("h", 2 * e + half + 1))
                        act.activation(hT[n][:, 4 * half:4 * half + 4, :].rearrange("p m s -> p (m s)"), bank[half][:], ACT.Gelu).then_inc(cm["g"], 1)

                hidden(0, 0, first=True)
                hidden(1, 1, first=True)
                with act.Fori(1, E // 2) as i:
                    for n in range(2):
                        hidden(i * 2 + n, n)

            signal_ahead(act, "act")
            act.wait_ge(const_ready, 1)
            layer_norm(0)
            cross(X0, 0)
            stage_end(act, 1)
            layer_norm(1)
            local_attention()
            stage_end(act, 2)
            layer_norm(2)
            dense_mixture()
            stage_end(act, 3)
            layer_norm(3)
            cross(X1, 3)
            stage_end(act, 4)
            layer_norm(4)
            rwkv()
            stage_end(act, 5)
            layer_norm(5)
            chunk_mixture()
            stage_end(act, 6)

        @program.tensor
        def _(pe):
            mm = nc.tensor.matmul

            def layer_norm(n):
                ln = LN[n]
                pe.wait_ge(ln["xn"], ln.n("xn", TT))
                for f in range(2):
                    for t in range(TT):
                        last = nc.tensor.transpose(bank[f][:, 128 * t:128 * t + 128], xn[:, t, 128 * f:128 * f + 128], ident[:])
                last.then_inc(ln["tr"], 1)

            def turn_chunk(ph, f, i, dst):
                if f == 0:
                    pe.wait_ge(ph["ctx"], ph.n("ctx", 16 * i + 16))
                for k in range(KT):
                    last = nc.tensor.transpose(dst[:, 128 * k:128 * k + 128], c_in[:, k, 128 * f:128 * f + 128], ident[:])
                last.then_inc(ph["tr"], 1)

            def three(dst, pairs):
                for n, (l, r) in enumerate(pairs):
                    last = mm(dst, l, r, start=(n == 0), stop=(n == len(pairs) - 1))
                return last

            def cross(c, stage):
                a = CA[c.layer]
                if c.layer == 1:
                    pe.wait_ge(a["w"], 64)
                    pe.wait_ge(LN[3]["xT"], LN[3].n("xT", 2))
                    for n in range(3):
                        if n >= 2:
                            pe.wait_ge(a["wTc"], 1)
                        for f in range(2):
                            for o in range(2):
                                last = nc.tensor.transpose(bank[n % 2][:, 256 * f + 128 * o:256 * f + 128 * o + 128],
                                                           w_nat[:, n, o, 128 * f:128 * f + 128], ident[:])
                        last.then_inc(a["wT"], 1)
                else:
                    pe.wait_ge(a["w"], 48)
                    pe.wait_ge(LN[0]["xT"], LN[0].n("xT", 2))
                wq = w_raw[:, 0] if c.layer == 0 else w_raw[:, 0, 0, :].rearrange("p (f n) -> p f n", f=2)
                for n in range(c.tiles):
                    if n >= 2:
                        pe.wait_ge(a["q"], n - 1)
                    for f in range(2):
                        last = mm(bank[2 + n % 2][:], wq[:, f, 128 * n:128 * n + 128], xnT[:, f, :], start=(f == 0), stop=(f == 1))
                    last.then_inc(a["qp"], 1)
                if c.layer == 1:
                    pe.wait_ge(a["pad"], 2)
                    for k in range(4):
                        for o in range(2):
                            last = nc.tensor.transpose(score[0][:, 256 * k + 128 * o:256 * k + 128 * o + 128],
                                                       wo_pad[:, o, 128 * k:128 * k + 128], ident[:])
                    last.then_inc(a["wop"], 1)
                for b in range(B):
                    m, t = MAXP[c.layer, b], ATT[c.layer, b]
                    pe.sem_inc(m["s"], c.hpt)
                    pe.wait_ge(m["qh"], m.n("qh", c.heads))
                    if b == 0:
                        pe.wait_ge(a["whl"], 2)
                        pe.wait_ge(a["q"], c.tiles)
                        if c.layer == 1:
                            pe.wait_ge(a["wop"], 2)
                    if b == 1:
                        pe.wait_ge(ATT[c.layer, 0]["o"], ATT[c.layer, 0].n("o", 4))
                    def turn_both(i):
                        pe.wait_ge(m["cl"], m.n("cl", 2 * i))
                        turn_chunk(m, 0, i, bank[0])
                        turn_chunk(m, 1, i, bank[1])

                    def project(i, n):
                        if n == 0:
                            pe.wait_ge(m["cl"], m.n("cl", 2 * i + 2))
                        if n < 2:
                            pe.wait_ge(m["kev"], m.n("kev", c.tiles * i))
                        else:
                            pe.wait_ge(m["kev"], m.n("kev", c.tiles * i + n - 1))
                        cols = slice(128 * n, 128 * n + 128)
                        pairs = [(w[:, f, cols], v[:, f, :]) for f in range(2)
                                 for w, v in ((wk_hi, c_hi), (wk_hi, c_lo), (wk_lo, c_hi))]
                        three(bank[2 + n % 2][:], pairs).then_inc(m["kp"], 1)

                    def maxima(i, n, heads):
                        pe.wait_ge(m["kev"], m.n("kev", c.tiles * i + n + 1))
                        for j in heads:
                            h = n * c.hpt + j
                            pe.wait_ge(m["red"], m.n("red", i * c.heads + h - 1))
                            for qt in range(2):
                                if c.layer == 1 and qt == 1:
                                    pe.wait_ge(m["cp"], m.n("cp", i * c.heads + h - 1))
                                last = mm(max_buffer(c, h, qt), q_hi[:, h, 128 * qt:128 * qt + 128],
                                          k_max[n % 2][:], start=True, stop=True)
                            last.then_inc(m["s"], 1)

                    def chunk(i, last=False):
                        for n in range(1, c.tiles):
                            project(i, n)
                            maxima(i, n - 1, range(c.hpt))
                        if last:
                            maxima(i, c.tiles - 1, range(c.hpt))
                        else:
                            turn_both(i + 1)
                            maxima(i, c.tiles - 1, range(c.hpt - 1) if c.layer == 0 else range(c.hpt - 2))
                            project(i + 1, 0)
                            maxima(i, c.tiles - 1, range(c.hpt - 1, c.hpt) if c.layer == 0 else range(c.hpt - 2, c.hpt))

                    turn_both(0)
                    project(0, 0)
                    with pe.Fori(0, NCH - 1) as i:
                        chunk(i)
                    chunk(NCH - 1, last=True)
                    pe.wait_ge(m["m"], m.n("m", 1))
                    nc.tensor.transpose(bank[0][0:2 * c.heads, 0:128], mneg[:, 0:2 * c.heads], ident[:]).then_inc(m["mt"], 1)
                    def turn(i, f):
                        pe.wait_ge(t["cl"], t.n("cl", 2 * i + f))
                        turn_chunk(t, f, i, bank[2])

                    turn(0, 0), turn(0, 1)
                    pe.wait_ge(m["mr"], m.n("mr", 1))
                    pe.sem_inc(t["s"], c.ups)
                    pe.sem_inc(t["pfree"], 4)
                    for k in range(2):
                        for n in range(4):
                            mm(bank[k][:, 128 * n:128 * n + 128], zeros[:], zeros[:], start=(n == 0), stop=False, skip_group_check=True)
                    pe.wait_ge(m["md"], m.n("md", 16 if c.layer == 0 else 128))
                    pe.wait_ge(m["ql"], m.n("ql", c.heads))
                    pe.wait_ge(m["qhh"], m.n("qhh", 2 * c.groups))
                    if c.layer == 1 and b == 0:
                        pe.wait_ge(t["z"], t.n("z", 1))
                    def weigh(i, u):
                        if c.layer == 0:
                            pe.wait_ge(t["p"], t.n("p", i * 8 + u + 2))
                            if u == 0:
                                pe.wait_ge(t["v"], t.n("v", KT * i + KT))
                            for k in range(KT):
                                for j in range(2):
                                    p = u // 2
                                    last = mm(bank[p // 2][64 * j:64 * j + 64, S * (p % 2):S * (p % 2) + S],
                                              V[:, k, 64 * (u + j):64 * (u + j) + 64], P[:, (u + j) % 4, S * k:S * k + S],
                                              start=False, stop=False, skip_group_check=True, tile_position=(0, 64 * j))
                            last.then_inc(t["pfree"], 2)
                        else:
                            g, k = u // KT, u % KT
                            pe.wait_ge(t["p"], t.n("p", i * 16 + u + 1))
                            pe.wait_ge(t["v"], t.n("v", KT * i + k + 1)) if u < 4 else None
                            for j in range(4):
                                last = mm(bank[g // 2][32 * j:32 * j + 32, S * (g % 2):S * (g % 2) + S],
                                          Vp[:, k, 4 * g + j, :], P[:, u % 4, S * j:S * j + S],
                                          start=False, stop=False, skip_group_check=True, tile_position=(0, 32 * j))
                            last.then_inc(t["pfree"], 1)

                    def chunk(i, first=False, last=False):
                        def values(k):
                            if k == 0:
                                pe.wait_ge(t["cl"], t.n("cl", 2 * i + 2))
                            pe.wait_ge(t["v"], t.n("v", KT * i + k))
                            cols = slice(128 * k, 128 * k + 128)
                            pairs = [(v[:, f, cols], w[:, f, 0:c.hid]) for f in range(2)
                                     for v, w in ((c_hi, wv_hi), (c_hi, wv_lo), (c_lo, wv_hi))]
                            three(bank[3][:, 0:c.hid], pairs).then_inc(t["vp"], 1)

                        def scores(u):
                            g = u // c.ups
                            if u % c.ups == 0:
                                pe.wait_ge(t["kl"], t.n("kl", i * c.groups + c.gps * (g + 1)))
                                if c.layer == 0:
                                    pe.wait_ge(t["kone"], t.n("kone", i * 8 + g + 1))
                            if u >= 2:
                                pe.wait_ge(t["p"], t.n("p", i * c.units + u - 1))
                            else:
                                pe.wait_ge(t["s"], t.n("s", i * c.units))
                                if u == 0:
                                    pe.wait_ge(t["p"], t.n("p", i * c.units))
                            if c.layer == 0:
                                hl, h1 = k_hl[g % 2], k_h1[g % 2]
                                for k in range(KT):
                                    o = score[u % 2][:, S * k:S * k + S]
                                    cols = slice(128 * k, 128 * k + 128)
                                    mm(o, hl[:, cols], q_hh[:, g, :], start=True, stop=False)
                                    last = mm(o, h1[0:65, cols], q_lm[0:65, g, :], start=False, stop=True)
                            else:
                                cols = slice(128 * (u % KT), 128 * (u % KT) + 128)
                                for j in range(0, 4, 2):
                                    h = 4 * g + j
                                    o = score[u % 2][:, S * j:S * j + 2 * S]
                                    last = mm(o, k_st[h // 2 % 4][:, cols], q_hh[:, h:h + 2, :], start=True, stop=True)
                            last.then_inc(t["s"], 1)

                        for u in range(c.units):
                            scores(u)
                            if c.layer == 0:
                                if u == 1 and not first:
                                    weigh(i - 1, 6)
                                if 1 <= u <= KT:
                                    values(u - 1)
                                if u == 5:
                                    weigh(i, 0), weigh(i, 2)
                                if u == 7:
                                    weigh(i, 4)
                            else:
                                if u < 3 and not first:
                                    weigh(i - 1, 13 + u)
                                if u < KT:
                                    values(u)
                                if u >= 3:
                                    weigh(i, u - 3)
                            if u in TURNS[c.layer] and not last:
                                turn(i + 1, u - TURNS[c.layer][0])

                    chunk(0, first=True)
                    with pe.Fori(1, NCH - 1) as i:
                        chunk(i)
                    chunk(NCH - 1, last=True)
                    for u in ((6,) if c.layer == 0 else (13, 14, 15)):
                        weigh(NCH - 1, u)
                    pe.wait_ge(t["p"], t.n("p", NCH * c.units))
                    if c.layer == 0:
                        for h in (POOL_HEADS[-1], DVE_HEADS[-1]):
                            key, count = summed(NCH - 1, h)
                            pe.wait_ge(t[key], t.n(key, count))
                        for h in range(8):
                            p, j = h // 2, h % 2
                            last = mm(score[0][64 * j:64 * j + 64, S * p:S * p + S], ones[:, 0:64], acc_p[:, h, :],
                                      start=True, stop=True, tile_position=(0, 64 * j))
                        last.then_inc(t["d"], 1)
                    else:
                        pe.wait_ge(t["osb"], t.n("osb", 2))
                        for k in range(2):
                            last = mm(score[0][:, 512 * k:512 * k + 512], den_pick[:], P[:, 0, 512 * k:512 * k + 512], start=True, stop=True)
                        last.then_inc(t["d"], 1)
                if c.layer == 0:
                    pe.wait_ge(a["wo"], 16)
                pe.wait_ge(a["bias"], 16 if c.layer == 0 else 16 * 21)
                for n in range(TT):
                    if n == 2:
                        pe.wait_ge(ATT[c.layer, 1]["o"], ATT[c.layer, 1].n("o", 4))
                    if n >= 2:
                        pe.wait_ge(a["res"], n - 1)
                    for k in range(4):
                        mm(bank[2 + n % 2][:, 0:D], oT[:, k, 128 * n:128 * n + 128], wout[:, k, :], start=(k == 0), stop=False)
                    mm(bank[2 + n % 2][:, 0:D], ones[0:1, :], row[0:1, 0:D], start=False, stop=True).then_inc(a["op"], 1)


            def local_attention():
                pe.wait_ge(la["w"], 192)
                step = [0]

                def project(pairs, out=None):
                    n = step[0]
                    if n >= 2:
                        pe.wait_ge(la["pe"], n - 1)
                    dst = bank[2 + n % 2][:] if out is None else out
                    width = pairs[0][1].free_size()
                    for k, (l, r) in enumerate(pairs):
                        last = mm(bank[2 + n % 2][:, 0:width], l, r, start=(k == 0), stop=(k == len(pairs) - 1))
                    last.then_inc(la["pj"], 1)
                    step[0] += 1

                pe.wait_ge(LN[1]["xT"], LN[1].n("xT", 2))
                for w in (0, 1):
                    for m in range(2):
                        project([(la_wqkv[:, w, f, 128 * m:128 * m + 128], xnT[:, f, :]) for f in range(2)])
                project([(la_wg[:, 0, f, :], xnT[:, f, :]) for f in range(2)])
                for t in range(TT):
                    project([(xnT[:, f, 128 * t:128 * t + 128], la_wqkv[:, 2, f, :]) for f in range(2)])
                pe.wait_ge(la["g"], 1)
                for b in range(B):
                    project([(la_wg[:, 1, f, :], la_xp[:, f, b, 0, :]) for f in range(2)])
                for b in range(B):
                    project([(la_xp[:, f, b].rearrange("p c n -> p (c n)"), la_wg[:, 2, f, :]) for f in range(2)])
                pe.wait_ge(la["pe"], 13)
                pe.wait_ge(la["gt"], 1)
                for t in range(TT):
                    for f in range(2):
                        last = mm(bank[2][:, 32 * t:32 * t + 32], la_QT[:, f, 128 * t:128 * t + 128], la_G[:, f, :],
                                  start=(f == 0), stop=(f == 1))
                last.then_inc(la["gt"], 1)
                pe.wait_ge(la["g"], 2)
                def scores(t):
                    b, keys = t // 2, 128 * la_keys[t]
                    pe.wait_ge(la["qp"], t + 1)
                    hpb = 1024 // keys
                    for n in range(la_bufs[t]):
                        buf = upto_t(la_bufs, t) + n
                        if buf >= 2:
                            pe.wait_ge(la["sb"], buf - 1)
                        for h in range(hpb):
                            hh = n * hpb + h
                            last = mm(score[buf % 2][:, keys * h:keys * h + keys], la_q[:, hh, :],
                                      la_KT[:, hh // 8, b * S:b * S + keys], start=True, stop=True)
                        last.then_inc(la["s"], 1)
                    if t >= 2:
                        pe.wait_ge(la["res"], t - 1)
                    for h in range(NHG):
                        last = mm(bank[1][:, LAT * h:LAT * h + LAT], la_gq[:, h, :], la_GKT[:, b * LAT:b * LAT + LAT], start=True, stop=True)
                    last.then_inc(la["o"], 1)

                scores(0)
                for t in range(TT):
                    b = t // 2
                    if t < TT - 1:
                        scores(t + 1)
                    pe.wait_ge(la["e"], t + 1)
                    taken = (sum((q + 1) // 2 for q in la_quads[:t]), sum(q // 2 for q in la_quads[:t]))
                    for n in range(la_quads[t]):
                        pe.wait_ge(la["pta" if n % 2 else "ptd"], taken[n % 2] + n // 2)
                        for k in range(4):
                            if n < la_quads[t] - 1:
                                blk = 4 * n + k
                                src = la_S[t % 2][:, blk // la_keys[t], 128 * (blk % la_keys[t]):128 * (blk % la_keys[t]) + 128]
                            else:
                                src = la_LS[t % 2][:, 2 * k:2 * k + 2, :].rearrange("p h n -> p (h n)")
                            last = nc.tensor.transpose(bank[2 + n % 2][:, 128 * k:128 * k + 128], src, ident[:])
                        last.then_inc(la["tr"], 1)
                    pe.wait_ge(la["ptd"], taken[0] + (la_quads[t] + 1) // 2)
                    pe.wait_ge(la["pta"], taken[1] + la_quads[t] // 2)
                    nk = la_keys[t]
                    for h in range(NHL):
                        for k in range(nk):
                            blk = h * nk + k
                            mm(bank[0][:, 17 * h:17 * h + 17], la_PT[:, 128 * blk:128 * blk + 128], la_V[:, 2 * b + k, h, :],
                               start=(k == 0), stop=(k == nk - 1))
                    for h in range(0, NHG, 2):
                        last = mm(bank[0][:, 272 + 17 * h:306 + 17 * h], la_LPT[:, 64 * h:64 * h + 128],
                                  la_GV[:, b, h:h + 2, :].rearrange("p h d -> p (h d)"), start=True, stop=True)
                    last.then_inc(la["o"], 1)
                    pe.wait_ge(la["rq"], t + 1)
                    nc.tensor.transpose(bank[1][:, 0:128], la_rq, ident[:]).then_inc(la["rt"], 1)
                    pe.wait_ge(la["rtc"], t + 1)
                    mm(bank[1][:, 256:512], la_rqT, la_rout, start=True, stop=True).then_inc(la["rem"], 1)
                    pe.wait_ge(la["cb"], t + 1)
                    for f in range(2):
                        last = nc.tensor.transpose(bank[1][:, 128 * f:128 * f + 128], la_cb[:, 128 * f:128 * f + 128], ident[:])
                    last.then_inc(la["ct"], 1)
                    pe.wait_ge(la["ctc"], t + 1)
                    for f in range(2):
                        last = mm(bank[1][:, 256:512], la_cT[:, 128 * f:128 * f + 128], la_wout[:, f, :], start=(f == 0), stop=(f == 1))
                    last.then_inc(la["out"], 1)

            def logits(g, n, w):
                pe.wait_ge(LN[n]["xT"], LN[n].n("xT", 2))
                for t in range(TT):
                    for f in range(2):
                        last = mm(bank[2][:, E * t:E * t + E], xnT[:, f, 128 * t:128 * t + 128], w[:, f, :], start=(f == 0), stop=(f == 1))
                last.then_inc(g["lp"], 1)

            def dense_mixture():
                pe.wait_ge(gm["w"], 48)
                logits(gm, 2, gate_w)
                nc.tensor.transpose(bank[3][:, 0:64], b1n, ident[0:64, 0:64]).then_inc(gm["bt"], 1)
                pe.wait_ge(gm["cT"], 1)
                for t in range(TT):
                    last = nc.tensor.transpose(bank[2][0:8, 128 * t:128 * t + 128], comb[:, t, :], ident[:])
                last.then_inc(gm["cTc"], 1)
                pe.wait_ge(gm["b2"], 1)
                for t in range(TT):
                    last = mm(score[0][:, D * t:D * t + D], combT[:, 128 * t:128 * t + 128], b2sb, start=True, stop=True)
                last.then_inc(gm["done"], 1)
                pe.wait_ge(gm["done"], 2)
                with pe.Fori(0, E) as e:
                    pe.wait_ge(em["w1l"], em.n("w1l", e + 1))
                    for m in range(FM):
                        if m < 2:
                            pe.wait_ge(em["g"], em.n("g", FM * e))
                        else:
                            pe.wait_ge(em["g"], em.n("g", FM * e + m - 1))
                        cols = slice(128 * m, 128 * m + 128)
                        three(bank[m % 2][:], [(w[:, f, cols], r[:, f, :]) for f in range(2)
                                               for w, r in ((w1_hi, c_hi), (w1_hi, c_lo), (w1_lo, c_hi))]).then_inc(em["h"], 1)
                    pe.wait_ge(em["w2l"], em.n("w2l", e + 1))
                    for t in range(TT):
                        if t < 2:
                            pe.wait_ge(em["acc"], em.n("acc", TT * e))
                        else:
                            pe.wait_ge(em["acc"], em.n("acc", TT * e + t - 1))
                        cols = slice(128 * t, 128 * t + 128)
                        for k in range(FM):
                            if t == 0:
                                pe.wait_ge(em["hl"], em.n("hl", FM * e + k + 1))
                            for n, (h, w) in enumerate(((h_hi, w2_hi), (h_hi, w2_lo), (h_lo, w2_hi))):
                                last = mm(bank[2 + t % 2][:, 0:D], h[:, k, cols], w[:, k, :],
                                          start=(k == 0 and n == 0), stop=(k == FM - 1 and n == 2))
                        last.then_inc(em["y"], 1)

            def rwkv():
                pe.wait_ge(rw["w"], 64)
                pe.wait_ge(LN[4]["xT"], LN[4].n("xT", 2))
                for n in range(4):
                    if n >= 2:
                        pe.wait_ge(rw["trc"], n - 1)
                    for f in range(2):
                        for o in range(2):
                            last = nc.tensor.transpose(bank[n % 2][:, 256 * f + 128 * o:256 * f + 128 * o + 128],
                                                       rw_nat[:, n, o, 128 * f:128 * f + 128], ident[:])
                    last.then_inc(rw["tr"], 1)
                pe.wait_ge(rw["trc"], 4)
                for n, (w, src) in enumerate(((0, rw_xk), (1, rw_xv), (2, rw_xr))):
                    pe.wait_ge(rw["mx"], n + 1)
                    for m in range(2):
                        dst = (score[0][:, 512 * m:512 * m + 512], score[1][:, 512 * m:512 * m + 512], bank[2 + m][:])[n]
                        for f in range(2):
                            last = mm(dst, rw_W[:, w, f, 128 * m:128 * m + 128], src[:, f].rearrange("p b t -> p (b t)"),
                                      start=(f == 0), stop=(f == 1))
                        last.then_inc(rw["pj"], 1)
                pe.wait_ge(rw["o"], 1)
                for t in range(TT):
                    if t >= 2:
                        pe.wait_ge(rw["res"], t - 1)
                    b, u = t // 2, t % 2
                    for f in range(2):
                        last = mm(bank[t % 2][:, 0:D], rw_out[:, f, b, 128 * u:128 * u + 128], rw_W[:, 3, f, :], start=(f == 0), stop=(f == 1))
                    last.then_inc(rw["out"], 1)

            def chunk_mixture():
                pe.wait_ge(cm["wr"], cm.n("wr", 16))
                pe.wait_ge(LN[5]["xT"], LN[5].n("xT", 2))
                for f in range(2):
                    last = nc.tensor.transpose(bank[3][:, 8 * f:8 * f + 8], wr_nat[:, 128 * f:128 * f + 128], ident[0:8, 0:8])
                last.then_inc(cm["tr"], 1)
                pe.wait_ge(cm["trc"], cm.n("trc", 1))
                logits(cm, 5, gate_w)
                pe.wait_ge(cm["c"], cm.n("c", 1))
                pe.wait_ge(cm["iota"], cm.n("iota", 1))
                mm(bank[3][:, 0:32], before, comb.rearrange("p t e -> p (t e)"), start=True, stop=True)
                mm(bank[3][:, 32:64], ones[:], comb.rearrange("p t e -> p (t e)"), start=True, stop=True).then_inc(cm["c"], 1)
                pe.wait_ge(cm["xl"], cm.n("xl", 1))
                for t in range(TT):
                    pe.wait_ge(cm["pa"], cm.n("pa", t + 1))
                    for n in range(4):
                        f, half = n // 2, n % 2
                        for part in (xn_hi, xn_lo):
                            last = mm(score[f][:, 512 * half:512 * half + 512], part[:, t, 128 * f:128 * f + 128],
                                      PA[:, t, 512 * half:512 * half + 512], start=(t == 0 and part is xn_hi),
                                      stop=(t == TT - 1 and part is xn_lo))
                        if t == TT - 1:
                            last.then_inc(cm["pm"], 1)

                def hidden(e, n, loads, first=False):
                    pe.wait_ge(cm[f"a{n}"], cm.n(f"a{n}", loads * 16))
                    for m in range(FM):
                        if m % 4 == 0 and not first:
                            pe.wait_ge(cm["g"], cm.n("g", 2 * e - 1 + m // 4))
                        for f in range(2):
                            last = mm(bank[m // 4][:, 128 * (m % 4):128 * (m % 4) + 128], cw1[n][:, f, 128 * m:128 * m + 128],
                                      permT[:, f, bass.ts(e, 128)], start=(f == 0), stop=(f == 1))
                        if m % 4 == 3:
                            last.then_inc(cm["h"], 1)

                def second(e, n, loads):
                    pe.wait_ge(cm[f"b{n}"], cm.n(f"b{n}", loads * 16))
                    pe.wait_ge(cm["g"], cm.n("g", 2 * e + 2))
                    pe.wait_ge(cm["yc"], cm.n("yc", e))
                    for k in range(FM):
                        last = mm(bank[2][:, 0:D], hT[n][:, k, :], cw2[n][:, k, :], start=(k == 0), stop=(k == FM - 1))
                    last.then_inc(cm["y"], 1)

                pe.wait_ge(cm["pmc"], cm.n("pmc", 4))
                hidden(0, 0, 1, first=True)
                with pe.Fori(0, E // 2 - 1) as i:
                    hidden(i * 2 + 1, 1, i + 1)
                    second(i * 2, 0, i + 1)
                    hidden(i * 2 + 2, 0, i + 2)
                    second(i * 2 + 1, 1, i + 1)
                hidden(E - 1, 1, E // 2)
                second(E - 2, 0, E // 2)
                pe.wait_ge(cm["pw"], cm.n("pw", TT))
                for e in range(E):
                    if e >= 4:
                        pe.wait_ge(cm["trc"], cm.n("trc", 1 + e - 3))
                    for t in range(TT):
                        last = nc.tensor.transpose(score[e // 2 % 2][:, 512 * (e % 2) + 128 * t:512 * (e % 2) + 128 * t + 128],
                                                   PW[:, t, 128 * e:128 * e + 128], ident[:])
                    last.then_inc(cm["tr"], 1)
                second(E - 1, 1, E // 2)
                pe.wait_ge(cm["trc"], cm.n("trc", 1 + E))
                pe.wait_ge(cm["yc"], cm.n("yc", E))
                for t in range(TT):
                    if t >= 2:
                        pe.wait_ge(cm["res"], cm.n("res", t - 1))
                    for e in range(E):
                        last = mm(bank[t % 2][:, 0:D], PWT[:, e, 128 * t:128 * t + 128], yS[:, e, :], start=(e == 0), stop=(e == E - 1))
                    last.then_inc(cm["s"], 1)

            signal_ahead(pe, "pe")
            pe.wait_ge(const_ready, 1)
            layer_norm(0)
            cross(X0, 0)
            stage_end(pe, 1)
            layer_norm(1)
            local_attention()
            stage_end(pe, 2)
            layer_norm(2)
            dense_mixture()
            stage_end(pe, 3)
            layer_norm(3)
            cross(X1, 3)
            stage_end(pe, 4)
            layer_norm(4)
            rwkv()
            stage_end(pe, 5)
            layer_norm(5)
            chunk_mixture()
            stage_end(pe, 6)

        @program.vector
        def _(dve):
            v = nc.vector
            chain = [0]

            def link(i):
                chain[0] += 1
                i.then_inc(dve_chain, 1)
                dve.wait_ge(dve_chain, chain[0])

            def layer_norm(n):
                ln = LN[n]
                for t in range(TT):
                    last = v.bn_stats(stats[:, t, :], x[:, t, :])
                link(last)
                for t in range(TT):
                    last = v.bn_aggr(mv[:, t, :], stats[:, t, :])
                link(last)
                v.tensor_scalar(mv[:, :, 1], mv[:, :, 1], EPS, None, ALU.add).then_inc(ln["var"], 1)
                dve.wait_ge(ln["std"], ln.n("std", 1))
                link(v.reciprocal(rstd[:], rstd[:]))
                for t in range(TT):
                    v.tensor_scalar(xn[:, t, :], x[:, t, :], mv[:, t, 0:1], rstd[:, t:t + 1], ALU.subtract, ALU.mult).then_inc(ln["xn"], 1)
                dve.wait_ge(ln["tr"], ln.n("tr", 1))
                v.tensor_copy(xnT[:, 1, :], bank[1][:]).then_inc(ln["xT"], 1)
                dve.wait_ge(ln["xT"], ln.n("xT", 2))

            def context_low(ph, f, i, src):
                dve.wait_ge(ph["ch"], ph.n("ch", 2 * i + f + 1))
                v.tensor_tensor(c_lo[:, f, :], src[:], c_hi[:, f, :].bitcast(F32), ALU.subtract).then_inc(ph["cl"], 1)

            def cross(c, stage):
                a = CA[c.layer]
                if c.layer == 0:
                    for n, (hi, lo) in enumerate(((wk_hi, wk_lo), (wv_hi, wv_lo))):
                        dve.wait_ge(a["w0"], n + 1)
                        v.tensor_tensor(lo, w_raw[:, n + 1], hi.bitcast(F32), ALU.subtract).then_inc(a["whl"], 1)
                else:
                    link(v.memset(bias[:, 4:8], 0.0))
                    v.engine_nop().then_inc(a["pad"], 1)
                    link(v.memset(wo_pad, 0.0))
                    dve.wait_ge(a["w"], 64)
                    for o in range(2):
                        last = v.tensor_copy(wo_pad[:, o, :].rearrange("p (h d) -> p h d", d=32)[:, :, 0:16],
                                             wo_nat[:, o, :].rearrange("p (h d) -> p h d", d=16))
                    last.then_inc(a["pad"], 1)
                    for n, (hi, lo) in enumerate(((wk_hi, wk_lo), (wv_hi, wv_lo))):
                        dve.wait_ge(a["w0"], n + 1)
                        v.tensor_tensor(lo[:, :, 0:256], bank[(n + 1) % 2][:].rearrange("p (f n) -> p f n", f=2),
                                        hi[:, :, 0:256].bitcast(F32), ALU.subtract).then_inc(a["whl"], 1)
                    dve.wait_ge(a["bias"], 16 * 21)
                for n in range(c.tiles):
                    dve.wait_ge(a["qp"], n + 1)
                    if c.layer == 0:
                        v.tensor_scalar(qT[:, n, :], bank[2 + n % 2][:], c.scale, None, ALU.mult).then_inc(a["q"], 1)
                    else:
                        v.tensor_scalar(qT[:, 2 + n, :], bank[2 + n % 2][:], bias[:, n:n + 1], c.scale, ALU.add, ALU.mult).then_inc(a["q"], 1)
                dve.wait_ge(a["q"], c.tiles)
                if c.layer == 1:
                    dve.wait_ge(a["wop"], 1)
                    v.tensor_copy(wout, score[0][:].rearrange("p (k n) -> p k n", k=4)).then_inc(a["wop"], 1)
                mask = mask_half if c.layer == 0 else mask_16th
                qt0 = 0 if c.layer == 0 else 2

                def high_queries(b):
                    for h in range(c.heads):
                        v.tensor_scalar(q_hi[:, h, :], qT[:, qt0 + h // c.hpt, b * S:b * S + S], mask[:, h % c.hpt:h % c.hpt + 1], None,
                                        ALU.mult).then_inc(MAXP[c.layer, b]["qh"], 1)

                high_queries(0)
                for b in range(B):
                    m, t = MAXP[c.layer, b], ATT[c.layer, b]
                    toks = slice(b * S, b * S + S)
                    def reduce(i, h):
                        dve.wait_ge(m["s"], m.n("s", i * c.heads + h + 1))
                        if c.layer == 0:
                            v.tensor_reduce(mx[:, bass.ds(i, 1), 2 * h:2 * h + 2], score[h % 2][:].rearrange("p (q k) -> p q k", q=2),
                                            AX.X, ALU.max).then_inc(m["red"], 1)
                        else:
                            v.tensor_reduce(mx[:, bass.ds(i, 1), 2 * h:2 * h + 1], max_buffer(c, h, 0), AX.X, ALU.max).then_inc(m["red"], 1)

                    def run(i, h):
                        if h == 0:
                            dve.wait_ge(m["low"], m.n("low", 1))
                        dve.wait_ge(m["rm"], m.n("rm", (i - 1) * NR + h + 1))
                        dve.wait_ge(m["cp"], m.n("cp", i * NR + h + 1))
                        v.tensor_tensor(run_max[:, h, :], run_max[:, h, :], copied[:, h % 2, :], ALU.max).then_inc(m["rm"], 1)

                    def low_both(i):
                        for f in range(2):
                            context_low(m, f, i, bank[f])

                    low_both(0)
                    dve.wait_ge(m["qh"], m.n("qh", c.heads))
                    if c.layer == 1 and b == 0:
                        dve.wait_ge(a["clear"], 1)
                    for h in range(c.heads):
                        g = h // c.hpg
                        _, r = hidden_of(c, g)
                        rows = slice(r, r + c.rows)
                        v.scalar_tensor_tensor(out=q_lm[0:64, h, :] if c.layer == 0 else q_hh[block(g, 1), h, :],
                                               in0=qT[rows, qt0 + h // c.hpt, toks],
                                               scalar=mask[rows, h % c.hpt:h % c.hpt + 1], in1=q_hi[rows, h, :].bitcast(F32),
                                               op0=ALU.mult, op1=ALU.subtract).then_inc(m["ql"], 1)
                    dve.sem_inc(m["red"], c.heads)
                    if c.layer == 1:
                        dve.sem_inc(m["rm"], NR)

                    def heads(i, hs):
                        for h in hs:
                            reduce(i, h)
                            if c.layer == 1 and h:
                                run(i, h - 1)
                            if c.layer == 1 and h == c.heads - 1:
                                run(i, h)

                    ahead_of = 5 if c.layer == 0 else 12
                    with dve.Fori(0, NCH - 1) as i:
                        heads(i, range(ahead_of))
                        low_both(i + 1)
                        heads(i, range(ahead_of, c.heads))
                    heads(NCH - 1, range(c.heads))
                    dve.wait_ge(m["red"], m.n("red", NCH * c.heads))
                    if c.layer == 0:
                        v.tensor_reduce(mneg[:, 0:2 * c.heads], mx[:, :, 0:2 * c.heads].rearrange("p c h -> p h c"), AX.X, ALU.max,
                                        negate=True).then_inc(m["m"], 1)
                    else:
                        tile_of = mneg[:].rearrange("p (h q) -> p h q", q=2)
                        v.tensor_reduce(tile_of[:, :, 0], mx.rearrange("p c (h q) -> p h q c", q=2)[:, :, 0, :], AX.X, ALU.max, negate=True)
                        dve.wait_ge(m["rm"], m.n("rm", NCH * NR))
                        for width in (256, 128, 64):
                            link(v.tensor_tensor(run_max[:, :, 0:width], run_max[:, :, 0:width], run_max[:, :, width:2 * width], ALU.max))
                        v.tensor_reduce(tile_of[:, :, 1], run_max[:, :, 0:64], AX.X, ALU.max, negate=True).then_inc(m["m"], 1)
                    if c.layer == 0:
                        dve.sem_inc(t["accd"], len(DVE_HEADS) * KT)

                    def split(i, g):
                        n = i * c.groups + g
                        tile, r = hidden_of(c, g)
                        src = Kst[c.layer][r:r + c.rows, tile, bass.ts(i, CHUNK)]
                        if c.layer == 0:
                            high, rest = k_hl[g % 2][r:r + 64, :], k_hl[g % 2][64 - r:128 - r, :]
                        else:
                            high, rest = k_st[g % 4][block(g, 0), :], k_st[g % 4][block(g, 2), :]
                        dve.wait_ge(t["s"], t.n("s", (i * c.sets + g // c.gps - 1) * c.ups))
                        v.tensor_copy(high, src).then_inc(t["khi"], 1)
                        if c.layer == 1:
                            v.tensor_copy(k_st[g % 4][block(g, 1), :], src)
                        dve.wait_ge(t["khi"], t.n("khi", n + 1))
                        v.tensor_tensor(rest, src, high.bitcast(F32), ALU.subtract).then_inc(t["kl"], 1)

                    def values(i, k):
                        dve.wait_ge(t["vp"], t.n("vp", KT * i + k + 1))
                        if c.layer == 1:
                            dve.wait_ge(t["pfree"], t.n("pfree", c.units * i + k + 1))
                        elif k == 0:
                            dve.wait_ge(t["pfree"], t.n("pfree", c.units * i + 4))
                        if c.layer == 0:
                            v.tensor_copy(V[:, k, :], bank[3][:]).then_inc(t["v"], 1)
                        else:
                            v.tensor_copy(Vp[:, k, :, 0:16], bank[3][:, 0:256].rearrange("p (h d) -> p h d", h=16)).then_inc(t["v"], 1)

                    def sums(i, u):
                        dve.wait_ge(t["p"], t.n("p", i * 8 + u + 1))
                        for k in range(KT):
                            dve.wait_ge(t["accd"], t.n("accd", summed(i, u)[1] - KT + k))
                            v.tensor_tensor(acc_p[:, u, :], acc_p[:, u, :],
                                            P[:, u % 4, k * S:(k + 1) * S], ALU.add).then_inc(t["accd"], 1)

                    def begin(i):
                        if c.layer == 0:
                            context_low(t, 0, i, bank[2])
                            split(i, 0), split(i, 1)
                            context_low(t, 1, i, bank[2])
                        else:
                            split(i, 0), split(i, 1)
                            context_low(t, 0, i, bank[2]), context_low(t, 1, i, bank[2])

                    def chunk(i, last=False):
                        split(i, 2), split(i, 3)
                        for k in range(KT):
                            values(i, k)
                            if c.layer == 0 and k < 3:
                                split(i, 4 + k)
                        if c.layer == 0:
                            sums(i, 3), split(i, 7)
                        else:
                            for g in range(4, 8):
                                split(i, g)
                        if not last:
                            begin(i + 1)
                        if c.layer == 0:
                            sums(i, 5)

                    begin(0)
                    if c.layer == 0:
                        dve.wait_ge(t["z"], t.n("z", 1))
                    with dve.Fori(0, NCH - 1) as i:
                        chunk(i)
                    chunk(NCH - 1, last=True)
                    if b == 0:
                        dve.wait_ge(m["qhh"], m.n("qhh", 2 * c.groups))
                        high_queries(1)
                    dve.wait_ge(t["d"], t.n("d", 1))
                    dve.wait_ge(t["pfree"], t.n("pfree", NCH * c.units + 4))
                    if c.layer == 0:
                        v.reciprocal(P[:, 1, :], score[0][:]).then_inc(t["rd"], 1)
                        dve.wait_ge(t["rd"], t.n("rd", 1))
                        for k in range(4):
                            v.tensor_tensor(oT[:, k, toks], bank[k // 2][:, S * (k % 2):S * (k % 2) + S], P[:, 1, S * k:S * k + S],
                                            ALU.mult).then_inc(t["o"], 1)
                    else:
                        v.reciprocal(P[:, 1, :], score[0][:]).then_inc(t["rd"], 1)
                        dve.wait_ge(t["rd"], t.n("rd", 1))
                        for k in range(4):
                            link(v.tensor_tensor(oT[:, k, toks], bank[k // 2][:, S * (k % 2):S * (k % 2) + S], P[:, 1, S * k:S * k + S],
                                                 ALU.mult))
                            v.tensor_scalar(oT[:, k, toks], oT[:, k, toks], bias[:, 4 + k:5 + k], None, ALU.add).then_inc(t["o"], 1)
                for n in range(TT):
                    dve.wait_ge(a["op"], n + 1)
                    v.tensor_tensor(x[:, n, :], bank[2 + n % 2][:, 0:D], x[:, n, :], ALU.add).then_inc(a["res"], 1)


            def local_attention():
                link(v.tensor_reduce(la_xs, xnT.rearrange("p f (n g) -> p f n g", g=GRP), AX.X, ALU.add))
                for c in range(2):
                    last = v.tensor_scalar(la_xp[:, :, :, c, :], la_xs.rearrange("p f (b n) -> p f b n", b=B), 1.0 / GRP, None, ALU.mult)
                last.then_inc(la["g"], 1)
                dve.wait_ge(la["w"], 192)
                link(v.memset(la_G, 0.0))
                for f in range(2):
                    for w in range(2):
                        last = v.tensor_scalar(la_G[:, f, 16 * w + 8 * f:16 * w + 8 * f + 8], mask_16th[:], la_gcol[:, f, w:w + 1], None, ALU.mult)
                last.then_inc(la["gt"], 1)
                dsts = [(la_QT[:, 0, :], 512), (la_QT[:, 1, :], 512), (la_KT[:, 0, :], 512), (la_KT[:, 1, :], 512), (la_GQT, 512)]
                dsts += [(la_V[:, t, :, 0:HD], 256) for t in range(TT)]
                dsts += [(la_GKT[:, 64 * b:64 * b + 64], 64) for b in range(B)]
                dsts += [(la_GV[:, b, :, 0:HD], 128) for b in range(B)]
                dve.wait_ge(la["msk"], 1)
                for n, (dst, width) in enumerate(dsts):
                    dve.wait_ge(la["pj"], n + 1)
                    src = bank[2 + n % 2][:, 0:width]
                    if n in (5, 6, 7, 8, 11, 12):
                        src = src.rearrange("p (h d) -> p h d", d=HD)
                    if n < 11:
                        last = v.tensor_copy(dst, src)
                    else:
                        for r in (0, 1):
                            last = v.tensor_copy(dst[64 * r:64 * r + 64, r::2, :], src[64 * r:64 * r + 64, r::2, :])
                    last.then_inc(la["pe"], 1)
                dve.wait_ge(la["pe"], 13)
                def queries(t):
                    if t:
                        dve.wait_ge(la["o"], la_o_latent[t - 1])
                    for h in range(NHL):
                        v.tensor_scalar(la_q[:, h, :], la_QT[:, h // 8, 128 * t:128 * t + 128], mask_16th[:, h % 8:h % 8 + 1], None, ALU.mult)
                    for h in range(NHG):
                        last = v.tensor_scalar(la_gq[:, h, :], la_GQT[:, 128 * t:128 * t + 128], mask_16th[:, h:h + 1], None, ALU.mult)
                    last.then_inc(la["qp"], 1)

                def masked_scores(t):
                    u, keys = t % 2, 128 * la_keys[t]
                    hpb = 1024 // keys
                    for n in range(la_bufs[t]):
                        buf = upto_t(la_bufs, t) + n
                        dve.wait_ge(la["s"], buf + 1)
                        v.scalar_tensor_tensor(out=la_S[u][:, n * hpb:n * hpb + hpb, 0:keys],
                                               in0=score[buf % 2][:].rearrange("p (h k) -> p h k", h=hpb), scalar=HD ** -0.5,
                                               in1=bc(la_mask[:, 256 - keys:256], 1, hpb), op0=ALU.mult, op1=ALU.add).then_inc(la["sb"], 1)
                    dve.wait_ge(la["o"], la_o_latent[t])
                    link(v.scalar_tensor_tensor(out=la_LS[u], in0=bank[1][:].rearrange("p (h n) -> p h n", h=NHG), scalar=HD ** -0.5,
                                                in1=bc(la_lmask[:, u, :], 1, NHG), op0=ALU.mult, op1=ALU.add))

                def maxima(t):
                    dve.wait_ge(la["sb"], upto_t(la_bufs, t + 1))
                    v.tensor_reduce(la_m[t % 2][:, 0:NHL], la_S[t % 2][:, :, 0:128 * la_keys[t]], AX.X, ALU.max, negate=True).then_inc(la["m"], 1)
                    v.tensor_reduce(la_m[t % 2][:, NHL:], la_LS[t % 2], AX.X, ALU.max, negate=True).then_inc(la["m"], 1)

                queries(0)
                masked_scores(0)
                maxima(0)
                queries(1)
                for t in range(TT):
                    if t < TT - 1:
                        masked_scores(t + 1)
                    quads = upto_t(la_quads, t)
                    for n in range(0, la_quads[t], 2):
                        dve.wait_ge(la["tr"], quads + n + 1)
                        dst = la_LPT if n == la_quads[t] - 1 else la_PT[:, 512 * n:512 * n + 512]
                        v.tensor_copy(dst, bank[2 + n % 2][:]).then_inc(la["ptd"], 1)
                    if t < TT - 1:
                        maxima(t + 1)
                    if t < TT - 2:
                        queries(t + 2)
                    dve.wait_ge(la["o"], la_o_values[t])
                    if t == 0:
                        dve.wait_ge(la["g"], 2)
                    O = bank[0][:, 0:408].rearrange("p (h d) -> p h d", d=17)
                    link(v.reciprocal(la_r, O[:, :, 16]))
                    v.tensor_tensor(la_rq.rearrange("p (h d) -> p h d", d=HD), O[:, NHL:, 0:HD], bc(la_r[:, NHL:], 2, HD), ALU.mult).then_inc(la["rq"], 1)
                    link(v.tensor_tensor(la_rs, la_r[:, 0:NHL], la_gate[:, t, 0:NHL], ALU.mult))
                    link(v.tensor_tensor(la_cb.rearrange("p (h d) -> p h d", d=HD), O[:, 0:NHL, 0:HD], bc(la_rs, 2, HD), ALU.mult))
                    dve.wait_ge(la["rt"], t + 1)
                    v.tensor_copy(la_rqT, bank[1][:, 0:128]).then_inc(la["rtc"], 1)
                    dve.wait_ge(la["rem"], t + 1)
                    rem = P[:, 3, 256:512].rearrange("p (h d) -> p h d", d=HD)
                    link(v.tensor_tensor(rem, bank[1][:, 256:512].rearrange("p (h d) -> p h d", d=HD), bc(la_gate[:, t, NHL:], 2, HD), ALU.mult))
                    v.tensor_tensor(la_cb, la_cb, P[:, 3, 256:512], ALU.add).then_inc(la["cb"], 1)
                    dve.wait_ge(la["ct"], t + 1)
                    v.tensor_copy(la_cT, bank[1][:, 0:256]).then_inc(la["ctc"], 1)
                    dve.wait_ge(la["out"], t + 1)
                    v.tensor_tensor(x[:, t, :], bank[1][:, 256:512], x[:, t, :], ALU.add).then_inc(la["res"], 1)

            def top_two(g):
                dve.wait_ge(g["lp"], 1)
                link(v.tensor_copy(lg, bank[2][:, 0:E * TT].rearrange("p (t e) -> p t e", t=TT)))
                for t in range(TT):
                    last = v.max(top8[:, t, :], lg[:, t, :])
                link(last)
                for t in range(TT):
                    last = v.max_index(idx8[:, t, :], top8[:, t, :], lg[:, t, :])
                link(last)
                link(v.tensor_copy(idxf, idx8))
                v.tensor_tensor(tw[:, 0, :], top8[:, :, 1], top8[:, :, 0], ALU.subtract).then_inc(g["t"], 1)
                dve.wait_ge(g["ex"], 1)
                link(v.tensor_scalar(tw[:, 0, :], tw[:, 1, :], 1.0, None, ALU.add))
                link(v.reciprocal(tw[:, 0, :], tw[:, 0, :]))
                link(v.tensor_tensor(tw[:, 1, :], tw[:, 0, :], tw[:, 1, :], ALU.mult))

            def dense_mixture():
                dve.wait_ge(gm["bt"], 1)
                v.tensor_copy(b1T, bank[3][:, 0:64]).then_inc(gm["btc"], 1)
                for f in range(2):
                    last = v.tensor_copy(c_hi[:, f, :], xnT[:, f, :])
                link(last)
                last = v.tensor_tensor(c_lo[:], xnT, c_hi[:].bitcast(F32), ALU.subtract)
                link(last)
                top_two(gm)
                for t in range(TT):
                    for k in range(2):
                        last = v.tensor_scalar(ohtmp[:, k, t, :], iota8[:], idxf[:, t, k:k + 1], tw[:, k, t:t + 1], ALU.is_equal, ALU.mult)
                link(last)
                v.tensor_tensor(comb, ohtmp[:, 0], ohtmp[:, 1], ALU.add).then_inc(gm["cT"], 1)
                dve.wait_ge(gm["cTc"], 1)
                v.tensor_copy(combT, bank[2][0:8, :]).then_inc(gm["b2"], 1)
                dve.wait_ge(gm["done"], 1)
                v.tensor_tensor(x[:], score[0][:].rearrange("p (t d) -> p t d", t=TT), x[:], ALU.add).then_inc(gm["done"], 1)
                dve.wait_ge(gm["done"], 2)
                def low_w1(e):
                    dve.wait_ge(em["w1h"], em.n("w1h", e + 1))
                    v.tensor_tensor(w1_lo, w1raw, w1_hi.bitcast(F32), ALU.subtract).then_inc(em["w1l"], 1)

                def expert(e, last=False):
                    dve.wait_ge(em["y"], em.n("y", TT * e))
                    for m in range(FM):
                        dve.wait_ge(em["g"], em.n("g", FM * e + m + 1))
                        v.tensor_copy(h_hi[:, m, :], h32[:, m, :]).then_inc(em["hh"], 1)
                        dve.wait_ge(em["hh"], em.n("hh", FM * e + m + 1))
                        v.tensor_tensor(h_lo[:, m, :], h32[:, m, :], h_hi[:, m, :].bitcast(F32), ALU.subtract).then_inc(em["hl"], 1)
                        if m == 3:
                            dve.wait_ge(em["w2h"], em.n("w2h", e + 1))
                            v.tensor_tensor(w2_lo, w2raw, w2_hi.bitcast(F32), ALU.subtract).then_inc(em["w2l"], 1)
                    if not last:
                        low_w1(e + 1)
                    for t in range(TT):
                        dve.wait_ge(em["y"], em.n("y", TT * e + t + 1))
                        dve.wait_ge(em["acc"], em.n("acc", TT * e))
                        v.scalar_tensor_tensor(out=x[:, t, :], in0=bank[2 + t % 2][:, 0:D], scalar=comb[:, t, bass.ds(e, 1)],
                                               in1=x[:, t, :], op0=ALU.mult, op1=ALU.add).then_inc(em["acc"], 1)

                low_w1(0)
                with dve.Fori(0, E - 1) as e:
                    expert(e)
                expert(E - 1, last=True)

            def rwkv():
                full = lambda a: a.rearrange("p m b t -> p (m b t)")
                for n in range(4):
                    dve.wait_ge(rw["tr"], n + 1)
                    v.tensor_copy(rw_W[:, n], bank[n % 2][:].rearrange("p (f n) -> p f n", f=2)).then_inc(rw["trc"], 1)
                xt = xnT.rearrange("p f (b t) -> p f b t", b=B)
                v.memset(rw_xp[:, :, :, 0:1], 0.0)
                for f in range(2):
                    last = v.tensor_copy(rw_xp[:, f, :, 1:S], xt[:, f, :, 0:S - 1])
                link(last)
                link(v.tensor_tensor(full(rw_d), xnT.rearrange("p f t -> p (f t)"), full(rw_xp), ALU.subtract))
                dve.wait_ge(rw["v"], 160)
                for n, dst in enumerate((rw_xk, rw_xv, rw_xr)):
                    for f in range(2):
                        last = v.scalar_tensor_tensor(out=dst[:, f], in0=rw_d[:, f], scalar=rw_vec[:, 2 + n, f:f + 1],
                                                      in1=rw_xp[:, f], op0=ALU.mult, op1=ALU.add)
                    last.then_inc(rw["mx"], 1)
                dve.wait_ge(rw["we"], 1)
                link(v.tensor_scalar(rw_wexp, rw_wexp, -1.0, None, ALU.mult))
                v.memset(rw_o[:, :, :, 0:1], NEG)
                v.memset(rw_p[:, :, :, 0:1], 0.0)
                link(v.memset(rw_q[:, :, :, 0:1], 0.0))
                dve.wait_ge(rw["pj"], 4)
                v.tensor_copy(full(rw_k), score[0][:])
                link(v.tensor_copy(full(rw_v), score[1][:]))
                for m in range(2):
                    for b in range(B):
                        last = v.tensor_tensor_scan(rw_o[:, m, b, 1:S + 1], rw_wexp[:, m:m + 1].broadcast_to([128, S]), rw_k[:, m, b, :],
                                                    NEG, ALU.add, ALU.max)
                for m in range(2):
                    last = v.tensor_scalar(rw_Bc[:, m], rw_k[:, m], rw_vec[:, 1, m:m + 1], None, ALU.add)
                link(last)
                for m in range(2):
                    last = v.tensor_tensor(rw_no[:, m], rw_Bc[:, m], rw_o[:, m, :, 0:S], ALU.max)
                link(last)
                dve.wait_ge(rw["pj"], 6)
                for m in range(2):
                    v.tensor_tensor(rw_A[:, m], rw_o[:, m, :, 0:S], rw_no[:, m], ALU.subtract)
                    v.tensor_tensor(rw_Bc[:, m], rw_Bc[:, m], rw_no[:, m], ALU.subtract)
                    v.scalar_tensor_tensor(out=rw_A2[:, m], in0=rw_o[:, m, :, 0:S], scalar=rw_wexp[:, m:m + 1],
                                           in1=rw_o[:, m, :, 1:S + 1], op0=ALU.add, op1=ALU.subtract)
                    last = v.tensor_tensor(rw_B2[:, m], rw_k[:, m], rw_o[:, m, :, 1:S + 1], ALU.subtract)
                last.then_inc(rw["a"], 1)
                dve.wait_ge(rw["a2"], 1)
                link(v.tensor_tensor(full(rw_num), full(rw_B2), full(rw_v), ALU.mult))
                for m in range(2):
                    for b in range(B):
                        v.tensor_tensor_scan(rw_p[:, m, b, 1:S + 1], rw_A2[:, m, b, :], rw_num[:, m, b, :], 0.0, ALU.mult, ALU.add)
                        last = v.tensor_tensor_scan(rw_q[:, m, b, 1:S + 1], rw_A2[:, m, b, :], rw_B2[:, m, b, :], 0.0, ALU.mult, ALU.add)
                link(last)
                for m in range(2):
                    v.tensor_tensor(rw_num[:, m], rw_A[:, m], rw_p[:, m, :, 0:S], ALU.mult)
                    last = v.tensor_tensor(rw_den[:, m], rw_A[:, m], rw_q[:, m, :, 0:S], ALU.mult)
                link(last)
                v.tensor_tensor(full(rw_no), full(rw_Bc), full(rw_v), ALU.mult)
                link(v.tensor_tensor(full(rw_den), full(rw_den), full(rw_Bc), ALU.add))
                v.tensor_tensor(full(rw_num), full(rw_num), full(rw_no), ALU.add)
                link(v.reciprocal(full(rw_den), full(rw_den)))
                link(v.tensor_tensor(full(rw_num), full(rw_num), full(rw_den), ALU.mult))
                dve.wait_ge(rw["sr"], 2)
                v.tensor_tensor(full(rw_out), full(rw_num), full(rw_sr), ALU.mult).then_inc(rw["o"], 1)
                for t in range(TT):
                    dve.wait_ge(rw["out"], t + 1)
                    v.tensor_tensor(x[:, t, :], bank[t % 2][:, 0:D], x[:, t, :], ALU.add).then_inc(rw["res"], 1)

            def chunk_mixture():
                dve.wait_ge(cm["tr"], cm.n("tr", 1))
                v.tensor_copy(gate_w, bank[3][:, 0:16].rearrange("p (f e) -> p f e", f=2)).then_inc(cm["trc"], 1)
                top_two(cm)
                for t in range(TT):
                    for k in range(2):
                        last = v.tensor_scalar(ohtmp[:, k, t, :], iota8[:], idxf[:, t, k:k + 1], None, ALU.is_equal)
                link(last)
                v.tensor_tensor(comb, ohtmp[:, 0], ohtmp[:, 1], ALU.add).then_inc(cm["c"], 1)
                dve.wait_ge(cm["xh"], cm.n("xh", 1))
                v.tensor_tensor(xn_lo, xn, xn_hi.bitcast(F32), ALU.subtract).then_inc(cm["xl"], 1)
                dve.wait_ge(cm["c"], cm.n("c", 2))
                link(v.tensor_copy(tot.rearrange("p (e t) -> p e t", e=E), bank[3][:, 32:64].rearrange("p (t e) -> p e t", t=TT)))
                link(v.tensor_tensor_scan(incl, ones[:, 0:32], tot, 0.0, ALU.mult, ALU.add))
                link(v.tensor_tensor(incl, incl, tot, ALU.subtract))
                link(v.tensor_tensor(rank_e, bank[3][:, 0:32].rearrange("p (t e) -> p t e", t=TT),
                                     incl.rearrange("p (e t) -> p t e", e=E), ALU.add))
                for k in range(2):
                    last = v.tensor_tensor(ohtmp[:, k], ohtmp[:, k], rank_e, ALU.mult)
                link(last)
                for k in range(2):
                    last = v.tensor_reduce(rank[:, k, :], ohtmp[:, k], AX.X, ALU.add)
                link(last)
                dve.wait_ge(cm["iota"], cm.n("iota", 1))
                for t in range(TT):
                    link(v.tensor_scalar(Ptmp[:, 0, :], iota_s, rank[:, 0, t:t + 1], None, ALU.is_equal))
                    v.scalar_tensor_tensor(out=PA[:, t, :], in0=iota_s, scalar=rank[:, 1, t:t + 1], in1=Ptmp[:, 0, :], op0=ALU.is_equal, op1=ALU.add).then_inc(cm["pa"], 1)
                    dve.wait_ge(cm["pa"], cm.n("pa", t + 1))
                for t in range(TT):
                    for k in range(2):
                        last = v.tensor_scalar(Ptmp[:, k, :], iota_s, rank[:, k, t:t + 1], tw[:, k, t:t + 1], ALU.is_equal, ALU.mult)
                    link(last)
                    v.tensor_tensor(PW[:, t, :], Ptmp[:, 0, :], Ptmp[:, 1, :], ALU.add).then_inc(cm["pw"], 1)
                    dve.wait_ge(cm["pw"], cm.n("pw", t + 1))
                with dve.Fori(0, E - 1) as e:
                    dve.wait_ge(cm["y"], cm.n("y", e + 1))
                    v.tensor_copy(yS[:, bass.ds(e, 1), :].rearrange("p a d -> p (a d)"), bank[2][:, 0:D]).then_inc(cm["yc"], 1)
                for e in range(E):
                    dve.wait_ge(cm["tr"], cm.n("tr", e + 2))
                    v.tensor_copy(PWT[:, e, :], score[e // 2 % 2][:, 512 * (e % 2):512 * (e % 2) + 512]).then_inc(cm["trc"], 1)
                dve.wait_ge(cm["y"], cm.n("y", E))
                v.tensor_copy(yS[:, E - 1, :], bank[2][:, 0:D]).then_inc(cm["yc"], 1)
                for t in range(TT):
                    dve.wait_ge(cm["s"], cm.n("s", t + 1))
                    v.tensor_tensor(x[:, t, :], bank[t % 2][:, 0:D], x[:, t, :], ALU.add).then_inc(cm["res"], 1)

            signal_ahead(dve, "dve")
            dve.wait_ge(const_ready, 1)
            dve.wait_ge(x_in, 16)
            layer_norm(0)
            cross(X0, 0)
            stage_end(dve, 1)
            layer_norm(1)
            local_attention()
            stage_end(dve, 2)
            layer_norm(2)
            dense_mixture()
            stage_end(dve, 3)
            layer_norm(3)
            cross(X1, 3)
            stage_end(dve, 4)
            layer_norm(4)
            rwkv()
            stage_end(dve, 5)
            layer_norm(5)
            chunk_mixture()
            stage_end(dve, 6)


_INS = ['x', 'ctx_1024', 'L0_xattn_Wq', 'L0_xattn_Wk', 'L0_xattn_Wv', 'L0_xattn_Wo', 'L0_xattn_bo', 'L0_attn_wq', 'L0_attn_wk',
        'L0_attn_wv', 'L0_attn_wgq', 'L0_attn_wgk', 'L0_attn_wgv', 'L0_attn_r_out_w', 'L0_attn_gate_local_w',
        'L0_attn_gate_remote_w', 'L0_attn_w_out', 'L0_ffn_gate_w', 'L0_ffn_w1', 'L0_ffn_b1', 'L0_ffn_w2', 'L0_ffn_b2',
        'L1_xattn_wq', 'L1_xattn_bq', 'L1_xattn_wk', 'L1_xattn_bk', 'L1_xattn_wv', 'L1_xattn_bv', 'L1_xattn_wo', 'L1_xattn_bo',
        'L1_attn_w', 'L1_attn_u', 'L1_attn_mix_k', 'L1_attn_mix_v', 'L1_attn_mix_r', 'L1_attn_Wk', 'L1_attn_Wv', 'L1_attn_Wr',
        'L1_attn_Wo', 'L1_ffn_Wr', 'L1_ffn_W1', 'L1_ffn_W2']


def kernel(**inputs):
    import concourse.bacc as _bacc
    from concourse.bass_utils import run_bass_kernel_spmd as _run

    nc = _bacc.Bacc("TRN2", target_bir_lowering=False, num_devices=1)
    arrays, aps = {}, {}
    for name in _INS:
        a = np.ascontiguousarray(inputs[name])
        arrays[f"in_{name}"] = a
        aps[name] = nc.dram_tensor(f"in_{name}", a.shape, mybir.dt.from_np(a.dtype), kind="ExternalInput").ap()
    out = nc.dram_tensor("out_x", (B, S, D), F32, kind="ExternalOutput").ap()
    perceiver(nc, aps, out)
    r = _run(nc, [arrays], core_ids=[0])
    return r.results[0]["out_x"]
```
